# Optimizing a Trainium2 kernel written in Bass

```python
import numpy as np
import jax
import jax.numpy as jnp

def _softmax(x, axis=-1):
    return jax.nn.softmax(x, axis=axis)

def _gelu(x):
    return jax.nn.gelu(x, approximate=True)

def _silu(x):
    return jax.nn.silu(x)

def _sigmoid(x):
    return jax.nn.sigmoid(x)

def _layernorm(x, axis=-1, eps=1e-05):
    m = jnp.mean(x, axis=axis, keepdims=True)
    v = jnp.var(x, axis=axis, keepdims=True)
    return (x - m) / jnp.sqrt(v + eps)

def _scatter_add(tgt, idx, src, axis=0):
    return tgt.at[idx].add(src)

def _segment_sum(src, seg, n):
    return jax.ops.segment_sum(src, seg, n)
kernel_name = 'mk_metaformer_d2_conv_nchw512_r2_2c0a2f'

def setup_inputs(seed: int=0):
    np.random.seed(seed)
    _w = jnp.asarray

    def _rec_inputs():
        import jax
        import jax.numpy as jnp
        _gk = jax.random.key(seed)
        x = 7.22e-05 + 1 * jax.random.normal(jax.random.fold_in(_gk, 1), (4, 256, 32, 32), jnp.float32)
        return x
    x = _rec_inputs()

    def _L0_conv_setup():
        import jax, jax.numpy as jnp
        from jax import lax
        import numpy as np
        INPUT_DIM = 256
        OUTPUT_DIM = 256
        D_STATE = 16
        D_CONV = 4
        EXPAND = 2
        D_MODEL = INPUT_DIM // 4
        D_INNER = EXPAND * D_MODEL
        DT_RANK = (D_MODEL + 15) // 16
        EPS = 1e-05

        def layer_norm(x, g, b):
            mu = jnp.mean(x, axis=-1, keepdims=True)
            var = jnp.mean((x - mu) ** 2, axis=-1, keepdims=True)
            return (x - mu) * lax.rsqrt(var + EPS) * g + b

        def mamba(x, in_proj_w, conv_w, conv_b, x_proj_w, dt_proj_w, dt_proj_b, A_log, D_param, out_proj_w):
            Beff, L, _ = x.shape
            xz = jnp.einsum('bld,ed->ble', x, in_proj_w)
            xi, z = jnp.split(xz, 2, axis=-1)
            xc = lax.conv_general_dilated(xi.transpose(0, 2, 1), conv_w[:, None, :], (1,), [(D_CONV - 1, 0)], feature_group_count=D_INNER)
            xc = jax.nn.silu(xc + conv_b[None, :, None]).transpose(0, 2, 1)
            dbc = jnp.einsum('bld,ed->ble', xc, x_proj_w)
            dt = dbc[..., :DT_RANK]
            Bs = dbc[..., DT_RANK:DT_RANK + D_STATE]
            Cs = dbc[..., DT_RANK + D_STATE:]
            dt = jax.nn.softplus(jnp.einsum('blr,er->ble', dt, dt_proj_w) + dt_proj_b)
            A = -jnp.exp(A_log)

            def step(h, inp):
                dt_t, B_t, C_t, x_t = inp
                dA = jnp.exp(dt_t[:, :, None] * A)
                h = dA * h + (dt_t * x_t)[:, :, None] * B_t[:, None, :]
                y = jnp.einsum('bds,bs->bd', h, C_t)
                return (h, y)
            h0 = jnp.zeros((Beff, D_INNER, D_STATE), x.dtype)
            _, ys = lax.scan(step, h0, (dt.transpose(1, 0, 2), Bs.transpose(1, 0, 2), Cs.transpose(1, 0, 2), xc.transpose(1, 0, 2)))
            y = ys.transpose(1, 0, 2) + xc * D_param
            y = y * jax.nn.silu(z)
            return jnp.einsum('bld,od->blo', y, out_proj_w)
        key = jax.random.key(seed)
        ks = jax.random.split(key, 10)
        inp = {'x': jax.random.normal(ks[0], (4, INPUT_DIM, 32, 32), jnp.float32), 'norm_g': jnp.ones((INPUT_DIM,), jnp.float32), 'norm_b': jnp.zeros((INPUT_DIM,), jnp.float32), 'in_proj_w': jax.random.normal(ks[1], (2 * D_INNER, D_MODEL), jnp.float32) * 0.02, 'conv_w': jax.random.normal(ks[2], (D_INNER, D_CONV), jnp.float32) * 0.2, 'conv_b': jnp.zeros((D_INNER,), jnp.float32), 'x_proj_w': jax.random.normal(ks[3], (DT_RANK + 2 * D_STATE, D_INNER), jnp.float32) * 0.02, 'dt_proj_w': jax.random.normal(ks[4], (D_INNER, DT_RANK), jnp.float32) * 0.1, 'dt_proj_b': jnp.full((D_INNER,), -2.0, jnp.float32), 'A_log': jnp.log(jnp.broadcast_to(jnp.arange(1, D_STATE + 1, dtype=jnp.float32), (D_INNER, D_STATE))), 'D_param': jnp.ones((D_INNER,), jnp.float32), 'out_proj_w': jax.random.normal(ks[5], (D_MODEL, D_INNER), jnp.float32) * 0.02, 'proj_w': jax.random.normal(ks[6], (OUTPUT_DIM, INPUT_DIM), jnp.float32) * 0.02, 'proj_b': jnp.zeros((OUTPUT_DIM,), jnp.float32), 'skip_scale': jnp.ones((1,), jnp.float32)}
        return inp
    _L0_conv_all = _L0_conv_setup()
    _L0_conv_in = {k: v for k, v in _L0_conv_all.items() if k in ('norm_g', 'norm_b', 'in_proj_w', 'conv_w', 'conv_b', 'x_proj_w', 'dt_proj_w', 'dt_proj_b', 'A_log', 'D_param', 'out_proj_w', 'proj_w', 'proj_b', 'skip_scale')}
    del _L0_conv_all

    def _L0_ffn_setup():
        import jax, jax.numpy as jnp
        import numpy as np
        E4M3_MAX = 448.0

        def qdq(x, scale, fp8_dtype, fmax):
            scaled = x / scale
            clipped = jnp.clip(scaled, -fmax, fmax)
            return clipped.astype(fp8_dtype).astype(x.dtype) * scale.astype(x.dtype)
        key = jax.random.key(seed)
        k1, k2, k3 = jax.random.split(key, 3)
        B, S, D, F = (8, 4096, 256, 256)
        x = jax.random.normal(k1, (B, S, D), jnp.float32)
        kernel = jax.random.normal(k2, (D, F), jnp.float32) * (1.0 / np.sqrt(D))
        bias = jax.random.normal(k3, (F,), jnp.float32) * 0.01
        return {'x': x, 'kernel': kernel, 'bias': bias, 'input_scale': jnp.ones((1,), jnp.float32), 'kernel_scale': jnp.ones((1,), jnp.float32), 'output_grad_scale': jnp.ones((1,), jnp.float32)}
    _L0_ffn_all = _L0_ffn_setup()
    _L0_ffn_in = {k: v for k, v in _L0_ffn_all.items() if k in ('kernel', 'bias', 'input_scale', 'kernel_scale', 'output_grad_scale')}
    del _L0_ffn_all

    def _L1_conv_setup():
        import jax, jax.numpy as jnp
        import numpy as np
        EPS = 1e-05
        NUM_GROUPS = 32

        def _group_norm(x, gamma, beta):
            B, C, H, W = x.shape
            G = NUM_GROUPS
            xg = x.reshape(B, G, C // G, H, W)
            mean = jnp.mean(xg, axis=(2, 3, 4), keepdims=True)
            var = jnp.var(xg, axis=(2, 3, 4), keepdims=True)
            xn = (xg - mean) * jax.lax.rsqrt(var + EPS)
            xn = xn.reshape(B, C, H, W)
            return xn * gamma[None, :, None, None] + beta[None, :, None, None]
        key = jax.random.key(seed)
        ks = jax.random.split(key, 10)
        B, C, H, W = (32, 256, 32, 32)
        scale = 1.0 / np.sqrt(C)
        inp = {'x': jax.random.normal(ks[0], (B, C, H, W), dtype=jnp.float32), 'gn_gamma': jnp.ones((C,), dtype=jnp.float32), 'gn_beta': jnp.zeros((C,), dtype=jnp.float32), 'wq': jax.random.normal(ks[1], (C, C), dtype=jnp.float32) * scale, 'bq': jnp.zeros((C,), dtype=jnp.float32), 'wk': jax.random.normal(ks[2], (C, C), dtype=jnp.float32) * scale, 'bk': jnp.zeros((C,), dtype=jnp.float32), 'wv': jax.random.normal(ks[3], (C, C), dtype=jnp.float32) * scale, 'bv': jnp.zeros((C,), dtype=jnp.float32), 'wp': jax.random.normal(ks[4], (C, C), dtype=jnp.float32) * scale, 'bp': jnp.zeros((C,), dtype=jnp.float32)}
        return inp
    _L1_conv_all = _L1_conv_setup()
    _L1_conv_in = {k: v for k, v in _L1_conv_all.items() if k in ('gn_gamma', 'gn_beta', 'wq', 'bq', 'wk', 'bk', 'wv', 'bv', 'wp', 'bp')}
    del _L1_conv_all

    def _L1_ffn_setup():
        import jax, jax.numpy as jnp
        import numpy as np
        B, S, D = (8, 1024, 256)
        E, K, H = (8, 2, 1024)
        key = jax.random.key(seed)
        ks = jax.random.split(key, 6)
        scale = 0.02
        return {'x': jax.random.normal(ks[0], (B, S, D), dtype=jnp.float32), 'gate_w': jax.random.normal(ks[1], (E, D), dtype=jnp.float32) * scale, 'w1': jax.random.normal(ks[2], (E, H, D), dtype=jnp.float32) * scale, 'b1': jax.random.normal(ks[3], (E, H), dtype=jnp.float32) * scale, 'w2': jax.random.normal(ks[4], (E, D, H), dtype=jnp.float32) * scale, 'b2': jax.random.normal(ks[5], (E, D), dtype=jnp.float32) * scale}
    _L1_ffn_all = _L1_ffn_setup()
    _L1_ffn_in = {k: v for k, v in _L1_ffn_all.items() if k in ('gate_w', 'w1', 'b1', 'w2', 'b2')}
    del _L1_ffn_all
    return {'x': x, 'L0_conv_norm_g': _L0_conv_in['norm_g'], 'L0_conv_norm_b': _L0_conv_in['norm_b'], 'L0_conv_in_proj_w': _L0_conv_in['in_proj_w'], 'L0_conv_conv_w': _L0_conv_in['conv_w'], 'L0_conv_conv_b': _L0_conv_in['conv_b'], 'L0_conv_x_proj_w': _L0_conv_in['x_proj_w'], 'L0_conv_dt_proj_w': _L0_conv_in['dt_proj_w'], 'L0_conv_dt_proj_b': _L0_conv_in['dt_proj_b'], 'L0_conv_A_log': _L0_conv_in['A_log'], 'L0_conv_D_param': _L0_conv_in['D_param'], 'L0_conv_out_proj_w': _L0_conv_in['out_proj_w'], 'L0_conv_proj_w': _L0_conv_in['proj_w'], 'L0_conv_proj_b': _L0_conv_in['proj_b'], 'L0_conv_skip_scale': _L0_conv_in['skip_scale'], 'L0_ffn_kernel': _L0_ffn_in['kernel'], 'L0_ffn_bias': _L0_ffn_in['bias'], 'L0_ffn_input_scale': _L0_ffn_in['input_scale'], 'L0_ffn_kernel_scale': _L0_ffn_in['kernel_scale'], 'L0_ffn_output_grad_scale': _L0_ffn_in['output_grad_scale'], 'L1_conv_gn_gamma': _L1_conv_in['gn_gamma'], 'L1_conv_gn_beta': _L1_conv_in['gn_beta'], 'L1_conv_wq': _L1_conv_in['wq'], 'L1_conv_bq': _L1_conv_in['bq'], 'L1_conv_wk': _L1_conv_in['wk'], 'L1_conv_bk': _L1_conv_in['bk'], 'L1_conv_wv': _L1_conv_in['wv'], 'L1_conv_bv': _L1_conv_in['bv'], 'L1_conv_wp': _L1_conv_in['wp'], 'L1_conv_bp': _L1_conv_in['bp'], 'L1_ffn_gate_w': _L1_ffn_in['gate_w'], 'L1_ffn_w1': _L1_ffn_in['w1'], 'L1_ffn_b1': _L1_ffn_in['b1'], 'L1_ffn_w2': _L1_ffn_in['w2'], 'L1_ffn_b2': _L1_ffn_in['b2']}

def reference(x, L0_conv_norm_g, L0_conv_norm_b, L0_conv_in_proj_w, L0_conv_conv_w, L0_conv_conv_b, L0_conv_x_proj_w, L0_conv_dt_proj_w, L0_conv_dt_proj_b, L0_conv_A_log, L0_conv_D_param, L0_conv_out_proj_w, L0_conv_proj_w, L0_conv_proj_b, L0_conv_skip_scale, L0_ffn_kernel, L0_ffn_bias, L0_ffn_input_scale, L0_ffn_kernel_scale, L0_ffn_output_grad_scale, L1_conv_gn_gamma, L1_conv_gn_beta, L1_conv_wq, L1_conv_bq, L1_conv_wk, L1_conv_bk, L1_conv_wv, L1_conv_bv, L1_conv_wp, L1_conv_bp, L1_ffn_gate_w, L1_ffn_w1, L1_ffn_b1, L1_ffn_w2, L1_ffn_b2):
    import jax
    import jax.numpy as jnp

    def _L0_conv_ref(x, norm_g, norm_b, in_proj_w, conv_w, conv_b, x_proj_w, dt_proj_w, dt_proj_b, A_log, D_param, out_proj_w, proj_w, proj_b, skip_scale):
        import jax, jax.numpy as jnp
        from jax import lax
        import numpy as np
        INPUT_DIM = 256
        OUTPUT_DIM = 256
        D_STATE = 16
        D_CONV = 4
        EXPAND = 2
        D_MODEL = INPUT_DIM // 4
        D_INNER = EXPAND * D_MODEL
        DT_RANK = (D_MODEL + 15) // 16
        EPS = 1e-05

        def layer_norm(x, g, b):
            mu = jnp.mean(x, axis=-1, keepdims=True)
            var = jnp.mean((x - mu) ** 2, axis=-1, keepdims=True)
            return (x - mu) * lax.rsqrt(var + EPS) * g + b

        def mamba(x, in_proj_w, conv_w, conv_b, x_proj_w, dt_proj_w, dt_proj_b, A_log, D_param, out_proj_w):
            Beff, L, _ = x.shape
            xz = jnp.einsum('bld,ed->ble', x, in_proj_w)
            xi, z = jnp.split(xz, 2, axis=-1)
            xc = lax.conv_general_dilated(xi.transpose(0, 2, 1), conv_w[:, None, :], (1,), [(D_CONV - 1, 0)], feature_group_count=D_INNER)
            xc = jax.nn.silu(xc + conv_b[None, :, None]).transpose(0, 2, 1)
            dbc = jnp.einsum('bld,ed->ble', xc, x_proj_w)
            dt = dbc[..., :DT_RANK]
            Bs = dbc[..., DT_RANK:DT_RANK + D_STATE]
            Cs = dbc[..., DT_RANK + D_STATE:]
            dt = jax.nn.softplus(jnp.einsum('blr,er->ble', dt, dt_proj_w) + dt_proj_b)
            A = -jnp.exp(A_log)

            def step(h, inp):
                dt_t, B_t, C_t, x_t = inp
                dA = jnp.exp(dt_t[:, :, None] * A)
                h = dA * h + (dt_t * x_t)[:, :, None] * B_t[:, None, :]
                y = jnp.einsum('bds,bs->bd', h, C_t)
                return (h, y)
            h0 = jnp.zeros((Beff, D_INNER, D_STATE), x.dtype)
            _, ys = lax.scan(step, h0, (dt.transpose(1, 0, 2), Bs.transpose(1, 0, 2), Cs.transpose(1, 0, 2), xc.transpose(1, 0, 2)))
            y = ys.transpose(1, 0, 2) + xc * D_param
            y = y * jax.nn.silu(z)
            return jnp.einsum('bld,od->blo', y, out_proj_w)
        B, C, H, W = x.shape
        L = H * W
        xf = x.reshape(B, C, L).transpose(0, 2, 1)
        xn = layer_norm(xf, norm_g, norm_b)
        chunks = xn.reshape(B, L, 4, D_MODEL).transpose(2, 0, 1, 3).reshape(4 * B, L, D_MODEL)
        ym = mamba(chunks, in_proj_w, conv_w, conv_b, x_proj_w, dt_proj_w, dt_proj_b, A_log, D_param, out_proj_w)
        ym = ym + skip_scale * chunks
        y = ym.reshape(4, B, L, D_MODEL).transpose(1, 2, 0, 3).reshape(B, L, C)
        y = layer_norm(y, norm_g, norm_b)
        y = jnp.einsum('blc,oc->blo', y, proj_w) + proj_b
        return y.transpose(0, 2, 1).reshape(B, OUTPUT_DIM, H, W)

    def _L0_ffn_ref(x, kernel, bias, input_scale, kernel_scale, output_grad_scale):
        import jax, jax.numpy as jnp
        import numpy as np
        E4M3_MAX = 448.0

        def qdq(x, scale, fp8_dtype, fmax):
            scaled = x / scale
            clipped = jnp.clip(scaled, -fmax, fmax)
            return clipped.astype(fp8_dtype).astype(x.dtype) * scale.astype(x.dtype)
        B, S, D = x.shape
        inp_mat = x.reshape(-1, D)
        inp_q = qdq(inp_mat, input_scale, jnp.float8_e4m3fn, E4M3_MAX)
        ker_q = qdq(kernel, kernel_scale, jnp.float8_e4m3fn, E4M3_MAX)
        out = inp_q @ ker_q
        b = bias.astype(jnp.bfloat16).astype(jnp.float32)
        out = out + b
        return out.reshape(B, S, out.shape[-1])

    def _L1_conv_ref(x, gn_gamma, gn_beta, wq, bq, wk, bk, wv, bv, wp, bp):
        import jax, jax.numpy as jnp
        import numpy as np
        EPS = 1e-05
        NUM_GROUPS = 32

        def _group_norm(x, gamma, beta):
            B, C, H, W = x.shape
            G = NUM_GROUPS
            xg = x.reshape(B, G, C // G, H, W)
            mean = jnp.mean(xg, axis=(2, 3, 4), keepdims=True)
            var = jnp.var(xg, axis=(2, 3, 4), keepdims=True)
            xn = (xg - mean) * jax.lax.rsqrt(var + EPS)
            xn = xn.reshape(B, C, H, W)
            return xn * gamma[None, :, None, None] + beta[None, :, None, None]
        B, C, H, W = x.shape
        h = x
        xn = _group_norm(x, gn_gamma, gn_beta)
        xf = xn.reshape(B, C, H * W)
        Q = jnp.einsum('oc,bcn->bon', wq, xf) + bq[None, :, None]
        K = jnp.einsum('oc,bcn->bon', wk, xf) + bk[None, :, None]
        V = jnp.einsum('oc,bcn->bon', wv, xf) + bv[None, :, None]
        scores = jnp.einsum('bcn,bdn->bcd', Q, K) / jnp.sqrt(jnp.float32(C))
        attn = jax.nn.softmax(scores, axis=-1)
        ctx = jnp.einsum('bcd,bdn->bcn', attn, V)
        out = jnp.einsum('oc,bcn->bon', wp, ctx) + bp[None, :, None]
        return h + out.reshape(B, C, H, W)

    def _L1_ffn_ref(x, gate_w, w1, b1, w2, b2):
        import jax, jax.numpy as jnp
        import numpy as np
        B, S, D = (8, 1024, 256)
        E, K, H = (8, 2, 1024)
        batch, seq, dim = x.shape
        x_flat = x.reshape(-1, dim)
        T = x_flat.shape[0]
        gate_logits = x_flat @ gate_w.T
        topk_vals, topk_idx = jax.lax.top_k(gate_logits, K)
        topk_w = jax.nn.softmax(topk_vals, axis=-1)
        comb = jnp.zeros((T, E), dtype=x_flat.dtype)
        comb = comb.at[jnp.arange(T)[:, None], topk_idx].add(topk_w)
        out = jnp.zeros_like(x_flat)
        for e in range(E):
            h = jax.nn.gelu(x_flat @ w1[e].T + b1[e], approximate=False)
            y = h @ w2[e].T + b2[e]
            out = out + comb[:, e:e + 1] * y
        return out.reshape(batch, seq, dim)

    def _gn(v, G=32, eps=1e-05):
        B_, C_, H_, W_ = v.shape
        g = v.reshape(B_, G, C_ // G, H_, W_)
        m = jnp.mean(g, axis=(2, 3, 4), keepdims=True)
        s = jnp.var(g, axis=(2, 3, 4), keepdims=True)
        return ((g - m) / jnp.sqrt(s + eps)).reshape(v.shape)

    def _ln_c(v, eps=1e-06):
        m = jnp.mean(v, axis=1, keepdims=True)
        s = jnp.var(v, axis=1, keepdims=True)
        return (v - m) / jnp.sqrt(s + eps)

    def _ln_t(v, eps=1e-05):
        m = jnp.mean(v, axis=-1, keepdims=True)
        s = jnp.var(v, axis=-1, keepdims=True)
        return (v - m) / jnp.sqrt(s + eps)

    def _to_tokens(v):
        B_, C_, H_, W_ = v.shape
        return v.reshape(B_, C_, H_ * W_).transpose(0, 2, 1)

    def _from_tokens(t, like):
        B_, C_, H_, W_ = like.shape
        return t.transpose(0, 2, 1).reshape(B_, C_, H_, W_)
    x = x + _L0_conv_ref(_ln_c(x), L0_conv_norm_g, L0_conv_norm_b, L0_conv_in_proj_w, L0_conv_conv_w, L0_conv_conv_b, L0_conv_x_proj_w, L0_conv_dt_proj_w, L0_conv_dt_proj_b, L0_conv_A_log, L0_conv_D_param, L0_conv_out_proj_w, L0_conv_proj_w, L0_conv_proj_b, L0_conv_skip_scale)
    t = _to_tokens(x)
    t = t + _L0_ffn_ref(_ln_t(t), L0_ffn_kernel, L0_ffn_bias, L0_ffn_input_scale, L0_ffn_kernel_scale, L0_ffn_output_grad_scale)
    x = _from_tokens(t, x)
    x = x + _L1_conv_ref(_ln_c(x), L1_conv_gn_gamma, L1_conv_gn_beta, L1_conv_wq, L1_conv_bq, L1_conv_wk, L1_conv_bk, L1_conv_wv, L1_conv_bv, L1_conv_wp, L1_conv_bp)
    t = _to_tokens(x)
    t = t + _L1_ffn_ref(_ln_t(t), L1_ffn_gate_w, L1_ffn_w1, L1_ffn_b1, L1_ffn_w2, L1_ffn_b2)
    x = _from_tokens(t, x)
    return x

_drawn_inputs = setup_inputs


def setup_inputs(seed=0):
    import zlib

    import numpy as np

    out = dict(_drawn_inputs(seed))
    spreads = {'L0_conv_norm_g': (1.0, 0.2),
     'L0_conv_norm_b': (0.0, 0.1),
     'L0_conv_conv_b': (0.0, 0.8),
     'L0_conv_dt_proj_b': (-2.0, 0.6),
     'L0_conv_D_param': (1.0, 0.6),
     'L0_conv_proj_b': (0.0, 0.1),
     'L1_conv_gn_gamma': (1.0, 0.2),
     'L1_conv_gn_beta': (0.0, 0.1),
     'L1_conv_bq': (0.0, 0.1),
     'L1_conv_bk': (0.0, 0.1),
     'L1_conv_bv': (0.0, 0.1),
     'L1_conv_bp': (0.0, 0.1)}
    factors = {'L0_conv_in_proj_w': 8.0,
     'L0_conv_conv_w': 8.0,
     'L0_conv_x_proj_w': 8.0,
     'L0_conv_dt_proj_w': 8.0,
     'L0_conv_A_log': 8.0,
     'L0_conv_out_proj_w': 8.0,
     'L0_ffn_bias': 2.753,
     'L1_ffn_b1': 28.531,
     'L1_ffn_b2': 8.0}
    for name, (base, spread) in spreads.items():
        noise = np.random.default_rng([zlib.crc32(name.encode()), seed]).standard_normal(out[name].shape)
        drawn = base * np.exp(spread * noise) if base else spread * noise
        out[name] = jnp.asarray(drawn.astype(out[name].dtype))
    for name, factor in factors.items():
        out[name] = (out[name] * factor).astype(out[name].dtype)
    return out
```

```python
from contextlib import ExitStack

import concourse.bass as bass
from concourse import mybir

F32 = mybir.dt.float32
BF16 = mybir.dt.bfloat16
U32 = mybir.dt.uint32
ALU = mybir.AluOpType
ACT = mybir.ActivationFunctionType
AX_X = mybir.AxisListType.X

P = 128
B, C, L = 4, 256, 1024
CT = C // P
NH = 2
HL = L // NH
NC = 4
DM = C // NC
DI = 128
NS = 16
TAPS = 4
NI = NC * NS
NB = L // P
E = 8
HID = 1024
HB = HID // P
LNS = 6
FP8_MAX = 448.0
FP8_MIN_NORMAL = 2.0 ** -6
LOG_SERIES = 1.0 / 64
SP_STEPS = 7
ROUND_AT = 1.5 * 2.0 ** 20


def build_front(nc, t, x3_dram, xm_dram):
    with ExitStack() as ctx:
        def sb(name, shape, dt=F32):
            return ctx.enter_context(nc.sbuf_tensor(f"{name}_sb", shape, dt))

        def sem(name):
            return ctx.enter_context(nc.semaphore(name))

        psum = ctx.enter_context(nc.psum_tensor("psum", [P, 8, 512], F32))

        ident = sb("ident", [P, P])
        mean_w = sb("mean_w", [P, P])
        group_w = sb("group_w", [P, P])
        sel = sb("sel", [P, 2 * NS, P], BF16)
        in_w = sb("in_w", [P, 2, 2 * DI])
        
        conv_in_w = sb("conv_in_w", [P, 2, TAPS, DI])
        xproj_dt = sb("xproj_dt", [4, DI])
        dtw = sb("dtw", [4, DI])
        dt_w = sb("dt_w", [P, DI])
        bc_w = sb("bc_w", [P, P])
        outp_w = sb("outp_w", [P, DM])
        proj_w = sb("proj_w", [P, CT, C])
        ffn_w = sb("ffn_w", [P, CT, C])
        ffn_q = sb("ffn_q", [P, CT, C], BF16)
        qk_w = sb("qk_w", [P, CT, 2 * C])
        v_w = sb("v_w", [P, CT, C])
        p_w = sb("p_w", [P, CT, C])
        qk_b = sb("qk_b", [P, 2 * C])
        cols = sb("cols", [P, 24])
        NG, NBB, PB, FB, GG, GB, BV, BP_ = (cols[:, 2 * i:2 * i + 2] for i in range(8))
        dcols = sb("dcols", [P, 4])
        scal = sb("scal", [P, 8])
        alog = sb("alog", [P, NS])
        a_neg = sb("a_neg", [P, NS])
        fbias_b = sb("fbias_b", [P, CT], BF16)
        fbias = sb("fbias", [P, CT])
        eps6 = sb("eps6", [P, 1])
        eps5 = sb("eps5", [P, 1])
        small = sb("small", [P, 32])
        g_sum, g_mean, g_sq, g_std, g_rs, g_sc = (small[:, 2 * i:2 * i + 2] for i in range(6))
        s_max, s_neg, s_sum, s_rec = (small[:, 12 + 2 * i:14 + 2 * i] for i in range(4))

        X = sb("X", [P, CT, L])
        X1 = sb("X1", [P, CT, L])
        X2 = sb("X2", [P, CT, L])
        T = sb("T", [P, CT, L])
        SQ = sb("SQ", [P, CT, L])
        STD = sb("STD", [P, L])
        RSTD = sb("RSTD", [P, L])
        PAD = 4
        XN = sb("XN", [P, CT, PAD + L])
        XC = sb("XC", [P, NC, L])
        SZ = sb("SZ", [P, NC, L])
        DT = sb("DT", [P, NC, L])
        DTX = sb("DTX", [P, NC, L])
        BCS = sb("BCS", [P, NC, L], BF16)
        DA = sb("DA", [P, 2, L])
        DBX = sb("DBX", [P, 2, L])
        H = sb("H", [P, 2, L])
        HC = sb("HC", [P, 2, L])
        YF = sb("YF", [P, L])
        YM = T
        sel_f32 = XC[:, :, :].rearrange("p c l -> p (c l)").rearrange("p (s m) -> p s m", m=P)
        conv_rep = SQ[:, 1, 0:TAPS * DI].rearrange("p (k d) -> p k d", k=TAPS)

        xn = XN[:, :, PAD:]
        R1 = YF
        QB = DA[:, :, :].rearrange("p a l -> p (a l)").bitcast(BF16)[:, 0:CT * L].rearrange("p (c l) -> p c l", c=CT)
        QKT = XC[:, :, :].rearrange("p c l -> p (c l)").rearrange("p (n q) -> p n q", n=NB)
        V = SZ[:, 0:2, :]
        CTXT = SZ[:, 2:4, :]
        XG = DT[:, 0:2, :]
        H5 = DT[:, 2:4, :]
        ATT = DTX[:, 0, 0:2 * C].rearrange("p (a d) -> p a d", a=CT)
        ATTT = DTX[:, 1, 0:2 * C].rearrange("p (a d) -> p a d", a=CT)

        brep = psum[:, 0:2, :]
        crep = psum[:, 2:4, :]
        ysum = psum[:, 4:6, :]
        stat = psum[:, 6:8, :]

        def halves(ap):
            return ap.rearrange("p (h n) -> p h n", h=NH)

        w_loaded = sem("w_loaded")
        prep_dve = sem("prep_dve")
        prep_act = sem("prep_act")
        prep_pe = sem("prep_pe")
        x_loaded = sem("x_loaded")
        ln_mean = sem("ln_mean"); ln_cent = sem("ln_cent"); ln_sq = sem("ln_sq"); ln_var = sem("ln_var")
        ln_std = sem("ln_std"); ln_rstd = sem("ln_rstd"); ln_done = sem("ln_done")
        aff_done = sem("aff_done")
        inp_ready = sem("inp_ready"); silu_done = sem("silu_done")
        dtp_ready = sem("dtp_ready"); bcp_ready = sem("bcp_ready")
        sp_abs = sem("sp_abs"); sp_exp = sem("sp_exp"); sp_ln = sem("sp_ln"); sp_relu = sem("sp_relu"); sp_step = sem("sp_step")
        dt_done = sem("dt_done"); dtx_done = sem("dtx_done"); bc_split = sem("bc_split")
        brep_ready = sem("brep_ready"); dbx_ready = sem("dbx_ready"); da_ready = sem("da_ready")
        h_ready = sem("h_ready"); crep_ready = sem("crep_ready"); hc_ready = sem("hc_ready"); ysum_done = sem("ysum_done")
        y_read = sem("y_read"); yf_ready = sem("yf_ready"); op_ready = sem("op_ready"); ym_done = sem("ym_done")
        pj_ready = sem("pj_ready"); x1_done = sem("x1_done")
        q_step = sem("q_step"); ff_ready = sem("ff_ready"); ff_done = sem("ff_done"); x2_done = sem("x2_done")
        g_sum_ready = sem("g_sum_ready"); g_mean_ready = sem("g_mean_ready"); g_cent = sem("g_cent")
        g_sq_ready = sem("g_sq_ready"); g_var_ready = sem("g_var_ready"); g_std_ready = sem("g_std_ready")
        g_step = sem("g_step"); xg_ready = sem("xg_ready")
        qk_ready = sem("qk_ready"); qk_done = sem("qk_done"); v_ready = sem("v_ready"); v_done = sem("v_done")
        sc_ready = sem("sc_ready"); sm_step = sem("sm_step"); sm_exp = sem("sm_exp"); att_done = sem("att_done")
        at_ready = sem("at_ready"); at_done = sem("at_done"); cx_ready = sem("cx_ready"); cx_done = sem("cx_done")
        po_ready = sem("po_ready"); xh_done = sem("xh_done"); x3_done = sem("x3_done")
        stored = sem("stored")

        block = ctx.enter_context(nc.Block())

        loads = [
            (ident[:, :], t["c_ident"]), (mean_w[:, :], t["c_mean"]), (group_w[:, :], t["c_group"]),
            (sel_f32, t["c_sel"]), (conv_rep[:, :, :], t["conv_rep"]),
            (xproj_dt[:, :], t["xproj"][0:4, :]), (dtw[:, :], t["dtwT"]),
            (in_w[0:DM, 0, :], t["in_wT"]), (in_w[DM:P, 1, :], t["in_wT"]),
            (bc_w[:, :], t["bc_wT"]), (outp_w[:, :], t["outpT"]),
            (proj_w[:, :, :], t["projT"]), (ffn_w[:, :, :], t["ffn_k"]),
            (qk_w[:, :, 0:C], t["wqT"]), (qk_w[:, :, C:2 * C], t["wkT"]), (v_w[:, :, :], t["wvT"]),
            (p_w[:, :, :], t["wpT"]), (qk_b[:, :], t["qk_b"]),
            (cols[:, 0:16], t["cols"]), (dcols[:, 0:3], t["dcols"]), (scal[:, 0:3], t["scal"]),
            (alog[:, :], t["alog"]),
        ]
        W_ALL = 16 * len(loads)

        @block.sync
        def _(sp):
            for dst, src in loads:
                sp.dma_start(dst, src).then_inc(w_loaded, 16)

            def store(b):
                sp.wait_ge(x3_done, (b + 1) * 4)
                sp.dma_start(x3_dram[b], X2[:, :, :]).then_inc(stored, 16)
                sp.wait_ge(ln_done, (b + 1) * 2 * LNS)
                sp.dma_start(xm_dram[b], T[:, :, :]).then_inc(stored, 16)

            sp.dma_start(X[:, :, :], t["x"][0]).then_inc(x_loaded, 16)
            with sp.Fori(1, B) as b:
                sp.wait_ge(x1_done, b * 4)
                sp.dma_start(X[:, :, :], t["x"][b]).then_inc(x_loaded, 16)
                store(b - 1)
            store(B - 1)
            sp.wait_ge(stored, B * 32)

        @block.tensor
        def _(pe):
            def mm(o, lhsT, rhs, start, stop, **k):
                return nc.tensor.matmul(o, lhsT, rhs, start=start, stop=stop, **k)

            def layer_norm(k, b, src):
                n = (b * LNS + k) * 2
                pe.wait_ge(ln_std, n)
                for h in range(NH):
                    s = slice(h * HL, (h + 1) * HL)
                    for c in range(CT):
                        i = mm(psum[:, 6 + h, :], mean_w[:, :], src[:, c, s], c == 0, c == CT - 1)
                    i.then_inc(ln_mean, 1)
                for h in range(NH):
                    s = slice(h * HL, (h + 1) * HL)
                    pe.wait_ge(ln_sq, n + h + 1)
                    for c in range(CT):
                        i = mm(psum[:, 6 + h, :], mean_w[:, :], SQ[:, c, s], c == 0, c == CT - 1)
                    i.then_inc(ln_var, 1)

            def linear(w, src, bank, done):
                for o in range(CT):
                    for h in range(NH):
                        for c in range(CT):
                            i = mm(psum[:, bank(2 * o + h), :], w[:, c, o * P:(o + 1) * P],
                                   src[:, c, h * HL:(h + 1) * HL], c == 0, c == CT - 1)
                        i.then_inc(done, 1)

            pe.wait_ge(w_loaded, W_ALL)
            mm(psum[:, 0, 0:DI], xproj_dt[:, :], dtw[:, :], True, True).then_inc(prep_pe, 1)
            pe.wait_ge(prep_dve, PREP_DVE)
            with pe.Fori(0, B) as b:
                pe.wait_ge(x_loaded, b * 16 + 16)
                layer_norm(0, b, X)
                pe.wait_ge(ln_done, b * 2 * LNS + 2)
                layer_norm(1, b, T)
                pe.wait_ge(aff_done, b * 4 + 2)
                for u in range(16):
                    c, kind, h = u // 4, (u // 2) % 2, u % 2
                    if u >= 6:
                        pe.wait_ge(silu_done, b * 16 + u - 5)
                    if kind == 0:
                        for k in range(TAPS):
                            o = PAD - TAPS + 1 + k + h * HL
                            i = mm(psum[:, u % 6, :], conv_in_w[:, c % 2, k, :], XN[:, c // 2, o:o + HL],
                                   k == 0, k == TAPS - 1)
                    else:
                        i = mm(psum[:, u % 6, :], in_w[:, c % 2, DI:2 * DI],
                               XN[:, c // 2, PAD + h * HL:PAD + (h + 1) * HL], True, True)
                    i.then_inc(inp_ready, 1)
                pe.wait_ge(silu_done, b * 16 + 16)
                for c in range(NC):
                    if c >= 2:
                        pe.wait_ge(sp_abs, b * NC + c - 1)
                        pe.wait_ge(sp_relu, b * NC + c - 1)
                    for h in range(NH):
                        i = mm(psum[:, 2 * (c % 2) + h, :], dt_w[:, :], XC[:, c, h * HL:(h + 1) * HL], True, True)
                    i.then_inc(dtp_ready, 1)
                    if c >= 1:
                        pe.wait_ge(bc_split, (b * NC + c - 1) * 4 + 2)
                    for h in range(NH):
                        i = mm(psum[:, 4 + h, :], bc_w[:, :], XC[:, c, h * HL:(h + 1) * HL], True, True)
                    i.then_inc(bcp_ready, 1)
                pe.wait_ge(bc_split, b * 4 * NC + 4 * NC)
                pe.wait_ge(sp_relu, b * NC + NC)
                pe.wait_ge(sp_abs, b * NC + NC)

                def b_rows(c, s, i):
                    pe.wait_ge(dbx_ready, i)
                    for h in range(NH):
                        m = mm(psum[:, h, :], sel[:, s, :], BCS[:, c, h * HL:(h + 1) * HL], True, True)
                    m.then_inc(brep_ready, 1)

                def c_rows(c, s, i):
                    pe.wait_ge(hc_ready, i)
                    for h in range(NH):
                        m = mm(psum[:, 2 + h, :], sel[:, NS + s, :], BCS[:, c, h * HL:(h + 1) * HL], True, True)
                    m.then_inc(crep_ready, 1)

                def sum_states(slot, i, first, last):
                    pe.wait_ge(hc_ready, i + 1)
                    for h in range(NH):
                        m = mm(psum[:, 4 + h, :], ident[:, :], HC[:, slot, h * HL:(h + 1) * HL], first, last,
                               skip_group_check=True)
                    m.then_inc(ysum_done, 1)

                def out_proj(c):
                    pe.wait_ge(yf_ready, b * NC + c + 1)
                    if c:
                        pe.wait_ge(ym_done, b * NC + c)
                    for h in range(NH):
                        p0 = DM * (c % 2)
                        m = mm(psum[p0:p0 + DM, 6 + h, :], outp_w[:, :], YF[:, h * HL:(h + 1) * HL], True, True)
                    m.then_inc(op_ready, 1)

                b0 = b * NI
                b_rows(0, 0, b0)
                b_rows(0, 1, b0 + 1)
                for c in range(NC):
                    i = b0 + c * NS
                    b_rows(c, 2, i + 2)
                    c_rows(c, 0, i)
                    if c:
                        sum_states(1, i - 1, False, True)
                    b_rows(c, 3, i + 3)
                    c_rows(c, 1, i + 1)
                    if c:
                        pe.wait_ge(y_read, b * NC + c)
                    sum_states(0, i, True, False)
                    if c:
                        out_proj(c - 1)
                    with pe.Fori(2, NS - 3, 2) as s:
                        for d in range(2):
                            b_rows(c, s + (2 + d), i + s + (2 + d))
                            c_rows(c, s + d, i + s + d)
                            sum_states((1 + d) % 2, i + s + (d - 1), False, False)
                    for s in (14, 15):
                        if c + 1 < NC:
                            b_rows(c + 1, s - 14, i + s + 2)
                        c_rows(c, s, i + s)
                        sum_states((s - 1) % 2, i + s - 1, False, False)
                sum_states(1, b0 + NI - 1, False, True)
                out_proj(NC - 1)

                pe.wait_ge(ym_done, b * NC + NC)
                layer_norm(2, b, YM)
                pe.wait_ge(aff_done, b * 4 + 4)
                linear(proj_w, xn, lambda u: u, pj_ready)
                pe.wait_ge(x1_done, b * 4 + 4)
                layer_norm(3, b, X1)
                pe.wait_ge(q_step, b * 6 + 6)
                linear(ffn_q, QB, lambda u: u, ff_ready)
                pe.wait_ge(x2_done, b + 1)
                layer_norm(4, b, X2)
                pe.wait_ge(g_sum_ready, b + 1)
                mm(psum[:, 6, 0:2], group_w[:, :], g_sum, True, True).then_inc(g_mean_ready, 1)
                pe.wait_ge(g_sq_ready, b * 2 + 2)
                mm(psum[:, 7, 0:2], group_w[:, :], g_sq, True, True).then_inc(g_var_ready, 1)
                pe.wait_ge(xg_ready, b * 2 + 2)
                for n in range(NB):
                    if n >= 4:
                        pe.wait_ge(qk_done, b * NB + n - 3)
                    for c in range(CT):
                        i = mm(psum[:, n % 4, :], XG[:, c, n * P:(n + 1) * P], qk_w[:, c, :], c == 0, c == CT - 1)
                    i.then_inc(qk_ready, 1)
                for u in range(4):
                    o, h = u // 2, u % 2
                    if u >= 2:
                        pe.wait_ge(v_done, b * 4 + u - 1)
                    for c in range(CT):
                        i = mm(psum[:, 4 + u % 2, :], v_w[:, c, o * P:(o + 1) * P], XG[:, c, h * HL:(h + 1) * HL],
                               c == 0, c == CT - 1)
                    i.then_inc(v_ready, 1)
                pe.wait_ge(qk_done, b * NB + NB)
                for a in range(CT):
                    for n in range(NB):
                        i = mm(psum[:, a, 0:C], QKT[:, n, a * P:(a + 1) * P], QKT[:, n, C:2 * C], n == 0, n == NB - 1)
                    i.then_inc(sc_ready, 1)
                pe.wait_ge(att_done, b * 2 + 2)
                for a in range(CT):
                    for d in range(CT):
                        i = nc.tensor.transpose(psum[:, 2, (2 * d + a) * P:(2 * d + a + 1) * P],
                                                ATT[:, a, d * P:(d + 1) * P], ident[:, :])
                i.then_inc(at_ready, 1)
                pe.wait_ge(at_done, b + 1)
                pe.wait_ge(v_done, b * 4 + 4)
                for a in range(CT):
                    for h in range(NH):
                        u = 2 * a + h
                        for d in range(CT):
                            i = mm(psum[:, (3 + u) % 6, :], ATTT[:, d, a * P:(a + 1) * P], V[:, d, h * HL:(h + 1) * HL],
                                   d == 0, d == CT - 1)
                        i.then_inc(cx_ready, 1)
                pe.wait_ge(cx_done, b * 4 + 4)
                linear(p_w, CTXT, lambda u: u, po_ready)
                pe.wait_ge(x3_done, b * 4 + 4)
                layer_norm(5, b, X2)

        @block.scalar
        def _(act):
            def layer_norm(k, b, eps):
                n = (b * LNS + k) * 2
                for h in range(NH):
                    s = slice(h * HL, (h + 1) * HL)
                    act.wait_ge(ln_cent, n + h + 1)
                    nc.scalar.activation(SQ[:, :, s], T[:, :, s], ACT.Square).then_inc(ln_sq, 1)
                for h in range(NH):
                    s = slice(h * HL, (h + 1) * HL)
                    act.wait_ge(ln_var, n + h + 1)
                    nc.scalar.activation(STD[:, s], psum[:, 6 + h, :], ACT.Sqrt, bias=eps[:, :]).then_inc(ln_std, 1)

            def affine(k, b, m):
                act.wait_ge(ln_done, (b * LNS + k) * 2 + 2)
                for c in range(CT):
                    nc.scalar.activation(xn[:, c, :], T[:, c, :], ACT.Identity, scale=NG[:, c:c + 1],
                                         bias=NBB[:, c:c + 1]).then_inc(aff_done, 1)

            act.wait_ge(w_loaded, W_ALL)
            nc.scalar.activation(a_neg[:, :], alog[:, :], ACT.Exp).then_inc(prep_act, 1)
            act.wait_ge(prep_dve, PREP_DVE)
            with act.Fori(0, B) as b:
                layer_norm(0, b, eps6)
                layer_norm(1, b, eps5)
                affine(1, b, 0)
                for u in range(16):
                    c, kind, h = u // 4, (u // 2) % 2, u % 2
                    act.wait_ge(inp_ready, b * 16 + u + 1)
                    if kind == 0:
                        i = nc.scalar.activation(XC[:, c, h * HL:(h + 1) * HL], psum[:, u % 6, :], ACT.Silu,
                                                 bias=dcols[:, 0:1])
                    else:
                        i = nc.scalar.activation(SZ[:, c, h * HL:(h + 1) * HL], psum[:, u % 6, :], ACT.Silu)
                    i.then_inc(silu_done, 1)
                for c in range(NC):
                    n = b * NC + c
                    tmp = T[:, c % 2, :]
                    act.wait_ge(dtp_ready, n + 1)
                    if c >= 2:
                        act.wait_ge(dt_done, n - 1)
                    nc.scalar.activation(halves(tmp), psum[:, 2 * (c % 2):2 * (c % 2) + 2, :], ACT.Abs,
                                         bias=dcols[:, 1:2]).then_inc(sp_abs, 1)
                    act.wait_ge(sp_abs, n + 1)
                    nc.scalar.activation(tmp, tmp, ACT.Exp, scale=-1.0).then_inc(sp_exp, 1)
                    act.wait_ge(sp_exp, n + 1)
                    if c:
                        act.wait_ge(sp_step, (n - 1) * SP_STEPS + 6)
                    nc.scalar.activation(STD[:, :], tmp, ACT.Ln, bias=1.0).then_inc(sp_ln, 1)
                for c in range(NC):
                    act.wait_ge(dt_done, b * NC + c + 1)
                    i = b * NI + c * NS

                    def decay(s, d, free):
                        if free is not None:
                            act.wait_ge(h_ready, free)
                        nc.scalar.activation(DA[:, d, :], DT[:, c, :], ACT.Exp,
                                             scale=a_neg[:, bass.ds(s, 1)]).then_inc(da_ready, 1)
                    decay(0, 0, i - 1 if c else None)
                    decay(1, 1, i if c else None)
                    with act.Fori(2, NS - 1, 2) as s:
                        decay(s, 0, i + s - 1)
                        decay(s + 1, 1, i + s)
                layer_norm(2, b, eps5)
                affine(2, b, 1)
                layer_norm(3, b, eps5)
                for u in range(4):
                    o, h = u // 2, u % 2
                    act.wait_ge(ff_ready, b * 4 + u + 1)
                    nc.scalar.activation(SQ[:, o, h * HL:(h + 1) * HL], psum[:, u, :], ACT.Identity,
                                         scale=scal[:, 5:6], bias=fbias[:, o:o + 1]).then_inc(ff_done, 1)
                layer_norm(4, b, eps6)
                act.wait_ge(g_cent, b * 2 + 2)
                for c in range(CT):
                    nc.scalar.activation(SQ[:, c, :], XG[:, c, :], ACT.Square,
                                         accum_out=g_sq[:, c:c + 1]).then_inc(g_sq_ready, 1)
                act.wait_ge(g_var_ready, b + 1)
                nc.scalar.activation(g_std, psum[:, 7, 0:2], ACT.Sqrt, bias=eps5[:, :]).then_inc(g_std_ready, 1)
                for u in range(4):
                    o, h = u // 2, u % 2
                    act.wait_ge(v_ready, b * 4 + u + 1)
                    nc.scalar.activation(V[:, o, h * HL:(h + 1) * HL], psum[:, 4 + u % 2, :], ACT.Identity,
                                         bias=BV[:, o:o + 1]).then_inc(v_done, 1)
                act.wait_ge(sm_step, b * 3 + 2)
                for a in range(CT):
                    nc.scalar.activation(ATT[:, a, :], psum[:, a, 0:C], ACT.Exp, scale=float(C) ** -0.5,
                                         bias=s_neg[:, a:a + 1], accum_out=s_sum[:, a:a + 1]).then_inc(sm_exp, 1)
                act.wait_ge(at_ready, b + 1)
                nc.scalar.activation(ATTT[:, :, :], psum[:, 2, :].rearrange("p (a d) -> p a d", a=CT),
                                     ACT.Copy).then_inc(at_done, 1)
                for u in range(4):
                    act.wait_ge(cx_ready, b * 4 + u + 1)
                    nc.scalar.activation(CTXT[:, u // 2, (u % 2) * HL:(u % 2 + 1) * HL], psum[:, (3 + u) % 6, :],
                                         ACT.Copy).then_inc(cx_done, 1)
                layer_norm(5, b, eps5)

        @block.vector
        def _(dve):
            v = nc.vector

            def layer_norm(k, b, src, dst):
                n = (b * LNS + k) * 2
                for h in range(NH):
                    s = slice(h * HL, (h + 1) * HL)
                    dve.wait_ge(ln_mean, n + h + 1)
                    v.tensor_tensor(T[:, :, s], src[:, :, s],
                                    psum[:, 6 + h, :].unsqueeze(1).broadcast_to((P, CT, HL)),
                                    ALU.subtract).then_inc(ln_cent, 1)
                for h in range(NH):
                    s = slice(h * HL, (h + 1) * HL)
                    dve.wait_ge(ln_std, n + h + 1)
                    v.reciprocal(RSTD[:, s], STD[:, s]).then_inc(ln_rstd, 1)
                    dve.wait_ge(ln_rstd, n + h + 1)
                    v.tensor_tensor(dst[:, :, s], T[:, :, s], RSTD[:, s].unsqueeze(1).broadcast_to((P, CT, HL)),
                                    ALU.mult).then_inc(ln_done, 1)

            steps = [0]

            def prep(i):
                steps[0] += 1
                i.then_inc(prep_dve, 1)
                dve.wait_ge(prep_dve, steps[0])

            def round_fp8(val, mag, dst, inv_scale, done):
                done(v.tensor_scalar(val, val, inv_scale, FP8_MAX, ALU.mult, ALU.min))
                done(v.tensor_scalar(val, val, -FP8_MAX, None, ALU.max))
                done(v.tensor_scalar(mag.bitcast(U32), val.bitcast(U32), 0x7F800000, None, ALU.bitwise_and))
                done(v.tensor_scalar(mag, mag, FP8_MIN_NORMAL, ROUND_AT, ALU.max, ALU.mult))
                done(v.tensor_tensor(val, val, mag, ALU.add))
                done(v.tensor_tensor(dst, val, mag, ALU.subtract))

            def log1p(n, e, relu, dst):
                lo, r, hi = RSTD[:, :], H[:, 0, :], H[:, 1, :]
                done = [0]

                def step(i):
                    done[0] += 1
                    i.then_inc(sp_step, 1)
                    dve.wait_ge(sp_step, n * SP_STEPS + done[0])
                step(v.scalar_tensor_tensor(lo, e, LOG_SERIES, e, ALU.is_lt, ALU.mult))
                step(v.tensor_scalar(r, lo, -1.0 / 4, None, ALU.mult))
                step(v.scalar_tensor_tensor(r, r, 1.0 / 3, lo, ALU.add, ALU.mult))
                step(v.scalar_tensor_tensor(r, r, -1.0 / 2, lo, ALU.add, ALU.mult))
                step(v.scalar_tensor_tensor(r, r, 1.0, lo, ALU.add, ALU.mult))
                dve.wait_ge(sp_ln, n + 1)
                step(v.scalar_tensor_tensor(hi, e, LOG_SERIES, STD[:, :], ALU.is_ge, ALU.mult))
                step(v.tensor_tensor(r, r, hi, ALU.add))
                v.tensor_tensor(dst, relu, r, ALU.add).then_inc(dt_done, 1)

            v.memset(eps6[:, :], 1e-6)
            v.memset(eps5[:, :], 1e-5)
            prep(v.memset(XN[:, :, 0:PAD], 0.0))
            dve.wait_ge(w_loaded, W_ALL)
            prep(v.tensor_copy(sel[:, :, :], sel_f32))
            for par in range(2):
                lo = DM * (1 - par)
                prep(v.memset(in_w[lo:lo + DM, par, :], 0.0))
            for par in range(2):
                prep(v.tensor_tensor(conv_in_w[:, par, :, :], in_w[:, par, 0:DI].unsqueeze(1).broadcast_to((P, TAPS, DI)),
                                     conv_rep[:, :, :], ALU.mult))
            dve.wait_ge(prep_pe, 1)
            prep(v.tensor_copy(dt_w[:, :], psum[:, 0, 0:DI]))
            dve.wait_ge(prep_act, 1)
            prep(v.tensor_scalar(a_neg[:, :], a_neg[:, :], -1.0, None, ALU.mult))
            prep(v.reciprocal(scal[:, 3:5], scal[:, 1:3]))
            prep(v.tensor_tensor(scal[:, 5:6], scal[:, 1:2], scal[:, 2:3], ALU.mult))
            prep(v.tensor_copy(fbias_b[:, :], FB))
            prep(v.tensor_copy(fbias[:, :], fbias_b[:, :]))
            fw = SQ[:, 0, 0:CT * C].rearrange("p (c o) -> p c o", c=CT)
            round_fp8(ffn_w[:, :, :], fw, ffn_q[:, :, :], scal[:, 4:5], prep)
            assert steps[0] == PREP_DVE

            with dve.Fori(0, B) as b:
                dve.wait_ge(x_loaded, b * 16 + 16)
                dve.wait_ge(stored, b * 32)
                layer_norm(0, b, X, T)
                dve.wait_ge(ln_done, b * 2 * LNS + 2)
                layer_norm(1, b, T, T)
                for c in range(NC):
                    n = b * NC + c
                    relu = SQ[:, c % 2, :]
                    dve.wait_ge(sp_abs, n + 1)
                    v.tensor_scalar(halves(relu), psum[:, 2 * (c % 2):2 * (c % 2) + 2, :], dcols[:, 1:2], 0.0,
                                    ALU.add, ALU.max).then_inc(sp_relu, 1)
                    dve.wait_ge(bcp_ready, n + 1)
                    v.tensor_copy(halves(BCS[:, c, :]), psum[:, 4:6, :]).then_inc(bc_split, 1)
                    dve.wait_ge(bc_split, n * 4 + 1)
                    v.tensor_tensor(halves(R1[64:128, :]), psum[64:128, 4:6, :], halves(BCS[64:128, c, :]),
                                    ALU.subtract).then_inc(bc_split, 1)
                    dve.wait_ge(bc_split, n * 4 + 2)
                    v.tensor_copy(BCS[64:128, c, :], R1[64:128, :]).then_inc(bc_split, 1)
                    dve.wait_ge(bc_split, n * 4 + 3)
                    v.tensor_tensor(BCS[96:128, c, :], R1[96:128, :], BCS[96:128, c, :],
                                    ALU.subtract).then_inc(bc_split, 1)
                    dve.wait_ge(sp_exp, n + 1)
                    log1p(n, T[:, c % 2, :], relu, DT[:, c, :])
                    dve.wait_ge(dt_done, n + 1)
                    v.tensor_tensor(DTX[:, c, :], DT[:, c, :], XC[:, c, :], ALU.mult).then_inc(dtx_done, 1)
                dve.wait_ge(dtx_done, b * NC + NC)
                dve.wait_ge(bc_split, b * 4 * NC + 4 * NC)

                b0 = b * NI

                def drive(c, slot, i, again=True):
                    if again:
                        dve.wait_ge(h_ready, i - 1)
                    dve.wait_ge(brep_ready, i + 1)
                    v.tensor_tensor(halves(DBX[:, slot, :]), brep, halves(DTX[:, c, :]), ALU.mult).then_inc(dbx_ready, 1)

                def scan(slot, i, again=True):
                    if again:
                        dve.wait_ge(hc_ready, i - 1)
                    dve.wait_ge(da_ready, i + 1)
                    dve.wait_ge(dbx_ready, i + 1)
                    v.tensor_tensor_scan(H[:, slot, :], DA[:, slot, :], DBX[:, slot, :], 0.0, ALU.mult,
                                         ALU.add).then_inc(h_ready, 1)

                def read_out(slot, i):
                    dve.wait_ge(h_ready, i + 1)
                    dve.wait_ge(crep_ready, i + 1)
                    v.tensor_tensor(halves(HC[:, slot, :]), crep, halves(H[:, slot, :]), ALU.mult).then_inc(hc_ready, 1)

                def gate(c):
                    n = b * NC + c
                    dve.wait_ge(ysum_done, b0 + (c + 1) * NS)
                    if c:
                        dve.wait_ge(op_ready, n)
                    v.scalar_tensor_tensor(halves(YF[:, :]), halves(XC[:, c, :]), dcols[:, 2:3], ysum, ALU.mult,
                                           ALU.add).then_inc(y_read, 1)
                    dve.wait_ge(y_read, n + 1)
                    v.tensor_tensor(YF[:, :], YF[:, :], SZ[:, c, :], ALU.mult).then_inc(yf_ready, 1)

                def skip(c):
                    dve.wait_ge(op_ready, b * NC + c + 1)
                    p0 = DM * (c % 2)
                    v.scalar_tensor_tensor(halves(YM[p0:p0 + DM, c // 2, :]), halves(xn[p0:p0 + DM, c // 2, :]),
                                           scal[p0:p0 + DM, 0:1], psum[p0:p0 + DM, 6:8, :], ALU.mult,
                                           ALU.add).then_inc(ym_done, 1)

                def hc_free(i):
                    dve.wait_ge(ysum_done, i - 1)

                drive(0, 0, b0, again=False)
                for c in range(NC):
                    i = b0 + c * NS
                    drive(c, 1, i + 1, again=c > 0)
                    scan(0, i, again=c > 0)
                    if c:
                        hc_free(i - 1)
                        read_out(1, i - 1)
                    drive(c, 0, i + 2)
                    scan(1, i + 1, again=c > 0)
                    if c:
                        hc_free(i)
                    read_out(0, i)
                    if c:
                        gate(c - 1)
                    with dve.Fori(2, NS - 3, 2) as s:
                        for d in range(2):
                            drive(c, (1 + d) % 2, i + s + (1 + d))
                            scan(d, i + s + d)
                            hc_free(i + s + (d - 1))
                            read_out((1 + d) % 2, i + s + (d - 1))
                    drive(c, 1, i + 15)
                    scan(0, i + 14)
                    hc_free(i + 13)
                    read_out(1, i + 13)
                    if c + 1 < NC:
                        drive(c + 1, 0, i + 16)
                    scan(1, i + 15)
                    hc_free(i + 14)
                    read_out(0, i + 14)
                    if c:
                        skip(c - 1)
                hc_free(b0 + NI - 1)
                read_out(1, b0 + NI - 1)
                gate(NC - 1)
                skip(NC - 1)

                dve.wait_ge(ym_done, b * NC + NC)
                layer_norm(2, b, YM, T)
                for u in range(4):
                    o, h = u // 2, u % 2
                    s = slice(h * HL, (h + 1) * HL)
                    dve.wait_ge(pj_ready, b * 4 + u + 1)
                    v.scalar_tensor_tensor(X1[:, o, s], psum[:, u, :], PB[:, o:o + 1], X[:, o, s], ALU.add,
                                           ALU.add).then_inc(x1_done, 1)
                dve.wait_ge(x1_done, b * 4 + 4)
                layer_norm(3, b, X1, T)
                dve.wait_ge(ln_done, b * 2 * LNS + 8)
                qs = [0]

                def q_done(i):
                    qs[0] += 1
                    i.then_inc(q_step, 1)
                    dve.wait_ge(q_step, b * 6 + qs[0])
                round_fp8(T[:, :, :], SQ[:, :, :], QB, scal[:, 3:4], q_done)
                dve.wait_ge(ff_done, b * 4 + 4)
                v.tensor_tensor(X2[:, :, :], X1[:, :, :], SQ[:, :, :], ALU.add).then_inc(x2_done, 1)
                dve.wait_ge(x2_done, b + 1)
                layer_norm(4, b, X2, H5)
                dve.wait_ge(ln_done, b * 2 * LNS + 10)
                v.tensor_reduce(g_sum, H5, AX_X, ALU.add).then_inc(g_sum_ready, 1)
                v.tensor_tensor(X2[:, :, :], X2[:, :, :], H5, ALU.add).then_inc(xh_done, 1)
                dve.wait_ge(g_mean_ready, b + 1)
                v.tensor_copy(g_mean, psum[:, 6, 0:2]).then_inc(g_step, 1)
                dve.wait_ge(g_step, b * 3 + 1)
                for c in range(CT):
                    v.tensor_scalar(XG[:, c, :], H5[:, c, :], g_mean[:, c:c + 1], None, ALU.subtract).then_inc(g_cent, 1)
                dve.wait_ge(g_std_ready, b + 1)
                v.reciprocal(g_rs, g_std).then_inc(g_step, 1)
                dve.wait_ge(g_step, b * 3 + 2)
                v.tensor_tensor(g_sc, g_rs, GG, ALU.mult).then_inc(g_step, 1)
                dve.wait_ge(g_step, b * 3 + 3)
                for c in range(CT):
                    v.tensor_scalar(XG[:, c, :], XG[:, c, :], g_sc[:, c:c + 1], GB[:, c:c + 1], ALU.mult,
                                    ALU.add).then_inc(xg_ready, 1)
                for n in range(NB):
                    dve.wait_ge(qk_ready, b * NB + n + 1)
                    v.tensor_tensor(QKT[:, n, :], psum[:, n % 4, :], qk_b[:, :], ALU.add).then_inc(qk_done, 1)
                dve.wait_ge(sc_ready, b * 2 + 2)
                v.tensor_reduce(s_max, psum[:, 0:2, 0:C], AX_X, ALU.max).then_inc(sm_step, 1)
                dve.wait_ge(sm_step, b * 3 + 1)
                v.tensor_scalar(s_neg, s_max, -(float(C) ** -0.5), None, ALU.mult).then_inc(sm_step, 1)
                dve.wait_ge(sm_exp, b * 2 + 2)
                v.reciprocal(s_rec, s_sum).then_inc(sm_step, 1)
                dve.wait_ge(sm_step, b * 3 + 3)
                for a in range(CT):
                    v.tensor_scalar(ATT[:, a, :], ATT[:, a, :], s_rec[:, a:a + 1], None, ALU.mult).then_inc(att_done, 1)
                dve.wait_ge(xh_done, b + 1)
                for u in range(4):
                    o, h = u // 2, u % 2
                    s = slice(h * HL, (h + 1) * HL)
                    dve.wait_ge(po_ready, b * 4 + u + 1)
                    v.scalar_tensor_tensor(X2[:, o, s], psum[:, u, :], BP_[:, o:o + 1], X2[:, o, s], ALU.add,
                                           ALU.add).then_inc(x3_done, 1)
                dve.wait_ge(x3_done, b * 4 + 4)
                layer_norm(5, b, X2, T)


PREP_DVE = 1 + 1 + 2 + 2 + 1 + 1 + 1 + 1 + 1 + 1 + 6


def lay_out(inp):
    import numpy as np
    f = {k: np.asarray(v) for k, v in inp.items()}
    a = {}

    def by_tile(w):
        return np.ascontiguousarray(w.reshape(w.shape[0] // P, P, w.shape[1]).transpose(1, 0, 2))

    def cols(v):
        return v.reshape(-1, P).T

    c = "L0_conv_"
    a["x"] = np.ascontiguousarray(f["x"].reshape(B, CT, P, L).transpose(0, 2, 1, 3))
    a["conv_rep"] = np.ascontiguousarray(np.broadcast_to(f[c + "conv_w"].T, (P, TAPS, DI)))
    a["xproj"] = f[c + "x_proj_w"]
    a["dtwT"] = np.ascontiguousarray(f[c + "dt_proj_w"].T)
    a["in_wT"] = np.ascontiguousarray(f[c + "in_proj_w"].T)
    a["bc_wT"] = np.ascontiguousarray(np.tile(f[c + "x_proj_w"][4:36], (4, 1)).T)
    a["outpT"] = np.ascontiguousarray(f[c + "out_proj_w"].T)
    a["projT"] = by_tile(f[c + "proj_w"].T)
    a["ffn_k"] = by_tile(f["L0_ffn_kernel"])
    for k in "qkvp":
        a[f"w{k}T"] = by_tile(f[f"L1_conv_w{k}"].T)
    a["qk_b"] = np.ascontiguousarray(np.broadcast_to(np.concatenate([f["L1_conv_bq"], f["L1_conv_bk"]]), (P, 2 * C)))
    a["cols"] = np.ascontiguousarray(np.concatenate([cols(f[k]) for k in (
        c + "norm_g", c + "norm_b", c + "proj_b", "L0_ffn_bias", "L1_conv_gn_gamma", "L1_conv_gn_beta",
        "L1_conv_bv", "L1_conv_bp")], axis=1))
    a["dcols"] = np.ascontiguousarray(np.stack([f[c + k] for k in ("conv_b", "dt_proj_b", "D_param")], axis=1))
    a["scal"] = np.ascontiguousarray(np.broadcast_to(np.concatenate([
        f[c + "skip_scale"], f["L0_ffn_input_scale"], f["L0_ffn_kernel_scale"]]), (P, 3)))
    a["alog"] = f[c + "A_log"]
    a["c_ident"] = np.eye(P, dtype=np.float32)
    a["c_mean"] = np.full((P, P), 1.0 / C, np.float32)
    g = np.arange(P) // 8
    a["c_group"] = (g[:, None] == g[None, :]).astype(np.float32) / (8 * L)
    part = np.arange(P)
    used = (part < 32) | (part >= 64)
    a["c_sel"] = np.broadcast_to(((part[:, None] % 32 == np.arange(32)[None, :]) & used[:, None])[:, :, None],
                                 (P, 32, P)).astype(np.float32)
    m = "L1_ffn_"
    a["gateT"] = by_tile(f[m + "gate_w"].T)
    a["w1T"] = np.ascontiguousarray(f[m + "w1"].reshape(E, HID, CT, P).transpose(0, 3, 2, 1))
    a["w2T"] = np.ascontiguousarray(f[m + "w2"].reshape(E, C, HB, P).transpose(0, 3, 2, 1))
    a["b1"] = np.ascontiguousarray(f[m + "b1"].reshape(E, HB, P).transpose(2, 0, 1))
    a["b2"] = f[m + "b2"]
    a["c_iota"] = np.ascontiguousarray(np.broadcast_to(np.arange(E, dtype=np.float32), (P, NB, E)))
    return a


def build_moe(nc, t, x3_dram, xm_dram, out):
    with ExitStack() as ctx:
        def sb(name, shape, dt=F32):
            return ctx.enter_context(nc.sbuf_tensor(f"{name}_sb", shape, dt))

        def sem(name):
            return ctx.enter_context(nc.semaphore(name))

        psum = ctx.enter_context(nc.psum_tensor("psum_moe", [P, 8, 512], F32))
        ident = sb("m_ident", [P, P])
        gate_w = sb("gate_w", [P, CT, E])
        b1 = sb("b1", [P, E, HB])
        b2 = sb("b2", [E, C])
        iota = sb("iota", [P, NB, E])
        W1 = [sb(f"w1_{i}", [P, CT, HID]) for i in range(2)]
        W2 = [sb(f"w2_{i}", [P, HB, C]) for i in range(2)]
        XM = sb("XM", [P, CT, L])
        X3 = sb("X3", [P, CT, L])
        HT = sb("HT", [P, 2, L])
        ACC = sb("ACC", [P, NB, C])
        LG, EQ, CAND, OH1, OH2, LG2, COMB = (sb(n, [P, NB, E]) for n in ("lg", "eq", "cand", "oh1", "oh2", "lg2", "comb"))
        M1, M2, IDX, DIF, EX, P1, P2 = (sb(n, [P, NB]) for n in ("m1", "m2", "idx", "dif", "ex", "p1", "p2"))
        combT = sb("combT", [E, L])

        c_loaded = sem("c_loaded"); xm_loaded = sem("xm_loaded"); x3_loaded = sem("x3_loaded")
        w1_loaded = [sem(f"w1_loaded{i}") for i in range(2)]
        w2_loaded = [sem(f"w2_loaded{i}") for i in range(2)]
        gate_ready = sem("gate_ready"); route = sem("route"); route_exp = sem("route_exp")
        ct_ready = sem("ct_ready"); ct_done = sem("ct_done"); b2_ready = sem("b2_ready"); acc_init = sem("acc_init")
        h_up = sem("h_up"); h_used = sem("h_used"); route_w = sem("route_w"); y_tile = sem("y_tile"); h_act = sem("h_act"); y_ready = [sem(f"y_ready{i}") for i in range(2)]; y_added = sem("y_added")
        t_ready = sem("t_ready"); o_done = sem("o_done"); out_stored = sem("out_stored")
        block = ctx.enter_context(nc.Block())
        ROUTE = 16

        @block.sync
        def _(sp):
            consts = [(ident[:, :], t["c_ident"]), (gate_w[:, :, :], t["gateT"]), (b1[:, :, :], t["b1"]),
                      (b2[:, :], t["b2"]), (iota[:, :, :], t["c_iota"])]
            for d, s in consts:
                sp.dma_start(d, s).then_inc(c_loaded, 16)
            with sp.Fori(0, B) as b:
                sp.wait_ge(h_up, b * E * HB)
                sp.wait_ge(gate_ready, b)
                sp.dma_start(XM[:, :, :], xm_dram[b]).then_inc(xm_loaded, 16)
                sp.wait_ge(out_stored, b * 16)
                sp.dma_start(X3[:, :, :], x3_dram[b]).then_inc(x3_loaded, 16)
                with sp.Fori(0, E // 2) as e2:
                    for i in range(2):
                        sp.wait_ge(y_ready[i], b * (E // 2) + e2)
                        sp.dma_start(W1[i][:, :, :], t["w1T"][e2 * 2 + i]).then_inc(w1_loaded[i], 16)
                        sp.dma_start(W2[i][:, :, :], t["w2T"][e2 * 2 + i]).then_inc(w2_loaded[i], 16)
                sp.wait_ge(o_done, b * 4 + 4)
                sp.dma_start(out[b], X3[:, :, :]).then_inc(out_stored, 16)
            sp.wait_ge(out_stored, B * 16)

        @block.tensor
        def _(pe):
            def mm(o, lhsT, rhs, start, stop, **k):
                return nc.tensor.matmul(o, lhsT, rhs, start=start, stop=stop, **k)

            pe.wait_ge(c_loaded, 16 * 5)
            with pe.Fori(0, B) as b:
                pe.wait_ge(xm_loaded, b * 16 + 16)
                pe.wait_ge(o_done, b * 4)
                for n in range(NB):
                    for c in range(CT):
                        i = mm(psum[:, 0, n * E:(n + 1) * E], XM[:, c, n * P:(n + 1) * P], gate_w[:, c, :],
                               c == 0, c == CT - 1)
                i.then_inc(gate_ready, 1)
                pe.wait_ge(route, b * ROUTE + ROUTE)
                for n in range(NB):
                    i = nc.tensor.transpose(psum[0:E, 1 + n // 4, (n % 4) * P:(n % 4 + 1) * P], COMB[:, n, :], ident[:, :])
                i.then_inc(ct_ready, 1)
                pe.wait_ge(ct_done, b + 1)
                for n in range(NB):
                    i = mm(psum[:, 4 + n // 2, (n % 2) * C:(n % 2 + 1) * C], combT[:, n * P:(n + 1) * P], b2[:, :],
                           True, True)
                i.then_inc(b2_ready, 1)
                with pe.Fori(0, E // 2) as e2:
                    for i2 in range(2):
                        pe.wait_ge(acc_init, b + 1)
                        visit = b * E + e2 * 2 + i2
                        pe.wait_ge(w1_loaded[i2], b * (E // 2) * 16 + e2 * 16 + 16)
                        pe.wait_ge(w2_loaded[i2], b * (E // 2) * 16 + e2 * 16 + 16)

                        def up(k):
                            if k >= 2:
                                pe.wait_ge(h_act, visit * HB + k - 1)
                            for h in range(NH):
                                for c in range(CT):
                                    m = mm(psum[:, 2 * (k % 2) + h, :], W1[i2][:, c, k * P:(k + 1) * P],
                                           XM[:, c, h * HL:(h + 1) * HL], c == 0, c == CT - 1)
                            m.then_inc(h_up, 1)
                        pe.wait_ge(h_act, visit * HB)
                        up(0)
                        pe.wait_ge(y_added, visit)
                        for k in range(HB):
                            if k + 1 < HB:
                                up(k + 1)
                            pe.wait_ge(h_act, visit * HB + k + 1)
                            for n in range(NB):
                                m = mm(psum[:, 4 + n // 2, (n % 2) * C:(n % 2 + 1) * C],
                                       HT[:, k % 2, n * P:(n + 1) * P], W2[i2][:, k, :],
                                       k == 0 and n % 2 == 0, k == HB - 1, skip_group_check=True)
                            if k == HB - 1:
                                m.then_inc(y_ready[i2], 1)
                            else:
                                m.then_inc(h_used, 1)
                pe.wait_ge(y_added, b * E + E)
                for c in range(CT):
                    for n in range(NB):
                        i = nc.tensor.transpose(psum[:, 2 * c + n // 4, (n % 4) * P:(n % 4 + 1) * P],
                                                ACC[:, n, c * P:(c + 1) * P], ident[:, :])
                        if n % 4 == 3:
                            i.then_inc(t_ready, 1)

        @block.scalar
        def _(act):
            act.wait_ge(c_loaded, 16 * 5)
            with act.Fori(0, B) as b:
                act.wait_ge(route, b * ROUTE + 10)
                nc.scalar.activation(EX[:, :], DIF[:, :], ACT.Exp).then_inc(route_exp, 1)
                act.wait_ge(ct_ready, b + 1)
                nc.scalar.activation(combT[:, :].rearrange("p (h n) -> p h n", h=NH), psum[0:E, 1:3, :],
                                     ACT.Copy).then_inc(ct_done, 1)
                with act.Fori(0, E // 2) as e2:
                    for i2 in range(2):
                        visit = b * E + e2 * 2 + i2
                        for k in range(HB):
                            act.wait_ge(h_up, visit * HB + k + 1)
                            if k >= 2:
                                act.wait_ge(h_used, visit * (HB - 1) + k - 1)
                            nc.scalar.activation(HT[:, k % 2, :].rearrange("p (h n) -> p h n", h=NH),
                                                 psum[:, 2 * (k % 2):2 * (k % 2) + 2, :], ACT.Gelu,
                                                 bias=b1[:, bass.ds(e2 * 2 + i2, 1), k]).then_inc(h_act, 1)

        @block.vector
        def _(dve):
            v = nc.vector

            def wide(x):
                return x.unsqueeze(2).broadcast_to((P, NB, E))

            dve.wait_ge(c_loaded, 16 * 5)
            with dve.Fori(0, B) as b:
                done = [0]

                def step(i):
                    done[0] += 1
                    i.then_inc(route, 1)
                    dve.wait_ge(route, b * ROUTE + done[0])

                def best(logits, m, onehot):
                    step(v.tensor_reduce(m, logits, AX_X, ALU.max))
                    step(v.tensor_tensor(EQ[:, :, :], logits, wide(m), ALU.is_equal))
                    step(v.scalar_tensor_tensor(CAND[:, :, :], EQ[:, :, :], -float(E), iota[:, :, :], ALU.mult, ALU.add))
                    step(v.tensor_reduce(IDX[:, :], CAND[:, :, :], AX_X, ALU.min))
                    step(v.tensor_tensor(onehot, CAND[:, :, :], wide(IDX[:, :]), ALU.is_equal))

                dve.wait_ge(gate_ready, b + 1)
                lg = psum[:, 0, 0:NB * E].rearrange("p (n e) -> p n e", n=NB)
                best(lg, M1[:, :], OH1[:, :, :])
                step(v.scalar_tensor_tensor(LG2[:, :, :], OH1[:, :, :], -3.0e38, lg, ALU.mult, ALU.add))
                step(v.tensor_reduce(M2[:, :], LG2[:, :, :], AX_X, ALU.max))
                step(v.tensor_tensor(EQ[:, :, :], LG2[:, :, :], wide(M2[:, :]), ALU.is_equal))
                step(v.scalar_tensor_tensor(CAND[:, :, :], EQ[:, :, :], -float(E), iota[:, :, :], ALU.mult, ALU.add))
                step(v.tensor_tensor(DIF[:, :], M2[:, :], M1[:, :], ALU.subtract))
                step(v.tensor_reduce(IDX[:, :], CAND[:, :, :], AX_X, ALU.min))
                step(v.tensor_tensor(OH2[:, :, :], CAND[:, :, :], wide(IDX[:, :]), ALU.is_equal))
                dve.wait_ge(route_exp, b + 1)
                step(v.tensor_scalar(P2[:, :], EX[:, :], 1.0, None, ALU.add))
                step(v.reciprocal(P1[:, :], P2[:, :]))
                step(v.tensor_tensor(P2[:, :], EX[:, :], P1[:, :], ALU.mult))
                v.tensor_tensor(OH1[:, :, :], OH1[:, :, :], wide(P1[:, :]), ALU.mult).then_inc(route_w, 1)
                v.tensor_tensor(OH2[:, :, :], OH2[:, :, :], wide(P2[:, :]), ALU.mult).then_inc(route_w, 1)
                dve.wait_ge(route_w, b * 2 + 2)
                step(v.tensor_tensor(COMB[:, :, :], OH1[:, :, :], OH2[:, :, :], ALU.add))
                assert done[0] == ROUTE
                dve.wait_ge(b2_ready, b + 1)
                v.tensor_copy(ACC[:, :, :].rearrange("p (k n) c -> p k (n c)", k=4), psum[:, 4:8, :]).then_inc(acc_init, 1)
                with dve.Fori(0, E // 2) as e2:
                    for i2 in range(2):
                        dve.wait_ge(acc_init, b + 1)
                        dve.wait_ge(y_ready[i2], b * (E // 2) + e2 + 1)
                        dve.wait_ge(y_tile, b * E * NB + e2 * (2 * NB) + i2 * NB)
                        for n in range(NB):
                            m = v.scalar_tensor_tensor(ACC[:, n, :], psum[:, 4 + n // 2, (n % 2) * C:(n % 2 + 1) * C],
                                                       COMB[:, n, bass.ds(e2 * 2 + i2, 1)], ACC[:, n, :],
                                                       ALU.mult, ALU.add)
                            m.then_inc(y_tile, 1)
                        dve.wait_ge(y_tile, b * E * NB + e2 * (2 * NB) + (i2 + 1) * NB)
                        dve.nop().then_inc(y_added, 1)
                dve.wait_ge(x3_loaded, b * 16 + 16)
                for u in range(4):
                    dve.wait_ge(t_ready, b * 4 + u + 1)
                    s = slice((u % 2) * HL, (u % 2 + 1) * HL)
                    v.tensor_tensor(X3[:, u // 2, s], psum[:, u, :], X3[:, u // 2, s], ALU.add).then_inc(o_done, 1)


def kernel(**inputs):
    import numpy as np
    import concourse.bacc as bacc
    from concourse.bass_utils import run_bass_kernel_spmd

    arrays = lay_out(inputs)
    nc = bacc.Bacc("TRN2", target_bir_lowering=False, num_devices=1)
    t = {k: nc.dram_tensor(k, a.shape, mybir.dt.from_np(a.dtype), kind="ExternalInput").ap() for k, a in arrays.items()}
    out = nc.dram_tensor("out", (B, P, CT, L), F32, kind="ExternalOutput").ap()
    x3_dram = nc.dram_tensor("x3_dram", (B, P, CT, L), F32).ap()
    xm_dram = nc.dram_tensor("xm_dram", (B, P, CT, L), F32).ap()
    build_front(nc, t, x3_dram, xm_dram)
    build_moe(nc, t, x3_dram, xm_dram, out)
    r = run_bass_kernel_spmd(nc, [arrays], core_ids=[0])
    got = r.results[0]["out"]
    return np.ascontiguousarray(got.transpose(0, 2, 1, 3)).reshape(B, C, 32, 32)
```

```python
from contextlib import ExitStack

import concourse.bass as bass
from concourse import mybir

F32 = mybir.dt.float32
BF16 = mybir.dt.bfloat16
U32 = mybir.dt.uint32
ALU = mybir.AluOpType
ACT = mybir.ActivationFunctionType
AX_X = mybir.AxisListType.X

P = 128
B, C, L = 4, 256, 1024
CT = C // P
NH = 2
HL = L // NH
NC = 4
DM = C // NC
DI = 128
NS = 16
TAPS = 4
NI = NC * NS
NB = L // P
E = 8
HID = 1024
HB = HID // P
LNS = 5
FP8_MAX = 448.0
FP8_MIN_NORMAL = 2.0 ** -6
LOG_SERIES = 1.0 / 64
SP_STEPS = 7
ROUND_AT = 1.5 * 2.0 ** 20


NG_ = B * NB
NT = 2 * B * L // P + E
RING = 4
R_DIF, R_CHOSEN, R_ALL = 12, 13, 40


def build_front(nc, t, x3_dram, xm_rows, logits):
    with ExitStack() as ctx:
        def sb(name, shape, dt=F32):
            return ctx.enter_context(nc.sbuf_tensor(f"{name}_sb", shape, dt))

        def sem(name):
            return ctx.enter_context(nc.semaphore(name))

        psum = ctx.enter_context(nc.psum_tensor("psum", [P, 8, 512], F32))

        ident = sb("ident", [P, P])
        mean_w = sb("mean_w", [P, P])
        group_w = sb("group_w", [P, P])
        sel = sb("sel", [P, 2 * NS, P], BF16)
        in_w = sb("in_w", [P, 2, 2 * DI])
        
        conv_in_w = sb("conv_in_w", [P, 2, TAPS, DI])
        xproj_dt = sb("xproj_dt", [4, DI])
        dtw = sb("dtw", [4, DI])
        dt_w = sb("dt_w", [P, DI])
        bc_w = sb("bc_w", [P, P])
        outp_w = sb("outp_w", [P, DM])
        proj_w = sb("proj_w", [P, CT, C])
        ffn_w = sb("ffn_w", [P, CT, C])
        ffn_q = sb("ffn_q", [P, CT, C], BF16)
        qk_w = sb("qk_w", [P, CT, 2 * C])
        v_w = sb("v_w", [P, CT, C])
        p_w = sb("p_w", [P, CT, C])
        gate_w = sb("gate_w", [P, CT, E])
        qk_b = sb("qk_b", [P, 2 * C])
        cols = sb("cols", [P, 24])
        NG, NBB, PB, FB, GG, GB, BV, BP_ = (cols[:, 2 * i:2 * i + 2] for i in range(8))
        dcols = sb("dcols", [P, 4])
        scal = sb("scal", [P, 8])
        alog = sb("alog", [P, NS])
        a_neg = sb("a_neg", [P, NS])
        fbias_b = sb("fbias_b", [P, CT], BF16)
        fbias = sb("fbias", [P, CT])
        eps6 = sb("eps6", [P, 1])
        eps65 = sb("eps65", [P, 1])
        eps5 = sb("eps5", [P, 1])
        small = sb("small", [P, 32])
        g_sum, g_mean, g_sq, g_std, g_rs, g_sc = (small[:, 2 * i:2 * i + 2] for i in range(6))
        s_max, s_neg, s_sum, s_rec = (small[:, 12 + 2 * i:14 + 2 * i] for i in range(4))

        X = sb("X", [P, CT, L])
        X1 = sb("X1", [P, CT, L])
        X2 = sb("X2", [P, CT, L])
        T = sb("T", [P, CT, L])
        SQ = sb("SQ", [P, CT, L])
        STD = sb("STD", [P, L])
        RSTD = sb("RSTD", [P, L])
        PAD = 4
        XN = sb("XN", [P, CT, PAD + L])
        XC = sb("XC", [P, NC, L])
        SZ = sb("SZ", [P, NC, L])
        DT = sb("DT", [P, NC, L])
        DTX = sb("DTX", [P, NC, L])
        BCS = sb("BCS", [P, NC, L], BF16)
        DA = sb("DA", [P, 2, L])
        DBX = sb("DBX", [P, 2, L])
        H = sb("H", [P, 2, L])
        HC = sb("HC", [P, 2, L])
        YF = sb("YF", [P, L])
        YM = T
        sel_f32 = XC[:, :, :].rearrange("p c l -> p (c l)").rearrange("p (s m) -> p s m", m=P)
        conv_rep = SQ[:, 1, 0:TAPS * DI].rearrange("p (k d) -> p k d", k=TAPS)

        xn = XN[:, :, PAD:]
        R1 = YF
        QB = DA[:, :, :].rearrange("p a l -> p (a l)").bitcast(BF16)[:, 0:CT * L].rearrange("p (c l) -> p c l", c=CT)
        QKT = XC[:, :, :].rearrange("p c l -> p (c l)").rearrange("p (n q) -> p n q", n=NB)
        TM = XC[:, 0:2, :].rearrange("p c l -> p (c l)").rearrange("p (n q) -> p n q", n=NB)
        V = SZ[:, 0:2, :]
        CTXT = SZ[:, 2:4, :]
        XG = DT[:, 0:2, :]
        H5 = DT[:, 2:4, :]
        ATT = DTX[:, 0, 0:2 * C].rearrange("p (a d) -> p a d", a=CT)
        ATTT = DTX[:, 1, 0:2 * C].rearrange("p (a d) -> p a d", a=CT)

        brep = psum[:, 0:2, :]
        crep = psum[:, 2:4, :]
        ysum = psum[:, 4:6, :]
        stat = psum[:, 6:8, :]

        def halves(ap):
            return ap.rearrange("p (h n) -> p h n", h=NH)

        w_loaded = sem("w_loaded")
        prep_dve = sem("prep_dve")
        prep_act = sem("prep_act")
        prep_pe = sem("prep_pe")
        x_loaded = sem("x_loaded")
        ln_mean = sem("ln_mean"); ln_cent = sem("ln_cent"); ln_sq = sem("ln_sq"); ln_var = sem("ln_var")
        ln_std = sem("ln_std"); ln_rstd = sem("ln_rstd"); ln_done = sem("ln_done")
        aff_done = sem("aff_done")
        inp_ready = sem("inp_ready"); silu_done = sem("silu_done")
        dtp_ready = sem("dtp_ready"); bcp_ready = sem("bcp_ready")
        sp_abs = sem("sp_abs"); sp_exp = sem("sp_exp"); sp_ln = sem("sp_ln"); sp_relu = sem("sp_relu"); sp_step = sem("sp_step")
        dt_done = sem("dt_done"); dtx_done = sem("dtx_done"); bc_split = sem("bc_split")
        brep_ready = sem("brep_ready"); dbx_ready = sem("dbx_ready"); da_ready = sem("da_ready")
        h_ready = sem("h_ready"); crep_ready = sem("crep_ready"); hc_ready = sem("hc_ready"); ysum_done = sem("ysum_done")
        y_read = sem("y_read"); yf_ready = sem("yf_ready"); op_ready = sem("op_ready"); ym_done = sem("ym_done")
        pj_ready = sem("pj_ready"); x1_done = sem("x1_done")
        q_step = sem("q_step"); ff_ready = sem("ff_ready"); ff_done = sem("ff_done"); x2_done = sem("x2_done")
        g_sum_ready = sem("g_sum_ready"); g_mean_ready = sem("g_mean_ready"); g_cent = sem("g_cent")
        g_sq_ready = sem("g_sq_ready"); g_var_ready = sem("g_var_ready"); g_std_ready = sem("g_std_ready")
        g_step = sem("g_step"); xg_ready = sem("xg_ready")
        qk_ready = sem("qk_ready"); qk_done = sem("qk_done"); v_ready = sem("v_ready"); v_done = sem("v_done")
        sc_ready = sem("sc_ready"); sm_step = sem("sm_step"); sm_exp = sem("sm_exp"); att_done = sem("att_done")
        at_ready = sem("at_ready"); at_done = sem("at_done"); cx_ready = sem("cx_ready"); cx_done = sem("cx_done")
        po_ready = sem("po_ready"); xh_done = sem("xh_done"); x3_done = sem("x3_done")
        stored = sem("stored")
        tm_ready = sem("tm_ready"); tm_done = sem("tm_done"); gate_ready = sem("gate_ready"); gate_done = sem("gate_done")

        block = ctx.enter_context(nc.Block())

        loads = [
            (ident[:, :], t["c_ident"]), (mean_w[:, :], t["c_mean"]), (group_w[:, :], t["c_group"]),
            (sel_f32, t["c_sel"]), (conv_rep[:, :, :], t["conv_rep"]),
            (xproj_dt[:, :], t["xproj"][0:4, :]), (dtw[:, :], t["dtwT"]),
            (in_w[0:DM, 0, :], t["in_wT"]), (in_w[DM:P, 1, :], t["in_wT"]),
            (bc_w[:, :], t["bc_wT"]), (outp_w[:, :], t["outpT"]),
            (proj_w[:, :, :], t["projT"]), (ffn_w[:, :, :], t["ffn_k"]),
            (qk_w[:, :, 0:C], t["wqT"]), (qk_w[:, :, C:2 * C], t["wkT"]), (v_w[:, :, :], t["wvT"]),
            (p_w[:, :, :], t["wpT"]), (gate_w[:, :, :], t["gateT"]), (qk_b[:, :], t["qk_b"]),
            (cols[:, 0:16], t["cols"]), (dcols[:, 0:3], t["dcols"]), (scal[:, 0:3], t["scal"]),
            (alog[:, :], t["alog"]),
        ]
        W_ALL = 16 * len(loads)

        @block.sync
        def _(sp):
            for dst, src in loads:
                sp.dma_start(dst, src).then_inc(w_loaded, 16)

            def store(b):
                sp.wait_ge(x3_done, (b + 1) * 4)
                sp.dma_start(x3_dram[b], X2[:, :, :]).then_inc(stored, 16)
                sp.wait_ge(tm_done, (b + 1) * 2)
                sp.dma_start(xm_rows.rearrange("(b n p) c -> b p n c", n=NB, p=P)[b], TM).then_inc(stored, 16)

            sp.dma_start(X[:, :, :], t["x"][0]).then_inc(x_loaded, 16)
            with sp.Fori(1, B) as b:
                sp.wait_ge(x1_done, b * 4)
                sp.dma_start(X[:, :, :], t["x"][b]).then_inc(x_loaded, 16)
                store(b - 1)
            store(B - 1)
            sp.wait_ge(stored, B * 32)

        @block.tensor
        def _(pe):
            def mm(o, lhsT, rhs, start, stop, **k):
                return nc.tensor.matmul(o, lhsT, rhs, start=start, stop=stop, **k)

            def layer_norm(k, b, src):
                n = (b * LNS + k) * 2
                if k:
                    pe.wait_ge(ln_std, n)
                for h in range(NH):
                    s = slice(h * HL, (h + 1) * HL)
                    for c in range(CT):
                        i = mm(psum[:, 6 + h, :], mean_w[:, :], src[:, c, s], c == 0, c == CT - 1)
                    i.then_inc(ln_mean, 1)
                for h in range(NH):
                    s = slice(h * HL, (h + 1) * HL)
                    pe.wait_ge(ln_sq, n + h + 1)
                    for c in range(CT):
                        i = mm(psum[:, 6 + h, :], mean_w[:, :], SQ[:, c, s], c == 0, c == CT - 1)
                    i.then_inc(ln_var, 1)

            def linear(w, src, bank, done):
                for o in range(CT):
                    for h in range(NH):
                        for c in range(CT):
                            i = mm(psum[:, bank(2 * o + h), :], w[:, c, o * P:(o + 1) * P],
                                   src[:, c, h * HL:(h + 1) * HL], c == 0, c == CT - 1)
                        i.then_inc(done, 1)

            pe.wait_ge(w_loaded, W_ALL)
            mm(psum[:, 0, 0:DI], xproj_dt[:, :], dtw[:, :], True, True).then_inc(prep_pe, 1)
            pe.wait_ge(prep_dve, PREP_DVE)
            with pe.Fori(0, B) as b:
                pe.wait_ge(x_loaded, b * 16 + 16)
                layer_norm(0, b, X)
                pe.wait_ge(aff_done, b * 4 + 2)
                for u in range(16):
                    c, kind, h = u // 4, (u // 2) % 2, u % 2
                    if u >= 6:
                        pe.wait_ge(silu_done, b * 16 + u - 5)
                    if kind == 0:
                        for k in range(TAPS):
                            o = PAD - TAPS + 1 + k + h * HL
                            i = mm(psum[:, u % 6, :], conv_in_w[:, c % 2, k, :], XN[:, c // 2, o:o + HL],
                                   k == 0, k == TAPS - 1)
                    else:
                        i = mm(psum[:, u % 6, :], in_w[:, c % 2, DI:2 * DI],
                               XN[:, c // 2, PAD + h * HL:PAD + (h + 1) * HL], True, True)
                    i.then_inc(inp_ready, 1)
                pe.wait_ge(silu_done, b * 16 + 16)
                for c in range(NC):
                    if c >= 2:
                        pe.wait_ge(sp_abs, b * NC + c - 1)
                        pe.wait_ge(sp_relu, b * NC + c - 1)
                    for h in range(NH):
                        i = mm(psum[:, 2 * (c % 2) + h, :], dt_w[:, :], XC[:, c, h * HL:(h + 1) * HL], True, True)
                    i.then_inc(dtp_ready, 1)
                    if c >= 1:
                        pe.wait_ge(bc_split, (b * NC + c - 1) * 4 + 2)
                    for h in range(NH):
                        i = mm(psum[:, 4 + h, :], bc_w[:, :], XC[:, c, h * HL:(h + 1) * HL], True, True)
                    i.then_inc(bcp_ready, 1)
                pe.wait_ge(bc_split, b * 4 * NC + 4 * NC)
                pe.wait_ge(sp_relu, b * NC + NC)
                pe.wait_ge(sp_abs, b * NC + NC)

                def b_rows(c, s, i, first=False):
                    if not first:
                        pe.wait_ge(dbx_ready, i)
                    for h in range(NH):
                        m = mm(psum[:, h, :], sel[:, s, :], BCS[:, c, h * HL:(h + 1) * HL], True, True)
                    m.then_inc(brep_ready, 1)

                def c_rows(c, s, i, first=False):
                    if not first:
                        pe.wait_ge(hc_ready, i)
                    for h in range(NH):
                        m = mm(psum[:, 2 + h, :], sel[:, NS + s, :], BCS[:, c, h * HL:(h + 1) * HL], True, True)
                    m.then_inc(crep_ready, 1)

                def sum_states(slot, i, first, last):
                    pe.wait_ge(hc_ready, i + 1)
                    for h in range(NH):
                        m = mm(psum[:, 4 + h, :], ident[:, :], HC[:, slot, h * HL:(h + 1) * HL], first, last,
                               skip_group_check=True)
                    m.then_inc(ysum_done, 1)

                def out_proj(c):
                    pe.wait_ge(yf_ready, b * NC + c + 1)
                    if c:
                        pe.wait_ge(ym_done, b * NC + c)
                    for h in range(NH):
                        p0 = DM * (c % 2)
                        m = mm(psum[p0:p0 + DM, 6 + h, :], outp_w[:, :], YF[:, h * HL:(h + 1) * HL], True, True)
                    m.then_inc(op_ready, 1)

                b0 = b * NI
                b_rows(0, 0, b0, first=True)
                b_rows(0, 1, b0 + 1)
                for c in range(NC):
                    i = b0 + c * NS
                    b_rows(c, 2, i + 2)
                    c_rows(c, 0, i, first=c == 0)
                    if c:
                        sum_states(1, i - 1, False, True)
                    b_rows(c, 3, i + 3)
                    c_rows(c, 1, i + 1)
                    if c:
                        pe.wait_ge(y_read, b * NC + c)
                    sum_states(0, i, True, False)
                    if c:
                        out_proj(c - 1)
                    with pe.Fori(2, NS - 3, 2) as s:
                        for d in range(2):
                            b_rows(c, s + (2 + d), i + s + (2 + d))
                            c_rows(c, s + d, i + s + d)
                            sum_states((1 + d) % 2, i + s + (d - 1), False, False)
                    for s in (14, 15):
                        if c + 1 < NC:
                            b_rows(c + 1, s - 14, i + s + 2)
                        c_rows(c, s, i + s)
                        sum_states((s - 1) % 2, i + s - 1, False, False)
                sum_states(1, b0 + NI - 1, False, True)
                out_proj(NC - 1)

                pe.wait_ge(ym_done, b * NC + NC)
                layer_norm(1, b, YM)
                pe.wait_ge(aff_done, b * 4 + 4)
                linear(proj_w, xn, lambda u: u, pj_ready)
                pe.wait_ge(x1_done, b * 4 + 4)
                layer_norm(2, b, X1)
                pe.wait_ge(q_step, b * 6 + 6)
                linear(ffn_q, QB, lambda u: u, ff_ready)
                pe.wait_ge(x2_done, b + 1)
                layer_norm(3, b, X2)
                pe.wait_ge(g_sum_ready, b + 1)
                mm(psum[:, 6, 0:2], group_w[:, :], g_sum, True, True).then_inc(g_mean_ready, 1)
                pe.wait_ge(g_sq_ready, b * 2 + 2)
                mm(psum[:, 7, 0:2], group_w[:, :], g_sq, True, True).then_inc(g_var_ready, 1)
                pe.wait_ge(xg_ready, b * 2 + 2)
                for n in range(NB):
                    if n >= 4:
                        pe.wait_ge(qk_done, b * NB + n - 3)
                    for c in range(CT):
                        i = mm(psum[:, n % 4, :], XG[:, c, n * P:(n + 1) * P], qk_w[:, c, :], c == 0, c == CT - 1)
                    i.then_inc(qk_ready, 1)
                for u in range(4):
                    o, h = u // 2, u % 2
                    if u >= 2:
                        pe.wait_ge(v_done, b * 4 + u - 1)
                    for c in range(CT):
                        i = mm(psum[:, 4 + u % 2, :], v_w[:, c, o * P:(o + 1) * P], XG[:, c, h * HL:(h + 1) * HL],
                               c == 0, c == CT - 1)
                    i.then_inc(v_ready, 1)
                pe.wait_ge(qk_done, b * NB + NB)
                for a in range(CT):
                    for n in range(NB):
                        i = mm(psum[:, a, 0:C], QKT[:, n, a * P:(a + 1) * P], QKT[:, n, C:2 * C], n == 0, n == NB - 1)
                    i.then_inc(sc_ready, 1)
                pe.wait_ge(att_done, b * 2 + 2)
                for a in range(CT):
                    for d in range(CT):
                        i = nc.tensor.transpose(psum[:, 2, (2 * d + a) * P:(2 * d + a + 1) * P],
                                                ATT[:, a, d * P:(d + 1) * P], ident[:, :])
                i.then_inc(at_ready, 1)
                pe.wait_ge(at_done, b + 1)
                pe.wait_ge(v_done, b * 4 + 4)
                for a in range(CT):
                    for h in range(NH):
                        u = 2 * a + h
                        for d in range(CT):
                            i = mm(psum[:, (3 + u) % 6, :], ATTT[:, d, a * P:(a + 1) * P], V[:, d, h * HL:(h + 1) * HL],
                                   d == 0, d == CT - 1)
                        i.then_inc(cx_ready, 1)
                pe.wait_ge(cx_done, b * 4 + 4)
                linear(p_w, CTXT, lambda u: u, po_ready)
                pe.wait_ge(x3_done, b * 4 + 4)
                layer_norm(4, b, X2)
                pe.wait_ge(ln_done, b * 2 * LNS + 2 * LNS)
                for n in range(NB):
                    for c in range(CT):
                        i = nc.tensor.transpose(psum[:, n // 2, (n % 2) * C + c * P:(n % 2) * C + (c + 1) * P],
                                                T[:, c, n * P:(n + 1) * P], ident[:, :])
                    if n % 4 == 3:
                        i.then_inc(tm_ready, 1)
                for n in range(NB):
                    for c in range(CT):
                        i = mm(psum[:, 4, n * E:(n + 1) * E], T[:, c, n * P:(n + 1) * P], gate_w[:, c, :],
                               c == 0, c == CT - 1)
                i.then_inc(gate_ready, 1)
                pe.wait_ge(tm_done, b * 2 + 2)
                pe.wait_ge(gate_done, b + 1)

        @block.scalar
        def _(act):
            def layer_norm(k, b, eps, var_scale=1.0):
                n = (b * LNS + k) * 2
                for h in range(NH):
                    s = slice(h * HL, (h + 1) * HL)
                    act.wait_ge(ln_cent, n + h + 1)
                    nc.scalar.activation(SQ[:, :, s], T[:, :, s], ACT.Square).then_inc(ln_sq, 1)
                for h in range(NH):
                    s = slice(h * HL, (h + 1) * HL)
                    act.wait_ge(ln_var, n + h + 1)
                    nc.scalar.activation(STD[:, s], psum[:, 6 + h, :], ACT.Sqrt, bias=eps[:, :],
                                         scale=var_scale).then_inc(ln_std, 1)

            def affine(k, b):
                act.wait_ge(ln_done, (b * LNS + k) * 2 + 2)
                for c in range(CT):
                    nc.scalar.activation(xn[:, c, :], T[:, c, :], ACT.Identity, scale=NG[:, c:c + 1],
                                         bias=NBB[:, c:c + 1]).then_inc(aff_done, 1)

            act.wait_ge(w_loaded, W_ALL)
            nc.scalar.activation(a_neg[:, :], alog[:, :], ACT.Exp).then_inc(prep_act, 1)
            act.wait_ge(prep_dve, PREP_DVE)
            with act.Fori(0, B) as b:
                layer_norm(0, b, eps65, 1.0 + 1e-5)
                affine(0, b)
                for u in range(16):
                    c, kind, h = u // 4, (u // 2) % 2, u % 2
                    act.wait_ge(inp_ready, b * 16 + u + 1)
                    if kind == 0:
                        i = nc.scalar.activation(XC[:, c, h * HL:(h + 1) * HL], psum[:, u % 6, :], ACT.Silu,
                                                 bias=dcols[:, 0:1])
                    else:
                        i = nc.scalar.activation(SZ[:, c, h * HL:(h + 1) * HL], psum[:, u % 6, :], ACT.Silu)
                    i.then_inc(silu_done, 1)
                for c in range(NC):
                    n = b * NC + c
                    tmp = T[:, c % 2, :]
                    act.wait_ge(dtp_ready, n + 1)
                    if c >= 2:
                        act.wait_ge(dt_done, n - 1)
                    nc.scalar.activation(halves(tmp), psum[:, 2 * (c % 2):2 * (c % 2) + 2, :], ACT.Abs,
                                         bias=dcols[:, 1:2]).then_inc(sp_abs, 1)
                    act.wait_ge(sp_abs, n + 1)
                    nc.scalar.activation(tmp, tmp, ACT.Exp, scale=-1.0).then_inc(sp_exp, 1)
                    act.wait_ge(sp_exp, n + 1)
                    if c:
                        act.wait_ge(sp_step, (n - 1) * SP_STEPS + 6)
                    nc.scalar.activation(STD[:, :], tmp, ACT.Ln, bias=1.0).then_inc(sp_ln, 1)
                for c in range(NC):
                    act.wait_ge(dt_done, b * NC + c + 1)
                    i = b * NI + c * NS

                    def decay(s, d, free):
                        if free is not None:
                            act.wait_ge(h_ready, free)
                        nc.scalar.activation(DA[:, d, :], DT[:, c, :], ACT.Exp,
                                             scale=a_neg[:, bass.ds(s, 1)]).then_inc(da_ready, 1)
                    decay(0, 0, i - 1 if c else None)
                    decay(1, 1, i if c else None)
                    with act.Fori(2, NS - 1, 2) as s:
                        decay(s, 0, i + s - 1)
                        decay(s + 1, 1, i + s)
                layer_norm(1, b, eps5)
                affine(1, b)
                layer_norm(2, b, eps5)
                for u in range(4):
                    o, h = u // 2, u % 2
                    act.wait_ge(ff_ready, b * 4 + u + 1)
                    nc.scalar.activation(SQ[:, o, h * HL:(h + 1) * HL], psum[:, u, :], ACT.Identity,
                                         scale=scal[:, 5:6], bias=fbias[:, o:o + 1]).then_inc(ff_done, 1)
                layer_norm(3, b, eps6)
                act.wait_ge(g_cent, b * 2 + 2)
                for c in range(CT):
                    nc.scalar.activation(SQ[:, c, :], XG[:, c, :], ACT.Square,
                                         accum_out=g_sq[:, c:c + 1]).then_inc(g_sq_ready, 1)
                act.wait_ge(g_var_ready, b + 1)
                nc.scalar.activation(g_std, psum[:, 7, 0:2], ACT.Sqrt, bias=eps5[:, :]).then_inc(g_std_ready, 1)
                for u in range(4):
                    o, h = u // 2, u % 2
                    act.wait_ge(v_ready, b * 4 + u + 1)
                    nc.scalar.activation(V[:, o, h * HL:(h + 1) * HL], psum[:, 4 + u % 2, :], ACT.Identity,
                                         bias=BV[:, o:o + 1]).then_inc(v_done, 1)
                act.wait_ge(sm_step, b * 3 + 2)
                for a in range(CT):
                    nc.scalar.activation(ATT[:, a, :], psum[:, a, 0:C], ACT.Exp, scale=float(C) ** -0.5,
                                         bias=s_neg[:, a:a + 1], accum_out=s_sum[:, a:a + 1]).then_inc(sm_exp, 1)
                act.wait_ge(at_ready, b + 1)
                nc.scalar.activation(ATTT[:, :, :], psum[:, 2, :].rearrange("p (a d) -> p a d", a=CT),
                                     ACT.Copy).then_inc(at_done, 1)
                for u in range(4):
                    act.wait_ge(cx_ready, b * 4 + u + 1)
                    nc.scalar.activation(CTXT[:, u // 2, (u % 2) * HL:(u % 2 + 1) * HL], psum[:, (3 + u) % 6, :],
                                         ACT.Copy).then_inc(cx_done, 1)
                layer_norm(4, b, eps5)
                for k in range(2):
                    act.wait_ge(tm_ready, b * 2 + k + 1)
                    nc.scalar.activation(TM[:, 4 * k:4 * k + 4, :].rearrange("p (a n) c -> p a (n c)", a=2),
                                         psum[:, 2 * k:2 * k + 2, :], ACT.Copy).then_inc(tm_done, 1)
                act.wait_ge(stored, b * 32 + 32)

        @block.vector
        def _(dve):
            v = nc.vector

            def layer_norm(k, b, src, dst):
                n = (b * LNS + k) * 2
                for h in range(NH):
                    s = slice(h * HL, (h + 1) * HL)
                    dve.wait_ge(ln_mean, n + h + 1)
                    v.tensor_tensor(T[:, :, s], src[:, :, s],
                                    psum[:, 6 + h, :].unsqueeze(1).broadcast_to((P, CT, HL)),
                                    ALU.subtract).then_inc(ln_cent, 1)
                for h in range(NH):
                    s = slice(h * HL, (h + 1) * HL)
                    dve.wait_ge(ln_std, n + h + 1)
                    v.reciprocal(RSTD[:, s], STD[:, s]).then_inc(ln_rstd, 1)
                    dve.wait_ge(ln_rstd, n + h + 1)
                    v.tensor_tensor(dst[:, :, s], T[:, :, s], RSTD[:, s].unsqueeze(1).broadcast_to((P, CT, HL)),
                                    ALU.mult).then_inc(ln_done, 1)

            steps = [0]

            def prep(i):
                steps[0] += 1
                i.then_inc(prep_dve, 1)
                dve.wait_ge(prep_dve, steps[0])

            def round_fp8(val, mag, dst, inv_scale, done):
                done(v.tensor_scalar(val, val, inv_scale, FP8_MAX, ALU.mult, ALU.min))
                done(v.tensor_scalar(val, val, -FP8_MAX, None, ALU.max))
                done(v.tensor_scalar(mag.bitcast(U32), val.bitcast(U32), 0x7F800000, None, ALU.bitwise_and))
                done(v.tensor_scalar(mag, mag, FP8_MIN_NORMAL, ROUND_AT, ALU.max, ALU.mult))
                done(v.tensor_tensor(val, val, mag, ALU.add))
                done(v.tensor_tensor(dst, val, mag, ALU.subtract))

            def log1p(n, e, relu, dst):
                lo, r, hi = RSTD[:, :], H[:, 0, :], H[:, 1, :]
                done = [0]

                def step(i):
                    done[0] += 1
                    i.then_inc(sp_step, 1)
                    dve.wait_ge(sp_step, n * SP_STEPS + done[0])
                step(v.scalar_tensor_tensor(lo, e, LOG_SERIES, e, ALU.is_lt, ALU.mult))
                step(v.tensor_scalar(r, lo, -1.0 / 4, None, ALU.mult))
                step(v.scalar_tensor_tensor(r, r, 1.0 / 3, lo, ALU.add, ALU.mult))
                step(v.scalar_tensor_tensor(r, r, -1.0 / 2, lo, ALU.add, ALU.mult))
                step(v.scalar_tensor_tensor(r, r, 1.0, lo, ALU.add, ALU.mult))
                dve.wait_ge(sp_ln, n + 1)
                step(v.scalar_tensor_tensor(hi, e, LOG_SERIES, STD[:, :], ALU.is_ge, ALU.mult))
                step(v.tensor_tensor(r, r, hi, ALU.add))
                v.tensor_tensor(dst, relu, r, ALU.add).then_inc(dt_done, 1)

            v.memset(eps6[:, :], 1e-6)
            v.memset(eps65[:, :], 1e-11)
            v.memset(eps5[:, :], 1e-5)
            prep(v.memset(XN[:, :, 0:PAD], 0.0))
            dve.wait_ge(w_loaded, W_ALL)
            prep(v.tensor_copy(sel[:, :, :], sel_f32))
            for par in range(2):
                lo = DM * (1 - par)
                prep(v.memset(in_w[lo:lo + DM, par, :], 0.0))
            for par in range(2):
                prep(v.tensor_tensor(conv_in_w[:, par, :, :], in_w[:, par, 0:DI].unsqueeze(1).broadcast_to((P, TAPS, DI)),
                                     conv_rep[:, :, :], ALU.mult))
            dve.wait_ge(prep_pe, 1)
            prep(v.tensor_copy(dt_w[:, :], psum[:, 0, 0:DI]))
            dve.wait_ge(prep_act, 1)
            prep(v.tensor_scalar(a_neg[:, :], a_neg[:, :], -1.0, None, ALU.mult))
            prep(v.reciprocal(scal[:, 3:5], scal[:, 1:3]))
            prep(v.tensor_tensor(scal[:, 5:6], scal[:, 1:2], scal[:, 2:3], ALU.mult))
            prep(v.tensor_copy(fbias_b[:, :], FB))
            prep(v.tensor_copy(fbias[:, :], fbias_b[:, :]))
            fw = SQ[:, 0, 0:CT * C].rearrange("p (c o) -> p c o", c=CT)
            round_fp8(ffn_w[:, :, :], fw, ffn_q[:, :, :], scal[:, 4:5], prep)
            assert steps[0] == PREP_DVE

            with dve.Fori(0, B) as b:
                dve.wait_ge(x_loaded, b * 16 + 16)
                layer_norm(0, b, X, T)
                for c in range(NC):
                    n = b * NC + c
                    relu = SQ[:, c % 2, :]
                    dve.wait_ge(sp_abs, n + 1)
                    v.tensor_scalar(halves(relu), psum[:, 2 * (c % 2):2 * (c % 2) + 2, :], dcols[:, 1:2], 0.0,
                                    ALU.add, ALU.max).then_inc(sp_relu, 1)
                    dve.wait_ge(bcp_ready, n + 1)
                    v.tensor_copy(halves(BCS[:, c, :]), psum[:, 4:6, :]).then_inc(bc_split, 1)
                    dve.wait_ge(bc_split, n * 4 + 1)
                    v.tensor_tensor(halves(R1[64:128, :]), psum[64:128, 4:6, :], halves(BCS[64:128, c, :]),
                                    ALU.subtract).then_inc(bc_split, 1)
                    dve.wait_ge(bc_split, n * 4 + 2)
                    v.tensor_copy(BCS[64:128, c, :], R1[64:128, :]).then_inc(bc_split, 1)
                    dve.wait_ge(bc_split, n * 4 + 3)
                    v.tensor_tensor(BCS[96:128, c, :], R1[96:128, :], BCS[96:128, c, :],
                                    ALU.subtract).then_inc(bc_split, 1)
                    dve.wait_ge(sp_exp, n + 1)
                    log1p(n, T[:, c % 2, :], relu, DT[:, c, :])
                    dve.wait_ge(dt_done, n + 1)
                    v.tensor_tensor(DTX[:, c, :], DT[:, c, :], XC[:, c, :], ALU.mult).then_inc(dtx_done, 1)
                dve.wait_ge(dtx_done, b * NC + NC)
                dve.wait_ge(bc_split, b * 4 * NC + 4 * NC)

                b0 = b * NI

                def drive(c, slot, i, again=True):
                    if again:
                        dve.wait_ge(h_ready, i - 1)
                    dve.wait_ge(brep_ready, i + 1)
                    v.tensor_tensor(halves(DBX[:, slot, :]), brep, halves(DTX[:, c, :]), ALU.mult).then_inc(dbx_ready, 1)

                def scan(slot, i, again=True):
                    if again:
                        dve.wait_ge(hc_ready, i - 1)
                    dve.wait_ge(da_ready, i + 1)
                    dve.wait_ge(dbx_ready, i + 1)
                    v.tensor_tensor_scan(H[:, slot, :], DA[:, slot, :], DBX[:, slot, :], 0.0, ALU.mult,
                                         ALU.add).then_inc(h_ready, 1)

                def read_out(slot, i):
                    dve.wait_ge(h_ready, i + 1)
                    dve.wait_ge(crep_ready, i + 1)
                    v.tensor_tensor(halves(HC[:, slot, :]), crep, halves(H[:, slot, :]), ALU.mult).then_inc(hc_ready, 1)

                def gate(c):
                    n = b * NC + c
                    dve.wait_ge(ysum_done, b0 + (c + 1) * NS)
                    if c:
                        dve.wait_ge(op_ready, n)
                    v.scalar_tensor_tensor(halves(YF[:, :]), halves(XC[:, c, :]), dcols[:, 2:3], ysum, ALU.mult,
                                           ALU.add).then_inc(y_read, 1)
                    dve.wait_ge(y_read, n + 1)
                    v.tensor_tensor(YF[:, :], YF[:, :], SZ[:, c, :], ALU.mult).then_inc(yf_ready, 1)

                def skip(c):
                    dve.wait_ge(op_ready, b * NC + c + 1)
                    p0 = DM * (c % 2)
                    v.scalar_tensor_tensor(halves(YM[p0:p0 + DM, c // 2, :]), halves(xn[p0:p0 + DM, c // 2, :]),
                                           scal[p0:p0 + DM, 0:1], psum[p0:p0 + DM, 6:8, :], ALU.mult,
                                           ALU.add).then_inc(ym_done, 1)

                drive(0, 0, b0, again=False)
                for c in range(NC):
                    i = b0 + c * NS
                    drive(c, 1, i + 1, again=c > 0)
                    scan(0, i, again=c > 0)
                    if c:
                        read_out(1, i - 1)
                    drive(c, 0, i + 2)
                    scan(1, i + 1, again=c > 0)
                    read_out(0, i)
                    if c:
                        gate(c - 1)
                    with dve.Fori(2, NS - 3, 2) as s:
                        for d in range(2):
                            drive(c, (1 + d) % 2, i + s + (1 + d))
                            scan(d, i + s + d)
                            read_out((1 + d) % 2, i + s + (d - 1))
                    drive(c, 1, i + 15)
                    scan(0, i + 14)
                    read_out(1, i + 13)
                    if c + 1 < NC:
                        drive(c + 1, 0, i + 16)
                    scan(1, i + 15)
                    read_out(0, i + 14)
                    if c:
                        skip(c - 1)
                read_out(1, b0 + NI - 1)
                gate(NC - 1)
                skip(NC - 1)

                dve.wait_ge(ym_done, b * NC + NC)
                layer_norm(1, b, YM, T)
                for u in range(4):
                    o, h = u // 2, u % 2
                    s = slice(h * HL, (h + 1) * HL)
                    dve.wait_ge(pj_ready, b * 4 + u + 1)
                    v.scalar_tensor_tensor(X1[:, o, s], psum[:, u, :], PB[:, o:o + 1], X[:, o, s], ALU.add,
                                           ALU.add).then_inc(x1_done, 1)
                dve.wait_ge(x1_done, b * 4 + 4)
                layer_norm(2, b, X1, T)
                dve.wait_ge(ln_done, b * 2 * LNS + 6)
                qs = [0]

                def q_done(i):
                    qs[0] += 1
                    i.then_inc(q_step, 1)
                    dve.wait_ge(q_step, b * 6 + qs[0])
                round_fp8(T[:, :, :], SQ[:, :, :], QB, scal[:, 3:4], q_done)
                dve.wait_ge(ff_done, b * 4 + 4)
                v.tensor_tensor(X2[:, :, :], X1[:, :, :], SQ[:, :, :], ALU.add).then_inc(x2_done, 1)
                dve.wait_ge(x2_done, b + 1)
                layer_norm(3, b, X2, H5)
                dve.wait_ge(ln_done, b * 2 * LNS + 8)
                v.tensor_reduce(g_sum, H5, AX_X, ALU.add).then_inc(g_sum_ready, 1)
                v.tensor_tensor(X2[:, :, :], X2[:, :, :], H5, ALU.add).then_inc(xh_done, 1)
                dve.wait_ge(g_mean_ready, b + 1)
                v.tensor_copy(g_mean, psum[:, 6, 0:2]).then_inc(g_step, 1)
                dve.wait_ge(g_step, b * 3 + 1)
                for c in range(CT):
                    v.tensor_scalar(XG[:, c, :], H5[:, c, :], g_mean[:, c:c + 1], None, ALU.subtract).then_inc(g_cent, 1)
                dve.wait_ge(g_std_ready, b + 1)
                v.reciprocal(g_rs, g_std).then_inc(g_step, 1)
                dve.wait_ge(g_step, b * 3 + 2)
                v.tensor_tensor(g_sc, g_rs, GG, ALU.mult).then_inc(g_step, 1)
                dve.wait_ge(g_step, b * 3 + 3)
                for c in range(CT):
                    v.tensor_scalar(XG[:, c, :], XG[:, c, :], g_sc[:, c:c + 1], GB[:, c:c + 1], ALU.mult,
                                    ALU.add).then_inc(xg_ready, 1)
                for n in range(NB):
                    dve.wait_ge(qk_ready, b * NB + n + 1)
                    v.tensor_tensor(QKT[:, n, :], psum[:, n % 4, :], qk_b[:, :], ALU.add).then_inc(qk_done, 1)
                dve.wait_ge(sc_ready, b * 2 + 2)
                v.tensor_reduce(s_max, psum[:, 0:2, 0:C], AX_X, ALU.max).then_inc(sm_step, 1)
                dve.wait_ge(sm_step, b * 3 + 1)
                v.tensor_scalar(s_neg, s_max, -(float(C) ** -0.5), None, ALU.mult).then_inc(sm_step, 1)
                dve.wait_ge(sm_exp, b * 2 + 2)
                v.reciprocal(s_rec, s_sum).then_inc(sm_step, 1)
                dve.wait_ge(sm_step, b * 3 + 3)
                for a in range(CT):
                    v.tensor_scalar(ATT[:, a, :], ATT[:, a, :], s_rec[:, a:a + 1], None, ALU.mult).then_inc(att_done, 1)
                dve.wait_ge(xh_done, b + 1)
                for u in range(4):
                    o, h = u // 2, u % 2
                    s = slice(h * HL, (h + 1) * HL)
                    dve.wait_ge(po_ready, b * 4 + u + 1)
                    v.scalar_tensor_tensor(X2[:, o, s], psum[:, u, :], BP_[:, o:o + 1], X2[:, o, s], ALU.add,
                                           ALU.add).then_inc(x3_done, 1)
                dve.wait_ge(x3_done, b * 4 + 4)
                layer_norm(4, b, X2, T)
                dve.wait_ge(gate_ready, b + 1)
                v.tensor_copy(logits[:, bass.ds(b * NB, NB), :],
                              psum[:, 4, 0:NB * E].rearrange("p (n e) -> p n e", n=NB)).then_inc(gate_done, 1)
                dve.wait_ge(stored, b * 32 + 32)


PREP_DVE = 1 + 1 + 2 + 2 + 1 + 1 + 1 + 1 + 1 + 1 + 6


def lay_out(inp):
    import numpy as np
    f = {k: np.asarray(v) for k, v in inp.items()}
    a = {}

    def by_tile(w):
        return np.ascontiguousarray(w.reshape(w.shape[0] // P, P, w.shape[1]).transpose(1, 0, 2))

    def cols(v):
        return v.reshape(-1, P).T

    c = "L0_conv_"
    a["x"] = np.ascontiguousarray(f["x"].reshape(B, CT, P, L).transpose(0, 2, 1, 3))
    a["conv_rep"] = np.ascontiguousarray(np.broadcast_to(f[c + "conv_w"].T, (P, TAPS, DI)))
    a["xproj"] = f[c + "x_proj_w"]
    a["dtwT"] = np.ascontiguousarray(f[c + "dt_proj_w"].T)
    a["in_wT"] = np.ascontiguousarray(f[c + "in_proj_w"].T)
    a["bc_wT"] = np.ascontiguousarray(np.tile(f[c + "x_proj_w"][4:36], (4, 1)).T)
    a["outpT"] = np.ascontiguousarray(f[c + "out_proj_w"].T)
    a["projT"] = by_tile(f[c + "proj_w"].T)
    a["ffn_k"] = by_tile(f["L0_ffn_kernel"])
    for k in "qkvp":
        a[f"w{k}T"] = by_tile(f[f"L1_conv_w{k}"].T)
    a["qk_b"] = np.ascontiguousarray(np.broadcast_to(np.concatenate([f["L1_conv_bq"], f["L1_conv_bk"]]), (P, 2 * C)))
    a["cols"] = np.ascontiguousarray(np.concatenate([cols(f[k]) for k in (
        c + "norm_g", c + "norm_b", c + "proj_b", "L0_ffn_bias", "L1_conv_gn_gamma", "L1_conv_gn_beta",
        "L1_conv_bv", "L1_conv_bp")], axis=1))
    a["dcols"] = np.ascontiguousarray(np.stack([f[c + k] for k in ("conv_b", "dt_proj_b", "D_param")], axis=1))
    a["scal"] = np.ascontiguousarray(np.broadcast_to(np.concatenate([
        f[c + "skip_scale"], f["L0_ffn_input_scale"], f["L0_ffn_kernel_scale"]]), (P, 3)))
    a["alog"] = f[c + "A_log"]
    a["c_ident"] = np.eye(P, dtype=np.float32)
    a["c_mean"] = np.full((P, P), 1.0 / C, np.float32)
    g = np.arange(P) // 8
    a["c_group"] = (g[:, None] == g[None, :]).astype(np.float32) / (8 * L)
    part = np.arange(P)
    used = (part < 32) | (part >= 64)
    a["c_sel"] = np.broadcast_to(((part[:, None] % 32 == np.arange(32)[None, :]) & used[:, None])[:, :, None],
                                 (P, 32, P)).astype(np.float32)
    m = "L1_ffn_"
    a["gateT"] = by_tile(f[m + "gate_w"].T)
    a["w1T"] = np.ascontiguousarray(f[m + "w1"].reshape(E, HID, CT, P).transpose(0, 3, 2, 1))
    a["w2T"] = np.ascontiguousarray(f[m + "w2"].reshape(E, C, HB, P).transpose(0, 3, 2, 1))
    a["b1"] = np.ascontiguousarray(f[m + "b1"].reshape(E, HB, P).transpose(2, 0, 1))
    a["b2"] = f[m + "b2"].reshape(1, E, C)
    r = np.arange(P, dtype=np.float32)
    a["c_iota_e"] = np.ascontiguousarray(np.broadcast_to(np.arange(E, dtype=np.float32), (P, NG_, E)))
    a["c_iota_p"] = np.ascontiguousarray(np.broadcast_to(r, (P, P)))
    a["c_iota_t"] = np.ascontiguousarray(np.broadcast_to(np.arange(NT, dtype=np.float32) * P, (P, NT)))
    a["c_token"] = np.ascontiguousarray(r[:, None] + P * np.arange(NG_, dtype=np.float32)[None, :])
    a["c_before"] = (r[:, None] < r[None, :]).astype(np.float32)
    a["c_restart"] = np.ascontiguousarray(np.broadcast_to(np.arange(NG_) > 0, (P, E, NG_))).astype(np.float32)
    return a


def build_moe(nc, t, x3_dram, xm_rows, y_rows, logits, out):
    with ExitStack() as ctx:
        def sb(name, shape, dt=F32):
            return ctx.enter_context(nc.sbuf_tensor(f"{name}_sb", shape, dt))

        def sem(name):
            return ctx.enter_context(nc.semaphore(name))

        psum = ctx.enter_context(nc.psum_tensor("psum_moe", [P, 8, 512], F32))
        ident = sb("m_ident", [P, P])
        b1 = sb("b1", [P, E, HB])
        b2 = sb("b2", [1, E, C])
        one = sb("one", [1, P])
        iota_e = sb("iota_e", [P, NG_, E])
        iota_p = sb("iota_p", [P, P])
        iota_t = sb("iota_t", [P, NT])
        token = sb("token", [P, NG_])
        before = sb("before", [P, P])
        ones = sb("ones", [P, P])
        restart = sb("restart", [P, E, NG_])
        W1 = sb("W1", [P, E, CT, HID])
        W2 = sb("W2", [P, E, HB, C])
        EQ, CAND, OH1, OH2, LG2, POS = (sb(n, [P, NG_, E]) for n in ("eq", "cand", "oh1", "oh2", "lg2", "pos"))
        TOT, INCL = (sb(n, [P, E, NG_]) for n in ("tot", "incl"))
        M1, M2, IDX, DIF, EX, P1, P2, SL, SLF = (sb(n, [P, NG_]) for n in ("m1", "m2", "idx", "dif", "ex", "p1", "p2", "sl", "slf"))
        SLOT = sb("slot", [P, 2, NG_], U32)
        LO_I, HI_I = (sb(n, [P, 2, NG_], U32) for n in ("lo_i", "hi_i"))
        LO, HI = (sb(n, [P, 2, NG_]) for n in ("lo", "hi"))
        PADI = sb("padi", [P, E], U32)
        PADF, PINC, START = (sb(n, [P, E]) for n in ("padf", "pinc", "start"))
        TEC = sb("tec", [P, NT, E])
        TEF = sb("tef", [P, NT])
        TE = sb("te", [P, NT], mybir.dt.int32)
        TAB = sb("tab", [P, NT], U32)
        OLO = sb("olo", [P, 2, 8, P])
        OHI = sb("ohi", [P, 2, 8, NT])
        IX = sb("ix", [P, RING], U32)
        XG = sb("XG", [P, RING, C])
        XGT = sb("XGT", [P, 2, CT, P])
        HG = OLO[:, 0, :, :].rearrange("p a b -> p (a b)")
        HGT = OLO[:, 1, :, :]
        YS = sb("YS", [P, 2, C])
        Y1 = sb("Y1", [P, 2, C])
        Y2 = sb("Y2", [P, 2, C])
        O = sb("O", [P, 2, C])
        IY = sb("iy", [P, 2, 2], U32)
        X3 = sb("X3", [P, 2, CT, L])

        c_loaded = sem("c_loaded"); w_loaded = sem("w_loaded"); x3_loaded = [sem(f"x3_loaded{k}") for k in range(2)]
        route = sem("route"); route_exp = sem("route_exp"); rank_ready = sem("rank_ready")
        onehot_ready = sem("onehot_ready"); onehot_used = sem("onehot_used"); onehot_hi = sem("onehot_hi"); tab_done = sem("tab_done")
        ix_ready = sem("ix_ready"); indices_there = sem("indices_there")
        xg_ready = [sem(f"xg_ready{k}") for k in range(RING)]
        t1_ready = sem("t1_ready"); xgt_done = sem("xgt_done"); m1_ready = sem("m1_ready"); hg_done = sem("hg_done")
        t2_ready = sem("t2_ready"); gelu_done = sem("gelu_done"); m2_ready = sem("m2_ready"); y_copied = sem("y_copied")
        y_stored = [sem(f"y_stored{k}") for k in range(2)]
        iy_ready = sem("iy_ready"); yg_ready = [sem(f"yg_ready{k}") for k in range(2)]
        o_half = sem("o_half"); o_ready = sem("o_ready"); ot_ready = sem("ot_ready"); o_done = sem("o_done")
        out_stored = sem("out_stored")
        block = ctx.enter_context(nc.Block())

        consts = [(ident[:, :], t["c_ident"]), (b1[:, :, :], t["b1"]), (b2[:, :, :], t["b2"]),
                  (iota_e[:, :, :], t["c_iota_e"]), (iota_p[:, :], t["c_iota_p"]), (iota_t[:, :], t["c_iota_t"]),
                  (token[:, :], t["c_token"]), (before[:, :], t["c_before"]), (restart[:, :, :], t["c_restart"])]
        C_ALL = 16 * len(consts)

        @block.sync
        def _(sp):
            for d, s in consts:
                sp.dma_start(d, s).then_inc(c_loaded, 16)
            for e in range(E):
                sp.dma_start(W1[:, e, :, :], t["w1T"][e]).then_inc(w_loaded, 16)
                sp.dma_start(W2[:, e, :, :], t["w2T"][e]).then_inc(w_loaded, 16)
            rows = y_rows.rearrange("(t p) c -> t p c", p=P)
            with sp.Fori(0, NT // 2) as i:
                for k in range(2):
                    sp.wait_ge(y_copied, i * 2 + k + 1)
                    sp.dma_start(rows[i * 2 + k], YS[:, k, :]).then_inc(y_stored[k], 16)
            for k in range(2):
                sp.dma_start(X3[:, k, :, :], x3_dram[k]).then_inc(x3_loaded[k], 16)
            for b in range(B):
                sp.wait_ge(o_done, b * NB + NB)
                sp.dma_start(out[b], X3[:, b % 2, :, :]).then_inc(out_stored, 16)
                if b + 2 < B:
                    sp.wait_ge(out_stored, b * 16 + 16)
                    sp.dma_start(X3[:, b % 2, :, :], x3_dram[b + 2]).then_inc(x3_loaded[b % 2], 16)
            sp.wait_ge(out_stored, B * 16)

        @block.gpsimd
        def _(pool):
            def gather(tile, k):
                nc.gpsimd.tensor_copy(IX[:, k:k + 1], TAB[:, bass.ds(tile, 1)]).then_inc(ix_ready, 1)
                pool.wait_ge(ix_ready, tile + 1)
                pool.sem_inc(indices_there, 1)
                pool.indirect_dma_start(XG[:, k, :], None, xm_rows,
                                        bass.IndirectOffsetOnAxis(ap=IX[:, k:k + 1], axis=0)).then_inc(xg_ready[k], 16)

            pool.wait_ge(tab_done, 1)
            for k in range(RING):
                gather(k, k)
            with pool.Fori(1, NT // RING) as i:
                for k in range(RING):
                    pool.wait_ge(t1_ready, i * RING + (k - RING + 1))
                    gather(i * RING + k, k)
            for k in range(2):
                pool.wait_ge(y_stored[k], 16 * (NT // 2))

            def gather_results(n, k):
                for j in range(2):
                    nc.gpsimd.tensor_copy(IY[:, k, j:j + 1], SLOT[:, j, bass.ds(n, 1)]).then_inc(iy_ready, 1)
                pool.wait_ge(iy_ready, n * 2 + 2)
                pool.sem_inc(indices_there, 1)
                for j, y in enumerate((Y1, Y2)):
                    pool.indirect_dma_start(y[:, k, :], None, y_rows,
                                            bass.IndirectOffsetOnAxis(ap=IY[:, k, j:j + 1], axis=0)).then_inc(yg_ready[k], 16)
            for k in range(2):
                gather_results(k, k)
            with pool.Fori(1, NG_ // 2) as i:
                for k in range(2):
                    pool.wait_ge(o_ready, i * 2 + k - 1)
                    gather_results(i * 2 + k, k)

        @block.tensor
        def _(pe):
            def mm(o, lhsT, rhs, start, stop, **k):
                return nc.tensor.matmul(o, lhsT, rhs, start=start, stop=stop, **k)

            pe.wait_ge(c_loaded, C_ALL)
            pe.wait_ge(route, R_CHOSEN)
            flat = LG2[:, :, :].rearrange("p n e -> p (n e)")
            mm(psum[:, 0, 0:NG_ * E], before[:, :], flat, True, True)
            mm(psum[:, 1, 0:NG_ * E], ones[:, :], flat, True, True).then_inc(rank_ready, 1)
            for g in range(8):
                pe.wait_ge(onehot_ready, 2 * g + 2)
                for k in range(8):
                    i = mm(psum[:, 2, 0:NT], OLO[:, g % 2, k, :], OHI[:, g % 2, k, :], g == 0 and k == 0,
                           g == 7 and k == 7)
                i.then_inc(onehot_used, 1)

            def turn_rows(tile, k, i):
                pe.wait_ge(xg_ready[k], i)
                if not isinstance(tile, int) or tile:
                    pe.wait_ge(xgt_done, tile)
                for c in range(CT):
                    m = nc.tensor.transpose(psum[:, 6, c * P:(c + 1) * P], XG[:, k, c * P:(c + 1) * P], ident[:, :])
                m.then_inc(t1_ready, 1)

            def up(tile, k2):
                e = pe.value_load(TE[0:1, bass.ds(tile, 1)], min_val=0, max_val=E - 1)
                pe.wait_ge(xgt_done, tile + 1)
                for h in range(NH):
                    for c in range(CT):
                        m = mm(psum[:, h, :], XGT[:, k2, c, :], W1[:, bass.ds(e, 1), c, h * HL:(h + 1) * HL],
                               c == 0, c == CT - 1)
                m.then_inc(m1_ready, 1)

            def turn_hidden(tile):
                pe.wait_ge(hg_done, tile + 1)
                for k in range(HB):
                    m = nc.tensor.transpose(psum[:, 2 + k // 4, (k % 4) * P:(k % 4 + 1) * P], HG[:, k * P:(k + 1) * P],
                                            ident[:, :])
                m.then_inc(t2_ready, 1)

            def down(tile):
                e = pe.value_load(TE[0:1, bass.ds(tile, 1)], min_val=0, max_val=E - 1)
                if not isinstance(tile, int) or tile:
                    pe.wait_ge(y_copied, tile)
                mm(psum[:, 4, 0:C], one[:, :], b2[:, bass.ds(e, 1), :], True, False)
                pe.wait_ge(gelu_done, tile + 1)
                for k in range(HB):
                    m = mm(psum[:, 4, 0:C], HGT[:, k, :], W2[:, bass.ds(e, 1), k, :], False, k == HB - 1)
                m.then_inc(m2_ready, 1)

            pe.wait_ge(route, R_ALL)
            pe.wait_ge(w_loaded, 2 * E * 16)
            turn_rows(0, 0, 16)
            turn_rows(1, 1, 16)
            up(0, 0)

            def step(tile, k, i):
                turn_hidden(tile - 1)
                turn_rows(tile + 1, (k + 2) % RING, (i + (k + 2) // RING) * 16 + 16)
                up(tile, (k + 1) % 2)
                down(tile - 1)
            for k in range(RING):
                step(k + 1, k, 0)
            with pe.Fori(1, NT // RING - 1) as i:
                for k in range(RING):
                    step(i * RING + (k + 1), k, i)
            for tile in range(NT - RING + 1, NT):
                turn_hidden(tile - 1)
                if tile + 1 < NT:
                    turn_rows(tile + 1, (tile + 1) % RING, 16 * ((tile + 1) // RING + 1))
                up(tile, tile % 2)
                down(tile - 1)
            turn_hidden(NT - 1)
            down(NT - 1)
            with pe.Fori(0, NG_ // 2) as i:
                for k in range(2):
                    pe.wait_ge(o_ready, i * 2 + k + 1)
                    for c in range(CT):
                        m = nc.tensor.transpose(psum[:, 5 + 2 * k, c * P:(c + 1) * P], O[:, k, c * P:(c + 1) * P],
                                                ident[:, :])
                    m.then_inc(ot_ready, 1)

        @block.scalar
        def _(act):
            act.wait_ge(c_loaded, C_ALL)
            act.wait_ge(route, R_DIF)
            nc.scalar.activation(EX[:, :], DIF[:, :], ACT.Exp).then_inc(route_exp, 1)
            act.wait_ge(route, R_ALL)

            def tile_out(tile, k, free):
                e = act.value_load(TE[0:1, bass.ds(tile, 1)], min_val=0, max_val=E - 1)
                act.wait_ge(t2_ready, tile + 1)
                for j in range(HB):
                    m = nc.scalar.activation(HGT[:, j, :], psum[:, 2 + j // 4, (j % 4) * P:(j % 4 + 1) * P], ACT.Gelu,
                                             bias=b1[:, bass.ds(e, 1), j])
                m.then_inc(gelu_done, 1)
                act.wait_ge(m2_ready, tile + 1)
                if free is not None:
                    act.wait_ge(y_stored[k], free)
                nc.scalar.activation(YS[:, k, :], psum[:, 4, 0:C], ACT.Copy).then_inc(y_copied, 1)
            tile_out(0, 0, None)
            tile_out(1, 1, None)
            with act.Fori(1, NT // 2) as i:
                for k in range(2):
                    tile_out(i * 2 + k, k, i * 16)

        @block.vector
        def _(dve):
            v = nc.vector
            done = [0]

            def step(i):
                done[0] += 1
                i.then_inc(route, 1)
                dve.wait_ge(route, done[0])

            def wide(x):
                return x.unsqueeze(2).broadcast_to((P, NG_, E))

            def best(lg, m, onehot):
                step(v.tensor_reduce(m, lg, AX_X, ALU.max))
                step(v.tensor_tensor(EQ[:, :, :], lg, wide(m), ALU.is_equal))
                step(v.scalar_tensor_tensor(CAND[:, :, :], EQ[:, :, :], -float(E), iota_e[:, :, :], ALU.mult, ALU.add))
                step(v.tensor_reduce(IDX[:, :], CAND[:, :, :], AX_X, ALU.min))
                step(v.tensor_tensor(onehot, CAND[:, :, :], wide(IDX[:, :]), ALU.is_equal))

            dve.wait_ge(c_loaded, C_ALL)
            v.memset(one[:, :], 1.0)
            v.memset(ones[:, :], 1.0)
            best(logits[:, :, :], M1[:, :], OH1[:, :, :])
            step(v.scalar_tensor_tensor(LG2[:, :, :], OH1[:, :, :], -3.0e38, logits[:, :, :], ALU.mult, ALU.add))
            best(LG2[:, :, :], M2[:, :], OH2[:, :, :])
            step(v.tensor_tensor(DIF[:, :], M2[:, :], M1[:, :], ALU.subtract))
            assert done[0] == R_DIF
            step(v.tensor_tensor(LG2[:, :, :], OH1[:, :, :], OH2[:, :, :], ALU.add))
            assert done[0] == R_CHOSEN
            dve.wait_ge(rank_ready, 1)
            step(v.tensor_copy(TOT[:, :, :].rearrange("p e n -> p n e"),
                               psum[:, 1, 0:NG_ * E].rearrange("p (n e) -> p n e", n=NG_)))
            step(v.tensor_copy(POS[:, :, :].rearrange("p n e -> p (n e)"), psum[:, 0, 0:NG_ * E]))

            def flat(x):
                return x[:, :, :].rearrange("p e n -> p (e n)")
            step(v.tensor_tensor_scan(flat(INCL), flat(restart), flat(TOT), 0.0, ALU.mult, ALU.add))
            step(v.tensor_scalar(PADI[:, :], INCL[:, :, NG_ - 1], float(P - 1), None, ALU.add))
            step(v.tensor_scalar(PADI[:, :], PADI[:, :], 0xFFFFFFFF ^ (P - 1), None, ALU.bitwise_and))
            step(v.tensor_copy(PADF[:, :], PADI[:, :]))
            step(v.tensor_tensor_scan(PINC[:, :], ones[:, 0:E], PADF[:, :], 0.0, ALU.mult, ALU.add))
            step(v.tensor_tensor(START[:, :], PINC[:, :], PADF[:, :], ALU.subtract))
            step(v.tensor_tensor(INCL[:, :, :], INCL[:, :, :], TOT[:, :, :], ALU.subtract))
            step(v.tensor_tensor(INCL[:, :, :], INCL[:, :, :], START[:, :].unsqueeze(2).broadcast_to((P, E, NG_)), ALU.add))
            step(v.tensor_tensor(POS[:, :, :], POS[:, :, :], INCL[:, :, :].rearrange("p e n -> p n e"), ALU.add))
            for j, oh in enumerate((OH1, OH2)):
                step(v.tensor_tensor(EQ[:, :, :], oh[:, :, :], POS[:, :, :], ALU.mult))
                step(v.tensor_reduce(SLF[:, :], EQ[:, :, :], AX_X, ALU.add))
                step(v.tensor_copy(SLOT[:, j, :], SLF[:, :]))
            step(v.tensor_scalar(LO_I[:, :, :], SLOT[:, :, :], P - 1, None, ALU.bitwise_and))
            step(v.tensor_scalar(HI_I[:, :, :], SLOT[:, :, :], 7, None, ALU.logical_shift_right))
            step(v.tensor_copy(LO[:, :, :], LO_I[:, :, :]))
            step(v.tensor_copy(HI[:, :, :], HI_I[:, :, :]))
            step(v.tensor_tensor(TEC[:, :, :], START[:, :].unsqueeze(1).broadcast_to((P, NT, E)),
                                 iota_t[:, :].unsqueeze(2).broadcast_to((P, NT, E)), ALU.is_le))
            step(v.tensor_reduce(TEF[:, :], TEC[:, :, :], AX_X, ALU.add))
            step(v.tensor_scalar(TE[:, :], TEF[:, :], -1.0, None, ALU.add))
            dve.wait_ge(route_exp, 1)
            step(v.tensor_scalar(P2[:, :], EX[:, :], 1.0, None, ALU.add))
            step(v.reciprocal(P1[:, :], P2[:, :]))
            step(v.tensor_tensor(P2[:, :], EX[:, :], P1[:, :], ALU.mult))
            assert done[0] == R_ALL
            lo, hi = (x[:, :, :].rearrange("p j n -> p (j n)") for x in (LO, HI))
            for g in range(8):
                s = slice(8 * g, 8 * g + 8)
                if g >= 2:
                    dve.wait_ge(onehot_used, g - 1)
                v.tensor_tensor(OLO[:, g % 2, :, :], iota_p[:, :].unsqueeze(1).broadcast_to((P, 8, P)),
                                lo[:, s].unsqueeze(2).broadcast_to((P, 8, P)), ALU.is_equal).then_inc(onehot_ready, 1)
                v.tensor_tensor(OHI[:, g % 2, :, :], iota_p[:, 0:NT].unsqueeze(1).broadcast_to((P, 8, NT)),
                                hi[:, s].unsqueeze(2).broadcast_to((P, 8, NT)), ALU.is_equal).then_inc(onehot_hi, 1)
                dve.wait_ge(onehot_hi, g + 1)
                tok = token[:, 8 * (g % 4):8 * (g % 4) + 8].unsqueeze(2).broadcast_to((P, 8, NT))
                v.tensor_tensor(OHI[:, g % 2, :, :], OHI[:, g % 2, :, :], tok, ALU.mult).then_inc(onehot_ready, 1)
            dve.wait_ge(onehot_used, 8)
            v.tensor_copy(TAB[:, :], psum[:, 2, 0:NT]).then_inc(tab_done, 1)

            def rows_turned(tile, k2):
                dve.wait_ge(t1_ready, tile + 1)
                v.tensor_copy(XGT[:, k2, :, :].rearrange("p c m -> p (c m)"), psum[:, 6, 0:C]).then_inc(xgt_done, 1)

            def hidden(tile):
                dve.wait_ge(m1_ready, tile + 1)
                v.tensor_copy(HG.rearrange("p (h n) -> p h n", h=NH), psum[:, 0:2, :]).then_inc(hg_done, 1)
            rows_turned(0, 0)
            rows_turned(1, 1)
            hidden(0)
            with dve.Fori(0, NT // RING - 1) as i:
                for k in range(RING):
                    rows_turned(i * RING + (k + 2), k % 2)
                    hidden(i * RING + (k + 1))
            for tile in range(NT - RING + 1, NT):
                if tile + 1 < NT:
                    rows_turned(tile + 1, (tile + 1) % 2)
                hidden(tile)
            with dve.Fori(0, B // 2) as bb:
                for b2_ in range(2):
                    for n in range(NB):
                        k = n % 2
                        g = bb * (2 * NB) + (b2_ * NB + n)
                        dve.wait_ge(yg_ready[k], bb * (2 * NB * 16) + (b2_ * NB + n - k + 2) * 16)
                        v.tensor_scalar(O[:, k, :], Y1[:, k, :], P1[:, bass.ds(g, 1)], None, ALU.mult).then_inc(o_half, 1)
                        dve.wait_ge(o_half, g + 1)
                        v.scalar_tensor_tensor(O[:, k, :], Y2[:, k, :], P2[:, bass.ds(g, 1)], O[:, k, :], ALU.mult,
                                               ALU.add).then_inc(o_ready, 1)
                        if n == 0:
                            dve.wait_ge(x3_loaded[b2_], bb * 16 + 16)
                        dve.wait_ge(ot_ready, g + 1)
                        x = X3[:, b2_, :, n * P:(n + 1) * P]
                        v.tensor_tensor(x, psum[:, 5 + 2 * k, 0:C].rearrange("p (c m) -> p c m", c=CT), x,
                                        ALU.add).then_inc(o_done, 1)


def kernel(**inputs):
    import numpy as np
    import concourse.bacc as bacc
    from concourse.bass_utils import run_bass_kernel_spmd

    arrays = lay_out(inputs)
    nc = bacc.Bacc("TRN2", target_bir_lowering=False, num_devices=1)
    t = {k: nc.dram_tensor(k, a.shape, mybir.dt.from_np(a.dtype), kind="ExternalInput").ap() for k, a in arrays.items()}
    out = nc.dram_tensor("out", (B, P, CT, L), F32, kind="ExternalOutput").ap()
    x3_dram = nc.dram_tensor("x3_dram", (B, P, CT, L), F32).ap()
    xm_rows = nc.dram_tensor("xm_rows", (B * L, C), F32).ap()
    y_rows = nc.dram_tensor("y_rows", (NT * P, C), F32).ap()
    with nc.sbuf_tensor("logits_sb", [P, NG_, E], F32) as logits:
        build_front(nc, t, x3_dram, xm_rows, logits)
        build_moe(nc, t, x3_dram, xm_rows, y_rows, logits, out)
    r = run_bass_kernel_spmd(nc, [arrays], core_ids=[0])
    got = r.results[0]["out"]
    return np.ascontiguousarray(got.transpose(0, 2, 1, 3)).reshape(B, C, 32, 32)
```

```python
from collections import namedtuple
from contextlib import ExitStack

import concourse.bass as bass
from concourse import mybir

F32 = mybir.dt.float32
BF16 = mybir.dt.bfloat16
U32 = mybir.dt.uint32
ALU = mybir.AluOpType
ACT = mybir.ActivationFunctionType
AX_X = mybir.AxisListType.X

P = 128
B, C, L = 4, 256, 1024
CT = C // P
NH = 2
HL = L // NH
NC = 4
DM = C // NC
DI = 128
NS = 16
TAPS = 4
NI = NC * NS
NPAIR = NS // 2
NIP = NC * NPAIR
NB = L // P
E = 8
HID = 1024
HB = HID // P
LNS = 4
FP8_MAX = 448.0
FP8_MIN_NORMAL = 2.0 ** -6
LOG_SERIES = 1.0 / 64
SP_STEPS = 7
INV_POW = 1.0 / C ** 2
ROUND_AT = 1.5 * 2.0 ** 20


NG_ = B * NB
NT = 2 * B * L // P + E - 1
RING = 4
TAIL = RING * (NT // RING - 1) + 1
TOK = B * L
Y_ROWS = 3 * TOK + NT * P
R_DIF, R_CHOSEN, R_ALL = 14, 15, 42


EXPERT_FLOATS = 2 * E * CT * HID
LAST_W2 = EXPERT_FLOATS - HB * C
ROUTING_CONSTANTS = (("iota_e", [P, NG_, E]), ("iota_p", [P, P]), ("iota_t", [P, NT]), ("token", [P, 2, NG_, 2]),
                     ("empty", [P, NT]), ("before", [P, P]))


def expert_weights(experts):
    return (experts[:, 0:E * CT * HID].rearrange("p (e c h) -> p e c h", e=E, c=CT),
            experts[:, E * CT * HID:EXPERT_FLOATS].rearrange("p (e k c) -> p e k c", e=E, k=HB))


def build_front(nc, t, x3_dram, xm_rows, logits, routing, experts):
    with ExitStack() as ctx:
        def sb(name, shape, dt=F32):
            return ctx.enter_context(nc.sbuf_tensor(f"{name}_sb", shape, dt))

        def sem(name):
            return ctx.enter_context(nc.semaphore(name))

        place = [0]

        def shared(*shape, dt=F32):
            n, size = 1, 1 if dt == F32 else 2
            for d in shape:
                n *= d
            a = experts[:, place[0]:place[0] + n // size]
            place[0] += n // size
            if dt != F32:
                a = a.bitcast(dt)
            names = "abcd"[:len(shape)]
            if len(shape) == 1:
                return a
            return a.rearrange(f"p ({' '.join(names)}) -> p {' '.join(names)}", **dict(zip(names[1:], shape[1:])))

        psum = ctx.enter_context(nc.psum_tensor("psum", [P, 8, 512], F32))

        ident = sb("ident", [P, P])
        mean_w = sb("mean_w", [P, P])
        group_w = sb("group_w", [P, P])
        sel = shared(2 * NS, P, dt=BF16)
        in_w = shared(2, 2 * DI)
        
        conv_in_w = shared(2, TAPS, DI)
        xproj_dt = shared(DI)[0:4, :]
        dtw = shared(DI)[0:4, :]
        dt_w = shared(DI)
        bc_w = shared(P)
        outp_w = shared(DM)
        proj_w = sb("proj_w", [P, CT, C])
        ffn_w = shared(CT, C)
        ffn_q = sb("ffn_q", [P, CT, C], BF16)
        q_w = sb("q_w", [P, CT, C])
        k_w = sb("k_w", [P, CT, C])
        v_w = sb("v_w", [P, CT, C])
        p_w = sb("p_w", [P, CT, C])
        gate_w = sb("gate_w", [P, CT, E])
        qk_b = sb("qk_b", [1, 2 * C])
        bias_sel = sb("bias_sel", [1, 2, 2])
        XSUM = sb("XSUM", [P, CT, 2, 2])
        cols = sb("cols", [P, 24])
        NG, NBB, PB, FB, GG, GB, BV, BP_ = (cols[:, 2 * i:2 * i + 2] for i in range(8))
        dcols = sb("dcols", [P, 4])
        scal = sb("scal", [P, 8])
        alog = sb("alog", [P, NS])
        a_neg = sb("a_neg", [P, NS])
        fbias_b = sb("fbias_b", [P, CT], BF16)
        fbias = sb("fbias", [P, CT])
        eps6 = sb("eps6", [P, 1])
        eps65 = sb("eps65", [P, 1])
        eps5 = sb("eps5", [P, 1])
        eps6_n = sb("eps6_n", [P, 1])
        eps65_n = sb("eps65_n", [P, 1])
        eps5_n = sb("eps5_n", [P, 1])
        token_std = sb("token_std", [P, 4, NB])
        small = sb("small", [P, 32])
        g_sum, g_mean, g_sq, g_std, g_rs, g_sc = (small[:, 2 * i:2 * i + 2] for i in range(6))
        f_bias = small[:, 20:22]
        s_max, s_neg, s_sum, s_rec = (small[:, 12 + 2 * i:14 + 2 * i] for i in range(4))

        X1_XT = sb("X1_XT", [P, NB * (C + 1)])
        X1 = X1_XT[:, 0:CT * L].rearrange("p (c l) -> p c l", c=CT)
        X2 = sb("X2", [P, CT, L])
        T = sb("T", [P, CT, L])
        SQ = sb("SQ", [P, CT, L])
        STD = sb("STD", [P, L])
        RSTD = shared(L)
        PAD = 4
        XN = shared(CT, PAD + L)
        XC = shared(NC, L)
        SZ = shared(NC, L)
        DT = shared(NC, L)
        DTX = shared(NC, L)
        BCS = shared(NC, L, dt=BF16)
        DA = sb("DA", [P, 2, L])
        DBX = sb("DBX", [P, 2, L])
        H = shared(2, L)
        HC = sb("HC", [P, 2, L])
        YF = shared(L)
        assert place[0] <= LAST_W2
        place[0] = LAST_W2
        X = shared(CT, L)
        YM = T
        sel_f32 = XC[:, :, :].rearrange("p c l -> p (c l)").rearrange("p (s m) -> p s m", m=P)
        conv_rep = SQ[:, 1, 0:TAPS * DI].rearrange("p (k d) -> p k d", k=TAPS)

        xn = XN[:, :, PAD:]
        R1 = YF

        def log_tile(c):
            return SZ[:, c, :] if c + 1 < NC else H[:, 1, :]

        B_ODD = RSTD
        X_NEXT = H[:, :, :]

        def flat(ap):
            return ap.rearrange("p a l -> p (a l)")

        QB = flat(DA[:, :, :]).bitcast(BF16)[:, 0:CT * L].rearrange("p (c l) -> p c l", c=CT)
        FT = flat(DA[:, :, :])[:, 2 * HL:3 * HL].rearrange("p (a d) -> p a d", a=CT)
        QKROWS = flat(DA[:, :, :])[:, 3 * HL:4 * HL]
        ATT, GRAM, UT, PA = (flat(DBX[:, :, :])[:, i * HL:(i + 1) * HL].rearrange("p (a d) -> p a d", a=CT)
                             for i in range(4))
        H5 = XG = HC
        XT = X1_XT[:, :].rearrange("p (n q) -> p n q", n=NB)
        TM = X1_XT[:, 0:CT * L].rearrange("p (n q) -> p n q", n=NB)

        brep = psum[:, 0:2, :]
        crep = psum[:, 2:4, :]
        ysum = psum[:, 4:6, :]
        stat = psum[:, 6:8, :]

        def halves(ap):
            return ap.rearrange("p (h n) -> p h n", h=NH)

        w_loaded = sem("w_loaded"); c_loaded = sem("c_loaded"); experts_loaded = sem("experts_loaded")
        prep_dve = sem("prep_dve")
        prep_act = sem("prep_act")
        prep_pe = sem("prep_pe")
        x_loaded = sem("x_loaded"); next_loaded = sem("next_loaded")
        Norm = namedtuple("Norm", "mean centred squared var std rstd diag rep done bank T SQ DIAG std_t rstd_t")

        def norm(name, *tiles):
            return Norm(*(sem(f"{name}_{k}") for k in Norm._fields[:9]), *tiles)
        first = norm("first", 6, SZ[:, 0:2, :], DT[:, 0:2, :], DTX[:, 3, :], token_std[:, 0, :], token_std[:, 1, :])
        later = norm("later", 2, T[:, :, :], SQ[:, :, :], STD[:, :], token_std[:, 2, :], token_std[:, 3, :])
        x_aff = sem("x_aff"); y_aff = sem("y_aff")
        xi_ready = sem("xi_ready"); xc_done = sem("xc_done"); z_ready = sem("z_ready"); sz_done = sem("sz_done")
        dtp_ready = sem("dtp_ready"); bcp_ready = sem("bcp_ready")
        sp_abs = sem("sp_abs"); sp_exp = sem("sp_exp"); sp_ln = sem("sp_ln"); sp_relu = sem("sp_relu"); sp_step = sem("sp_step")
        dt_done = sem("dt_done"); dtx_done = sem("dtx_done"); bc_copy = sem("bc_copy"); bc_split = sem("bc_split")
        brep_ready = sem("brep_ready"); b_copied = sem("b_copied"); dbx_even = sem("dbx_even"); dbx_odd = sem("dbx_odd"); da_ready = sem("da_ready")
        h_ready = sem("h_ready"); crep_ready = sem("crep_ready"); hc_ready = sem("hc_ready"); ysum_done = sem("ysum_done")
        y_read = sem("y_read"); yf_ready = sem("yf_ready"); op_ready = sem("op_ready"); ym_done = sem("ym_done")
        pj_ready = sem("pj_ready"); x1_done = sem("x1_done")
        q_step = sem("q_step"); ff_ready = sem("ff_ready"); ff_done = sem("ff_done"); x2_done = sem("x2_done")
        g_sum_ready = sem("g_sum_ready"); g_mean_ready = sem("g_mean_ready"); g_cent = sem("g_cent")
        g_sq_ready = sem("g_sq_ready"); g_var_ready = sem("g_var_ready"); g_std_ready = sem("g_std_ready")
        g_step = sem("g_step"); xg_ready = sem("xg_ready")
        ones_set = sem("ones_set"); xt_ready = sem("xt_ready"); xt_done = sem("xt_done")
        gram_ready = sem("gram_ready"); gram_done = sem("gram_done"); u_ready = sem("u_ready"); u_done = sem("u_done")
        qk_rows_ready = sem("qk_rows_ready"); qk_rows_done = sem("qk_rows_done")
        sc_ready = sem("sc_ready"); sm_step = sem("sm_step"); sm_exp = sem("sm_exp"); sm_rec = sem("sm_rec")
        att_done = sem("att_done"); pa_ready = sem("pa_ready"); pa_done = sem("pa_done")
        f_ready = sem("f_ready"); f_done = sem("f_done"); f_bias_ready = sem("f_bias_ready"); f_bias_done = sem("f_bias_done")
        po_ready = sem("po_ready"); xh_done = sem("xh_done"); x3_done = sem("x3_done")
        stored = sem("stored")
        tm_ready = sem("tm_ready"); tm_done = sem("tm_done"); gate_ready = sem("gate_ready"); gate_done = sem("gate_done")

        block = ctx.enter_context(nc.Block())

        loads = [
            (ident[:, :], t["c_ident"]), (mean_w[:, :], t["c_mean"]), (group_w[:, :], t["c_group"]),
            (sel_f32, t["c_sel"]), (conv_rep[:, :, :], t["conv_rep"]),
            (xproj_dt[:, :], t["xproj"][0:4, :]), (dtw[:, :], t["dtwT"]),
            (in_w[0:DM, 0, :], t["in_wT"]), (in_w[DM:P, 1, :], t["in_wT"]),
            (bc_w[:, :], t["bc_wT"]), (outp_w[:, :], t["outpT"]),
            (proj_w[:, :, :], t["projT"]), (ffn_w[:, :, :], t["ffn_k"]),
            (q_w[:, :, :], t["wqT"]), (k_w[:, :, :], t["wkT"]), (v_w[:, :, :], t["wv"]), (bias_sel[:, :, :], t["c_bias_sel"]),
            (p_w[:, :, :], t["wpT"]), (gate_w[:, :, :], t["gateT"]), (qk_b[:, :], t["qk_b"]),
            (cols[:, 0:16], t["cols"]), (dcols[:, 0:3], t["dcols"]), (scal[:, 0:3], t["scal"]),
            (alog[:, :], t["alog"]),
        ]
        W_ALL = 16 * len(loads)

        @block.sync
        def _(sp):
            for dst, src in loads:
                sp.dma_start(dst, src).then_inc(w_loaded, 16)

            def store(b):
                sp.wait_ge(x3_done, (b + 1) * 4)
                sp.dma_start(x3_dram[b], X2[:, :, :]).then_inc(stored, 16)
                sp.wait_ge(tm_done, (b + 1) * NB)
                sp.dma_start(xm_rows.rearrange("(b n p) c -> b p n c", n=NB, p=P)[b], TM).then_inc(stored, 16)

            def load_next(b):
                sp.dma_start(X_NEXT, t["x"][b]).then_inc(next_loaded, 16)

            load_next(0)
            for name, _ in ROUTING_CONSTANTS:
                sp.dma_start(routing[name][:], t["c_" + name]).then_inc(c_loaded, 16)
            sp.dma_start(X[:, :, :], t["x"][0]).then_inc(x_loaded, 16)
            with sp.Fori(1, B) as b:
                sp.wait_ge(hc_ready, b * NI)
                load_next(b)
                sp.wait_ge(x1_done, b * 4)
                sp.dma_start(X[:, :, :], t["x"][b]).then_inc(x_loaded, 16)
                store(b - 1)
            W1, W2 = expert_weights(experts)
            sp.wait_ge(ym_done, B * NC)
            for e in range(E):
                sp.dma_start(W1[:, e, :, :], t["w1T"][e]).then_inc(experts_loaded, 16)
                if e + 1 < E:
                    sp.dma_start(W2[:, e, :, :], t["w2T"][e]).then_inc(experts_loaded, 16)
            sp.wait_ge(x1_done, B * 4)
            sp.dma_start(W2[:, E - 1, :, :], t["w2T"][E - 1]).then_inc(experts_loaded, 16)
            store(B - 1)
            sp.wait_ge(experts_loaded, 2 * E * 16)
            sp.wait_ge(stored, B * 32)
            sp.wait_ge(c_loaded, 16 * len(ROUTING_CONSTANTS))

        @block.tensor
        def _(pe):
            def mm(o, lhsT, rhs, start, stop, **k):
                return nc.tensor.matmul(o, lhsT, rhs, start=start, stop=stop, **k)

            def norm_mean(N, src):
                for h in range(NH):
                    for c in range(CT):
                        i = mm(psum[:, N.bank + h, :], mean_w[:, :], src[:, c, h * HL:(h + 1) * HL], c == 0, c == CT - 1)
                    i.then_inc(N.mean, 1)

            def norm_var(N, n):
                for h in range(NH):
                    pe.wait_ge(N.squared, n * NH + h + 1)
                    for j in range(NB // NH):
                        m = h * (NB // NH) + j
                        for c in range(CT):
                            i = mm(psum[:, N.bank + h, m:m + 1], N.SQ[:, c, m * P:(m + 1) * P], mean_w[:, 0:1],
                                   c == 0, c == CT - 1)
                    i.then_inc(N.var, 1)

            def norm_rep(N, n):
                for h in range(NH):
                    pe.wait_ge(N.diag, n * NH + h + 1)
                    mm(psum[:, N.bank + h, :], mean_w[:, :], N.DIAG[:, h * HL:(h + 1) * HL], True, True).then_inc(N.rep, 1)

            def linear(w, src, bank, done):
                for o in range(CT):
                    for h in range(NH):
                        for c in range(CT):
                            i = mm(psum[:, bank(2 * o + h), :], w[:, c, o * P:(o + 1) * P],
                                   src[:, c, h * HL:(h + 1) * HL], c == 0, c == CT - 1)
                        i.then_inc(done, 1)

            def conv_proj(b, c, h):
                if h == 0 and c:
                    pe.wait_ge(sp_relu, b * NC + c)
                for k in range(TAPS):
                    o = PAD - TAPS + 1 + k + h * HL
                    i = mm(psum[:, 4 + h, :], conv_in_w[:, c % 2, k, :], XN[:, c // 2, o:o + HL], k == 0, k == TAPS - 1)
                i.then_inc(xi_ready, 1)

            def dt_bc(b, c):
                pe.wait_ge(xc_done, (b * NC + c) * NH + NH)
                for h in range(NH):
                    i = mm(psum[:, 4 + h, :], dt_w[:, :], XC[:, c, h * HL:(h + 1) * HL], True, True)
                i.then_inc(dtp_ready, 1)
                if c:
                    pe.wait_ge(bc_split, (b * NC + c - 1) * 3 + 1)
                for h in range(NH):
                    i = mm(psum[:, 6 + h, :], bc_w[:, :], XC[:, c, h * HL:(h + 1) * HL], True, True)
                i.then_inc(bcp_ready, 1)

            def z_proj(b, sequences):
                for c in sequences:
                    if c == 0:
                        pe.wait_ge(sp_relu, (b + 1) * NC)
                    elif c == 1:
                        pe.wait_ge(bc_split, ((b + 1) * NC - 1) * 3 + 1)
                    else:
                        pe.wait_ge(sz_done, (b * NC + c - 2) * NH + NH)
                    for h in range(NH):
                        mm(psum[:, 4 + 2 * (c % 2) + h, :], in_w[:, c % 2, DI:2 * DI],
                           XN[:, c // 2, PAD + h * HL:PAD + (h + 1) * HL], True, True).then_inc(z_ready, 1)

            def start(b):
                pe.wait_ge(next_loaded, 16)
                norm_mean(first, X_NEXT)
                norm_var(first, b)
                norm_rep(first, b)
                pe.wait_ge(x_aff, 2)
                for c in range(NC):
                    for h in range(NH):
                        conv_proj(b, c, h)
                    dt_bc(b, c)
                z_proj(b, range(NC))

            def between(p, b):
                go_on = b is not None
                pe.wait_ge(ym_done, (p + 1) * NC)
                norm_mean(later, YM)
                norm_var(later, p * LNS)
                norm_rep(later, p * (LNS - 1))
                if go_on:
                    pe.wait_ge(next_loaded, b * 16 + 16)
                    norm_mean(first, X_NEXT)
                pe.wait_ge(y_aff, p * 2 + 2)
                linear(proj_w, T, lambda u: u, pj_ready)
                if go_on:
                    norm_var(first, b)
                pe.wait_ge(x1_done, p * 4 + 4)
                norm_mean(later, X1)
                if go_on:
                    norm_rep(first, b)
                norm_var(later, p * LNS + 1)
                norm_rep(later, p * (LNS - 1) + 1)
                if go_on:
                    pe.wait_ge(x_aff, b * 2 + 2)
                    conv_proj(b, 0, 0)
                    conv_proj(b, 0, 1)
                    dt_bc(b, 0)
                pe.wait_ge(q_step, p * 6 + 6)
                linear(ffn_q, QB, lambda u: u, ff_ready)
                if go_on:
                    conv_proj(b, 1, 0)
                    conv_proj(b, 1, 1)
                    dt_bc(b, 1)
                    conv_proj(b, 2, 0)
                    conv_proj(b, 2, 1)
                pe.wait_ge(x2_done, p + 1)
                norm_mean(later, X2)
                if go_on:
                    dt_bc(b, 2)
                norm_var(later, p * LNS + 2)
                norm_rep(later, p * (LNS - 1) + 2)
                if go_on:
                    conv_proj(b, 3, 0)
                pe.wait_ge(g_sum_ready, p + 1)
                mm(psum[:, 2, 0:2], group_w[:, :], g_sum, True, True).then_inc(g_mean_ready, 1)
                if go_on:
                    conv_proj(b, 3, 1)
                pe.wait_ge(g_sq_ready, p * 2 + 2)
                mm(psum[:, 3, 0:2], group_w[:, :], g_sq, True, True).then_inc(g_var_ready, 1)
                pe.wait_ge(xg_ready, p * 2 + 2)
                for n in range(NB):
                    for c in range(CT):
                        i = nc.tensor.transpose(psum[:, n // 2, (n % 2) * C + c * P:(n % 2) * C + (c + 1) * P],
                                                XG[:, c, n * P:(n + 1) * P], ident[:, :])
                    if n % 2:
                        i.then_inc(xt_ready, 1)
                if go_on:
                    dt_bc(b, 3)
                pe.wait_ge(xt_done, p * 4 + 4)
                pe.wait_ge(ones_set, p + 1)
                for a in range(CT):
                    for n in range(NB):
                        i = mm(psum[:, a, 0:C + 1], XT[:, n, a * P:(a + 1) * P], XT[:, n, :], n == 0, n == NB - 1)
                    i.then_inc(gram_ready, 1)
                pe.wait_ge(gram_done, p * 4 + 4)
                for j in range(CT):
                    for c in range(CT):
                        i = mm(psum[:, 2 + j, 0:C], GRAM[:, c, j * P:(j + 1) * P], q_w[:, c, :], c == 0, c == CT - 1)
                    i.then_inc(u_ready, 1)
                for k, w in enumerate((q_w, k_w)):
                    for c in range(CT):
                        mm(psum[0:2, 0, k * C:(k + 1) * C], XSUM[:, c, k, :], w[:, c, :], c == 0, False)
                    i = mm(psum[0:2, 0, k * C:(k + 1) * C], bias_sel[0:1, k, :], qk_b[0:1, k * C:(k + 1) * C], False, True)
                i.then_inc(qk_rows_ready, 1)
                pe.wait_ge(u_done, p * 2 + 2)
                pe.wait_ge(qk_rows_done, p + 1)
                for a in range(CT):
                    for j in range(CT):
                        mm(psum[:, 2 + a, 0:C], UT[:, j, a * P:(a + 1) * P], k_w[:, j, :], j == 0, False)
                    mm(psum[:, 2 + a, 0:C], QKROWS[0:2, a * P:(a + 1) * P], QKROWS[0:2, C:2 * C], False,
                       True).then_inc(sc_ready, 1)
                if go_on:
                    z_proj(b, (0,))
                pe.wait_ge(att_done, p * 2 + 2)
                for d in range(CT):
                    for a in range(CT):
                        i = mm(psum[:, d, 0:C], ATT[:, a, d * P:(d + 1) * P], p_w[:, a, :], a == 0, a == CT - 1)
                    i.then_inc(pa_ready, 1)
                pe.wait_ge(pa_done, p * 2 + 2)
                for c in range(CT):
                    for d in range(CT):
                        i = mm(psum[:, 2 + c, 0:C], v_w[:, d, c * P:(c + 1) * P], PA[:, d, :], d == 0, d == CT - 1)
                    i.then_inc(f_ready, 1)
                for o in range(CT):
                    for d in range(CT):
                        i = mm(psum[:, 0, o:o + 1], PA[:, d, o * P:(o + 1) * P], BV[:, d:d + 1], d == 0, d == CT - 1)
                i.then_inc(f_bias_ready, 1)
                pe.wait_ge(f_done, p * 2 + 2)
                pe.wait_ge(f_bias_done, p * 2 + 2)
                linear(FT, XG, lambda u: u, po_ready)
                if go_on:
                    z_proj(b, (1,))
                pe.wait_ge(x3_done, p * 4 + 4)
                norm_mean(later, X2)
                if go_on:
                    z_proj(b, (2, 3))

                def token_rows(n0, bank):
                    for n in range(n0, n0 + 2):
                        for c in range(CT):
                            i = nc.tensor.transpose(psum[:, bank, (n % 2) * C + c * P:(n % 2) * C + (c + 1) * P],
                                                    T[:, c, n * P:(n + 1) * P], ident[:, :])
                    i.then_inc(tm_ready, 1)
                norm_var(later, p * LNS + 3)
                token_rows(0, 0)
                token_rows(2, 1)
                pe.wait_ge(later.std, (p + 1) * LNS * NH)
                token_rows(4, 2)
                for n in range(NB):
                    for c in range(CT):
                        i = mm(psum[:, 3, n * E:(n + 1) * E], T[:, c, n * P:(n + 1) * P], gate_w[:, c, :],
                               c == 0, c == CT - 1)
                i.then_inc(gate_ready, 1)
                pe.wait_ge(tm_done, p * NB + 2)
                token_rows(6, 0)
                pe.wait_ge(tm_done, (p + 1) * NB)
                pe.wait_ge(gate_done, p + 1)

            def scans(b):
                pe.wait_ge(sz_done, (b + 1) * NC * NH)
                pe.wait_ge(bc_split, (b + 1) * NC * 3)

                def b_rows(c, s):
                    for h in range(NH):
                        m = mm(psum[:, h, :], sel[:, s, :], BCS[:, c, h * HL:(h + 1) * HL], True, True)
                    m.then_inc(brep_ready, 1)

                def b_odd(c, k, q):
                    pe.wait_ge(dbx_even, q)
                    b_rows(c, 2 * k + 1)

                def b_even(c, k, q):
                    pe.wait_ge(b_copied, q + 1)
                    b_rows(c, 2 * k)

                def c_rows(c, s, i, first=False):
                    if not first:
                        pe.wait_ge(hc_ready, i)
                    for h in range(NH):
                        m = mm(psum[:, 2 + h, :], sel[:, s + NS, :], BCS[:, c, h * HL:(h + 1) * HL], True, True)
                    m.then_inc(crep_ready, 1)

                def sum_states(slot, i, first=False, last=False):
                    pe.wait_ge(hc_ready, i + 1)
                    for h in range(NH):
                        m = mm(psum[:, 4 + h, :], ident[:, :], HC[:, slot, h * HL:(h + 1) * HL], first, last,
                               skip_group_check=True)
                    m.then_inc(ysum_done, 1)

                def out_proj(c):
                    pe.wait_ge(yf_ready, b * NC + c + 1)
                    if c:
                        pe.wait_ge(ym_done, b * NC + c)
                    for h in range(NH):
                        p0 = DM * (c % 2)
                        m = mm(psum[p0:p0 + DM, 6 + h, :], outp_w[:, :], YF[:, h * HL:(h + 1) * HL], True, True)
                    m.then_inc(op_ready, 1)

                b0, q0 = b * NI, b * NIP
                b_rows(0, 1)
                b_even(0, 0, q0)
                for c in range(NC):
                    i, q = b0 + c * NS, q0 + c * NPAIR
                    if c:
                        c_rows(c - 1, NS - 1, i - 1)
                        sum_states(0, i - 2)
                    b_odd(c, 1, q + 1)
                    c_rows(c, 0, i, first=c == 0)
                    if c:
                        sum_states(1, i - 1, last=True)
                    b_even(c, 1, q + 1)
                    c_rows(c, 1, i + 1)
                    if c:
                        pe.wait_ge(y_read, b * NC + c)
                    sum_states(0, i, first=True)
                    b_odd(c, 2, q + 2)
                    c_rows(c, 2, i + 2)
                    sum_states(1, i + 1)
                    b_even(c, 2, q + 2)
                    if c:
                        out_proj(c - 1)
                    with pe.Fori(2, NPAIR - 1) as k:
                        c_rows(c, k * 2 - 1, i + k * 2 - 1)
                        sum_states(0, i + k * 2 - 2)
                        b_odd(c, k + 1, q + k + 1)
                        c_rows(c, k * 2, i + k * 2)
                        sum_states(1, i + k * 2 - 1)
                        b_even(c, k + 1, q + k + 1)
                    c_rows(c, NS - 3, i + NS - 3)
                    sum_states(0, i + NS - 4)
                    if c + 1 < NC:
                        b_odd(c + 1, 0, q + NPAIR)
                    c_rows(c, NS - 2, i + NS - 2)
                    sum_states(1, i + NS - 3)
                    if c + 1 < NC:
                        b_even(c + 1, 0, q + NPAIR)
                c_rows(NC - 1, NS - 1, b0 + NI - 1)
                sum_states(0, b0 + NI - 2)
                sum_states(1, b0 + NI - 1, last=True)
                out_proj(NC - 1)

            pe.wait_ge(w_loaded, W_ALL)
            mm(psum[:, 0, 0:DI], xproj_dt[:, :], dtw[:, :], True, True).then_inc(prep_pe, 1)
            pe.wait_ge(prep_dve, PREP_DVE)
            start(0)
            scans(0)
            with pe.Fori(1, B) as b:
                between(b - 1, b)
                scans(b)
            between(B - 1, None)

        @block.scalar
        def _(act):
            def norm_square(N, n):
                for h in range(NH):
                    s = slice(h * HL, (h + 1) * HL)
                    act.wait_ge(N.centred, n * NH + h + 1)
                    nc.scalar.activation(N.SQ[:, :, s], N.T[:, :, s], ACT.Square).then_inc(N.squared, 1)

            def norm_std(N, n, eps, scale):
                for h in range(NH):
                    m = slice(h * (NB // NH), (h + 1) * (NB // NH))
                    act.wait_ge(N.var, n * NH + h + 1)
                    nc.scalar.activation(N.std_t[:, m], psum[:, N.bank + h, m], ACT.Sqrt, bias=eps[:, :],
                                         scale=scale).then_inc(N.std, 1)

            def affine(N, n, dst, signal):
                act.wait_ge(N.done, n * NH + 2)
                for c in range(CT):
                    nc.scalar.activation(dst[:, c, :], N.T[:, c, :], ACT.Identity, scale=NG[:, c:c + 1],
                                         bias=NBB[:, c:c + 1]).then_inc(signal, 1)

            def silu_x(b, c):
                for h in range(NH):
                    act.wait_ge(xi_ready, (b * NC + c) * NH + h + 1)
                    nc.scalar.activation(XC[:, c, h * HL:(h + 1) * HL], psum[:, 4 + h, :], ACT.Silu,
                                         bias=dcols[:, 0:1]).then_inc(xc_done, 1)

            def read_dt_bc(b, c):
                n = b * NC + c
                e = DT[:, c, :]
                act.wait_ge(dtp_ready, n + 1)
                nc.scalar.activation(halves(e), psum[:, 4:6, :], ACT.Abs, bias=dcols[:, 1:2]).then_inc(sp_abs, 1)
                nc.scalar.activation(halves(DTX[:, c, :]), psum[:, 4:6, :], ACT.Relu,
                                     bias=dcols[:, 1:2]).then_inc(sp_relu, 1)
                act.wait_ge(bcp_ready, n + 1)
                nc.scalar.activation(halves(BCS[:, c, :]), psum[:, 6:8, :], ACT.Copy).then_inc(bc_copy, 1)

            def exp_ln(b, c):
                n = b * NC + c
                e = DT[:, c, :]
                act.wait_ge(sp_abs, n + 1)
                nc.scalar.activation(e, e, ACT.Exp, scale=-1.0).then_inc(sp_exp, 1)
                act.wait_ge(sp_exp, n + 1)
                nc.scalar.activation(log_tile(c), e, ACT.Ln, bias=1.0).then_inc(sp_ln, 1)

            def softplus(b, c):
                read_dt_bc(b, c)
                exp_ln(b, c)

            def silu_z(b, sequences):
                for u in range(sequences[0] * NH, (sequences[-1] + 1) * NH):
                    c, h = u // NH, u % NH
                    if u == 0:
                        act.wait_ge(sp_step, ((b + 1) * NC - 1) * SP_STEPS)
                    act.wait_ge(z_ready, b * NC * NH + u + 1)
                    nc.scalar.activation(SZ[:, c, h * HL:(h + 1) * HL], psum[:, 4 + 2 * (c % 2) + h, :],
                                         ACT.Silu).then_inc(sz_done, 1)

            def start(b):
                norm_square(first, b)
                norm_std(first, b, eps65_n, (1.0 + 1e-5) * INV_POW)
                affine(first, b, xn, x_aff)
                for c in range(NC):
                    silu_x(b, c)
                    softplus(b, c)
                silu_z(b, range(NC))

            def between(p, b):
                go_on = b is not None
                norm_square(later, p * LNS)
                norm_std(later, p * LNS, eps5_n, INV_POW)
                affine(later, p * (LNS - 1), T, y_aff)
                if go_on:
                    norm_square(first, b)
                    norm_std(first, b, eps65_n, (1.0 + 1e-5) * INV_POW)
                norm_square(later, p * LNS + 1)
                norm_std(later, p * LNS + 1, eps5_n, INV_POW)
                if go_on:
                    affine(first, b, xn, x_aff)
                    silu_x(b, 0)
                    softplus(b, 0)
                for u in range(4):
                    o, h = u // 2, u % 2
                    act.wait_ge(ff_ready, p * 4 + u + 1)
                    nc.scalar.activation(SQ[:, o, h * HL:(h + 1) * HL], psum[:, u, :], ACT.Identity,
                                         scale=scal[:, 5:6], bias=fbias[:, o:o + 1]).then_inc(ff_done, 1)
                if go_on:
                    silu_x(b, 1)
                    softplus(b, 1)
                    silu_x(b, 2)
                norm_square(later, p * LNS + 2)
                norm_std(later, p * LNS + 2, eps6_n, INV_POW)
                if go_on:
                    softplus(b, 2)
                act.wait_ge(g_cent, p * 2 + 2)
                for c in range(CT):
                    nc.scalar.activation(SQ[:, c, :], XG[:, c, :], ACT.Square,
                                         accum_out=g_sq[:, c:c + 1]).then_inc(g_sq_ready, 1)
                act.wait_ge(g_var_ready, p + 1)
                nc.scalar.activation(g_std, psum[:, 3, 0:2], ACT.Sqrt, bias=eps5[:, :]).then_inc(g_std_ready, 1)
                if go_on:
                    silu_x(b, 3)
                for k in range(4):
                    act.wait_ge(xt_ready, p * 4 + k + 1)
                    nc.scalar.activation(XT[:, 2 * k:2 * k + 2, 0:C], psum[:, k, :].rearrange("p (n c) -> p n c", n=2),
                                         ACT.Copy).then_inc(xt_done, 1)
                if go_on:
                    read_dt_bc(b, 3)
                for a in range(CT):
                    act.wait_ge(gram_ready, p * 2 + a + 1)
                    nc.scalar.activation(GRAM[:, a, :], psum[:, a, 0:C], ACT.Copy).then_inc(gram_done, 1)
                    nc.scalar.activation(XSUM[:, a, :, :].rearrange("p k m -> p (k m)")[:, 0:4:3],
                                         psum[:, a, C:C + 1].broadcast_to((P, 2)), ACT.Copy).then_inc(gram_done, 1)
                for j in range(CT):
                    act.wait_ge(u_ready, p * 2 + j + 1)
                    nc.scalar.activation(UT[:, j, :], psum[:, 2 + j, 0:C], ACT.Copy).then_inc(u_done, 1)
                act.wait_ge(qk_rows_ready, p + 1)
                nc.scalar.activation(QKROWS[0:2, :], psum[0:2, 0, :], ACT.Copy).then_inc(qk_rows_done, 1)
                for a in range(CT):
                    act.wait_ge(sm_step, p * 4 + 2 * a + 2)
                    nc.scalar.activation(ATT[:, a, :], psum[:, 2 + a, 0:C], ACT.Exp, scale=float(C) ** -0.5,
                                         bias=s_neg[:, a:a + 1], accum_out=s_sum[:, a:a + 1]).then_inc(sm_exp, 1)
                for d in range(CT):
                    act.wait_ge(pa_ready, p * 2 + d + 1)
                    nc.scalar.activation(PA[:, d, :], psum[:, d, 0:C], ACT.Copy).then_inc(pa_done, 1)
                for c in range(CT):
                    act.wait_ge(f_ready, p * 2 + c + 1)
                    nc.scalar.activation(FT[:, c, :], psum[:, 2 + c, 0:C], ACT.Copy).then_inc(f_done, 1)
                act.wait_ge(f_bias_ready, p + 1)
                for o in range(CT):
                    nc.scalar.activation(f_bias[:, o:o + 1], psum[:, 0, o:o + 1], ACT.Identity,
                                         bias=BP_[:, o:o + 1]).then_inc(f_bias_done, 1)
                if go_on:
                    exp_ln(b, 3)
                    silu_z(b, (0, 1))
                norm_square(later, p * LNS + 3)
                norm_std(later, p * LNS + 3, eps5, 1.0)
                if go_on:
                    silu_z(b, (2, 3))
                act.wait_ge(later.rstd, (p + 1) * LNS * NH)
                for n in range(NB):
                    act.wait_ge(tm_ready, p * 4 + n // 2 + 1)
                    nc.scalar.activation(TM[:, n, :], psum[:, (0, 1, 2, 0)[n // 2], (n % 2) * C:(n % 2 + 1) * C],
                                         ACT.Identity, scale=later.rstd_t[:, n:n + 1]).then_inc(tm_done, 1)

            def scans(b):
                b0, q0 = b * NI, b * NIP

                def copy_odd(q, again=True):
                    if again:
                        act.wait_ge(dbx_odd, q)
                    else:
                        act.wait_ge(sp_step, ((b + 1) * NC - 1) * SP_STEPS + 5)
                    act.wait_ge(brep_ready, 2 * q + 1)
                    nc.scalar.activation(halves(B_ODD[:, :]), brep, ACT.Copy).then_inc(b_copied, 1)

                def decay(c, s, d, i, again=True):
                    if again:
                        act.wait_ge(h_ready, i - 1)
                    nc.scalar.activation(DA[:, d, :], DT[:, c, :], ACT.Exp,
                                         scale=a_neg[:, bass.ds(s, 1)]).then_inc(da_ready, 1)

                for c in range(NC):
                    i, q = b0 + c * NS, q0 + c * NPAIR
                    act.wait_ge(dt_done, b * NC + c + 1)
                    copy_odd(q, again=c > 0)
                    decay(c, 0, 0, i, again=c > 0)
                    decay(c, 1, 1, i + 1, again=c > 0)
                    with act.Fori(1, NPAIR) as k:
                        copy_odd(q + k)
                        decay(c, k * 2, 0, i + k * 2)
                        decay(c, k * 2 + 1, 1, i + k * 2 + 1)

            act.wait_ge(w_loaded, W_ALL)
            nc.scalar.activation(a_neg[:, :], alog[:, :], ACT.Exp).then_inc(prep_act, 1)
            act.wait_ge(prep_dve, PREP_DVE)
            start(0)
            scans(0)
            with act.Fori(1, B) as b:
                between(b - 1, b)
                scans(b)
            between(B - 1, None)

        @block.gpsimd
        def _(pool):
            def scans(b):
                pool.wait_ge(dtx_done, (b + 1) * NC)

                def drive(c, q, again=True):
                    if again:
                        pool.wait_ge(h_ready, 2 * q)
                    pool.wait_ge(b_copied, q + 1)
                    nc.gpsimd.tensor_tensor(DBX[:, 1, :], B_ODD[:, :], DTX[:, c, :], ALU.mult).then_inc(dbx_odd, 1)

                for c in range(NC):
                    q = b * NIP + c * NPAIR
                    drive(c, q, again=c > 0)
                    with pool.Fori(1, NPAIR) as k:
                        drive(c, q + k)

            scans(0)
            with pool.Fori(1, B) as b:
                scans(b)

        @block.vector
        def _(dve):
            v = nc.vector

            def norm_center(N, n, src):
                for h in range(NH):
                    s = slice(h * HL, (h + 1) * HL)
                    dve.wait_ge(N.mean, n * NH + h + 1)
                    v.tensor_tensor(N.T[:, :, s], src[:, :, s],
                                    psum[:, N.bank + h, :].unsqueeze(1).broadcast_to((P, CT, HL)),
                                    ALU.subtract).then_inc(N.centred, 1)

            def norm_rstd(N, n, diag=True):
                for h in range(NH):
                    m = slice(h * (NB // NH), (h + 1) * (NB // NH))
                    dve.wait_ge(N.std, n * NH + h + 1)
                    v.reciprocal(N.rstd_t[:, m], N.std_t[:, m]).then_inc(N.rstd, 1)
                    if diag:
                        dve.wait_ge(N.rstd, n * NH + h + 1)
                        v.tensor_tensor(N.DIAG[:, h * HL:(h + 1) * HL].rearrange("p (n q) -> p n q", q=P),
                                        ident[:, :].unsqueeze(1).broadcast_to((P, NB // NH, P)),
                                        N.rstd_t[:, m].unsqueeze(2).broadcast_to((P, NB // NH, P)),
                                        ALU.mult).then_inc(N.diag, 1)

            def norm_scale(N, n, dst):
                for h in range(NH):
                    s = slice(h * HL, (h + 1) * HL)
                    dve.wait_ge(N.rep, n * NH + h + 1)
                    v.tensor_tensor(dst[:, :, s], N.T[:, :, s],
                                    psum[:, N.bank + h, :].unsqueeze(1).broadcast_to((P, CT, HL)),
                                    ALU.mult).then_inc(N.done, 1)

            steps = [0]

            def prep(i):
                steps[0] += 1
                i.then_inc(prep_dve, 1)
                dve.wait_ge(prep_dve, steps[0])

            def round_fp8(val, mag, dst, inv_scale, done):
                done(v.tensor_scalar(val, val, inv_scale, FP8_MAX, ALU.mult, ALU.min))
                done(v.tensor_scalar(val, val, -FP8_MAX, None, ALU.max))
                done(v.tensor_scalar(mag.bitcast(U32), val.bitcast(U32), 0x7F800000, None, ALU.bitwise_and))
                done(v.tensor_scalar(mag, mag, FP8_MIN_NORMAL, ROUND_AT, ALU.max, ALU.mult))
                done(v.tensor_tensor(val, val, mag, ALU.add))
                done(v.tensor_tensor(dst, val, mag, ALU.subtract))

            def split(b, c):
                n = b * NC + c
                dve.wait_ge(bc_copy, n + 1)
                v.tensor_tensor(halves(R1[64:128, :]), psum[64:128, 6:8, :], halves(BCS[64:128, c, :]),
                                ALU.subtract).then_inc(bc_split, 1)
                dve.wait_ge(bc_split, n * 3 + 1)
                v.tensor_copy(BCS[64:128, c, :], R1[64:128, :]).then_inc(bc_split, 1)
                dve.wait_ge(bc_split, n * 3 + 2)
                v.tensor_tensor(BCS[96:128, c, :], R1[96:128, :], BCS[96:128, c, :],
                                ALU.subtract).then_inc(bc_split, 1)

            lo, r = RSTD[:, :], H[:, 0, :]

            def log1p_small(b, c):
                n = b * NC + c
                e = DT[:, c, :]
                done = [0]

                def step(i):
                    done[0] += 1
                    i.then_inc(sp_step, 1)
                    dve.wait_ge(sp_step, n * SP_STEPS + done[0])
                dve.wait_ge(sp_exp, n + 1)
                step(v.scalar_tensor_tensor(lo, e, LOG_SERIES, e, ALU.is_lt, ALU.mult))
                step(v.tensor_scalar(r, lo, -1.0 / 4, None, ALU.mult))
                step(v.scalar_tensor_tensor(r, r, 1.0 / 3, lo, ALU.add, ALU.mult))
                step(v.scalar_tensor_tensor(r, r, -1.0 / 2, lo, ALU.add, ALU.mult))
                step(v.scalar_tensor_tensor(r, r, 1.0, lo, ALU.add, ALU.mult))

            def log1p(b, c, small=True):
                n = b * NC + c
                if small:
                    log1p_small(b, c)
                dve.wait_ge(sp_ln, n + 1)
                log = log_tile(c)
                v.scalar_tensor_tensor(log, DT[:, c, :], LOG_SERIES, log, ALU.is_ge, ALU.mult).then_inc(sp_step, 1)
                dve.wait_ge(sp_step, n * SP_STEPS + 6)
                v.tensor_tensor(r, r, log, ALU.add).then_inc(sp_step, 1)
                dve.wait_ge(sp_step, n * SP_STEPS + 7)
                v.tensor_tensor(DT[:, c, :], DTX[:, c, :], r, ALU.add).then_inc(dt_done, 1)
                dve.wait_ge(dt_done, n + 1)
                v.tensor_tensor(DTX[:, c, :], DT[:, c, :], XC[:, c, :], ALU.mult).then_inc(dtx_done, 1)

            def start(b):
                dve.wait_ge(next_loaded, 16)
                norm_center(first, b, X_NEXT)
                norm_rstd(first, b)
                norm_scale(first, b, first.T)
                for c in range(NC):
                    split(b, c)
                    log1p(b, c)

            def between(p, b):
                go_on = b is not None
                dve.wait_ge(ym_done, (p + 1) * NC)
                norm_center(later, p * LNS, YM)
                norm_rstd(later, p * LNS)
                norm_scale(later, p * (LNS - 1), T)
                if go_on:
                    norm_center(first, b, X_NEXT)
                dve.wait_ge(x_loaded, p * 16 + 16)
                for u in range(4):
                    o, h = u // 2, u % 2
                    s = slice(h * HL, (h + 1) * HL)
                    dve.wait_ge(pj_ready, p * 4 + u + 1)
                    v.scalar_tensor_tensor(X1[:, o, s], psum[:, u, :], PB[:, o:o + 1], X[:, o, s], ALU.add,
                                           ALU.add).then_inc(x1_done, 1)
                if go_on:
                    norm_rstd(first, b)
                dve.wait_ge(x1_done, p * 4 + 4)
                norm_center(later, p * LNS + 1, X1)
                if go_on:
                    norm_scale(first, b, first.T)
                norm_rstd(later, p * LNS + 1)
                norm_scale(later, p * (LNS - 1) + 1, T)
                dve.wait_ge(later.done, (p * (LNS - 1) + 2) * NH)
                qs = [0]

                def q_done(i):
                    qs[0] += 1
                    i.then_inc(q_step, 1)
                    dve.wait_ge(q_step, p * 6 + qs[0])
                round_fp8(T[:, :, :], SQ[:, :, :], QB, scal[:, 3:4], q_done)
                if go_on:
                    split(b, 0)
                    log1p(b, 0)
                dve.wait_ge(ff_done, p * 4 + 4)
                v.tensor_tensor(X2[:, :, :], X1, SQ[:, :, :], ALU.add).then_inc(x2_done, 1)
                if go_on:
                    split(b, 1)
                dve.wait_ge(x2_done, p + 1)
                norm_center(later, p * LNS + 2, X2)
                norm_rstd(later, p * LNS + 2)
                norm_scale(later, p * (LNS - 1) + 2, H5)
                dve.wait_ge(later.done, (p + 1) * (LNS - 1) * NH)
                v.tensor_reduce(g_sum, H5[:, :, :], AX_X, ALU.add).then_inc(g_sum_ready, 1)
                v.tensor_tensor(X2[:, :, :], X2[:, :, :], H5[:, :, :], ALU.add).then_inc(xh_done, 1)
                v.memset(XT[:, :, C:C + 1], 1.0).then_inc(ones_set, 1)
                dve.wait_ge(g_mean_ready, p + 1)
                v.tensor_copy(g_mean, psum[:, 2, 0:2]).then_inc(g_step, 1)
                dve.wait_ge(g_step, p * 3 + 1)
                dve.wait_ge(xh_done, p + 1)
                for c in range(CT):
                    v.tensor_scalar(XG[:, c, :], H5[:, c, :], g_mean[:, c:c + 1], None, ALU.subtract).then_inc(g_cent, 1)
                if go_on:
                    split(b, 2)
                dve.wait_ge(g_std_ready, p + 1)
                v.reciprocal(g_rs, g_std).then_inc(g_step, 1)
                dve.wait_ge(g_step, p * 3 + 2)
                v.tensor_tensor(g_sc, g_rs, GG, ALU.mult).then_inc(g_step, 1)
                dve.wait_ge(g_step, p * 3 + 3)
                for c in range(CT):
                    v.tensor_scalar(XG[:, c, :], XG[:, c, :], g_sc[:, c:c + 1], GB[:, c:c + 1], ALU.mult,
                                    ALU.add).then_inc(xg_ready, 1)
                if go_on:
                    log1p(b, 1)
                    log1p(b, 2)
                for a in range(CT):
                    dve.wait_ge(sc_ready, p * 2 + a + 1)
                    v.tensor_reduce(s_max[:, a:a + 1], psum[:, 2 + a, 0:C], AX_X, ALU.max).then_inc(sm_step, 1)
                    dve.wait_ge(sm_step, p * 4 + 2 * a + 1)
                    v.tensor_scalar(s_neg[:, a:a + 1], s_max[:, a:a + 1], -(float(C) ** -0.5), None,
                                    ALU.mult).then_inc(sm_step, 1)
                for a in range(CT):
                    dve.wait_ge(sm_exp, p * 2 + a + 1)
                    v.reciprocal(s_rec[:, a:a + 1], s_sum[:, a:a + 1]).then_inc(sm_rec, 1)
                    dve.wait_ge(sm_rec, p * 2 + a + 1)
                    v.tensor_scalar(ATT[:, a, :], ATT[:, a, :], s_rec[:, a:a + 1], None, ALU.mult).then_inc(att_done, 1)
                if go_on:
                    split(b, 3)
                dve.wait_ge(f_bias_done, p * 2 + 2)
                for u in range(4):
                    o, h = u // 2, u % 2
                    s = slice(h * HL, (h + 1) * HL)
                    dve.wait_ge(po_ready, p * 4 + u + 1)
                    v.scalar_tensor_tensor(X2[:, o, s], psum[:, u, :], f_bias[:, o:o + 1], X2[:, o, s], ALU.add,
                                           ALU.add).then_inc(x3_done, 1)
                dve.wait_ge(x3_done, p * 4 + 4)
                norm_center(later, p * LNS + 3, X2)
                if go_on:
                    log1p_small(b, 3)
                norm_rstd(later, p * LNS + 3, diag=False)
                if go_on:
                    log1p(b, 3, small=False)
                dve.wait_ge(gate_ready, p + 1)
                dve.wait_ge(later.rstd, (p + 1) * LNS * NH)
                v.tensor_tensor(logits[:, bass.ds(p * NB, NB), :],
                                psum[:, 3, 0:NB * E].rearrange("p (n e) -> p n e", n=NB),
                                later.rstd_t[:, :].unsqueeze(2).broadcast_to((P, NB, E)), ALU.mult).then_inc(gate_done, 1)

            def scans(b, stored_before):
                dve.wait_ge(dtx_done, b * NC + NC)
                dve.wait_ge(bc_split, (b + 1) * NC * 3)

                b0 = b * NI

                def drive(c, q):
                    dve.wait_ge(brep_ready, 2 * q + 2)
                    v.tensor_tensor(halves(DBX[:, 0, :]), brep, halves(DTX[:, c, :]), ALU.mult).then_inc(dbx_even, 1)

                def scan(slot, i, q, again=True):
                    if again:
                        dve.wait_ge(hc_ready, i - 1)
                    dve.wait_ge(da_ready, i + 1)
                    dve.wait_ge((dbx_even, dbx_odd)[slot], q + 1)
                    v.tensor_tensor_scan(H[:, slot, :], DA[:, slot, :], DBX[:, slot, :], 0.0, ALU.mult,
                                         ALU.add).then_inc(h_ready, 1)

                def read_out(slot, i):
                    dve.wait_ge(h_ready, i + 1)
                    dve.wait_ge(crep_ready, i + 1)
                    v.tensor_tensor(halves(HC[:, slot, :]), crep, halves(H[:, slot, :]), ALU.mult).then_inc(hc_ready, 1)

                def gate(c):
                    n = b * NC + c
                    dve.wait_ge(ysum_done, b0 + (c + 1) * NS)
                    if c:
                        dve.wait_ge(op_ready, n)
                    v.scalar_tensor_tensor(halves(YF[:, :]), halves(XC[:, c, :]), dcols[:, 2:3], ysum, ALU.mult,
                                           ALU.add).then_inc(y_read, 1)
                    dve.wait_ge(y_read, n + 1)
                    v.tensor_tensor(YF[:, :], YF[:, :], SZ[:, c, :], ALU.mult).then_inc(yf_ready, 1)

                def skip(c):
                    dve.wait_ge(op_ready, b * NC + c + 1)
                    p0 = DM * (c % 2)
                    v.scalar_tensor_tensor(halves(YM[p0:p0 + DM, c // 2, :]), halves(xn[p0:p0 + DM, c // 2, :]),
                                           scal[p0:p0 + DM, 0:1], psum[p0:p0 + DM, 6:8, :], ALU.mult,
                                           ALU.add).then_inc(ym_done, 1)

                q0 = b * NIP
                for c in range(NC):
                    i, q = b0 + c * NS, q0 + c * NPAIR
                    if c:
                        read_out(0, i - 2)
                    drive(c, q)
                    if c:
                        read_out(1, i - 1)
                    scan(0, i, q, again=c > 0)
                    scan(1, i + 1, q, again=c > 0)
                    if c:
                        gate(c - 1)
                    with dve.Fori(1, NPAIR) as k:
                        read_out(0, i + k * 2 - 2)
                        drive(c, q + k)
                        read_out(1, i + k * 2 - 1)
                        scan(0, i + k * 2, q + k)
                        scan(1, i + k * 2 + 1, q + k)
                    if c:
                        skip(c - 1)
                read_out(0, b0 + NI - 2)
                read_out(1, b0 + NI - 1)
                gate(NC - 1)
                skip(NC - 1)
                if stored_before:
                    dve.wait_ge(stored, b * 32)

            v.memset(eps6[:, :], 1e-6)
            v.memset(eps65[:, :], 1e-11)
            v.memset(eps5[:, :], 1e-5)
            v.memset(eps6_n[:, :], 1e-6 * INV_POW)
            v.memset(eps65_n[:, :], 1e-11 * INV_POW)
            v.memset(eps5_n[:, :], 1e-5 * INV_POW)
            prep(v.memset(XN[:, :, 0:PAD], 0.0))
            prep(v.memset(XSUM[:, :, :, :], 0.0))
            dve.wait_ge(w_loaded, W_ALL)
            prep(v.tensor_copy(sel[:, :, :], sel_f32))
            for par in range(2):
                other = DM * (1 - par)
                prep(v.memset(in_w[other:other + DM, par, :], 0.0))
            for par in range(2):
                prep(v.tensor_tensor(conv_in_w[:, par, :, :], in_w[:, par, 0:DI].unsqueeze(1).broadcast_to((P, TAPS, DI)),
                                     conv_rep[:, :, :], ALU.mult))
            dve.wait_ge(prep_pe, 1)
            prep(v.tensor_copy(dt_w[:, :], psum[:, 0, 0:DI]))
            dve.wait_ge(prep_act, 1)
            prep(v.tensor_scalar(a_neg[:, :], a_neg[:, :], -1.0, None, ALU.mult))
            prep(v.reciprocal(scal[:, 3:5], scal[:, 1:3]))
            prep(v.tensor_tensor(scal[:, 5:6], scal[:, 1:2], scal[:, 2:3], ALU.mult))
            prep(v.tensor_copy(fbias_b[:, :], FB))
            prep(v.tensor_copy(fbias[:, :], fbias_b[:, :]))
            fw = SQ[:, 0, 0:CT * C].rearrange("p (c o) -> p c o", c=CT)
            round_fp8(ffn_w[:, :, :], fw, ffn_q[:, :, :], scal[:, 4:5], prep)
            assert steps[0] == PREP_DVE

            start(0)
            scans(0, False)
            with dve.Fori(1, B) as b:
                between(b - 1, b)
                scans(b, True)
            between(B - 1, None)


PREP_DVE = 1 + 1 + 1 + 2 + 2 + 1 + 1 + 1 + 1 + 1 + 1 + 6


def lay_out(inp):
    import numpy as np
    f = {k: np.asarray(v) for k, v in inp.items()}
    a = {}

    def by_tile(w):
        return np.ascontiguousarray(w.reshape(w.shape[0] // P, P, w.shape[1]).transpose(1, 0, 2))

    def cols(v):
        return v.reshape(-1, P).T

    c = "L0_conv_"
    a["x"] = np.ascontiguousarray(f["x"].reshape(B, CT, P, L).transpose(0, 2, 1, 3))
    a["conv_rep"] = np.ascontiguousarray(np.broadcast_to(f[c + "conv_w"].T, (P, TAPS, DI)))
    a["xproj"] = f[c + "x_proj_w"]
    a["dtwT"] = np.ascontiguousarray(f[c + "dt_proj_w"].T)
    a["in_wT"] = np.ascontiguousarray(f[c + "in_proj_w"].T)
    a["bc_wT"] = np.ascontiguousarray(np.tile(f[c + "x_proj_w"][4:36], (4, 1)).T)
    a["outpT"] = np.ascontiguousarray(f[c + "out_proj_w"].T)
    a["projT"] = by_tile(f[c + "proj_w"].T)
    a["ffn_k"] = by_tile(f["L0_ffn_kernel"])
    for k in "qkp":
        a[f"w{k}T"] = by_tile(f[f"L1_conv_w{k}"].T)
    a["wv"] = by_tile(f["L1_conv_wv"])
    a["qk_b"] = np.concatenate([f["L1_conv_bq"], f["L1_conv_bk"]])[None, :]
    a["c_bias_sel"] = np.array([[[L, 1], [1, 0]]], np.float32)
    a["cols"] = np.ascontiguousarray(np.concatenate([cols(f[k]) for k in (
        c + "norm_g", c + "norm_b", c + "proj_b", "L0_ffn_bias", "L1_conv_gn_gamma", "L1_conv_gn_beta",
        "L1_conv_bv", "L1_conv_bp")], axis=1))
    a["dcols"] = np.ascontiguousarray(np.stack([f[c + k] for k in ("conv_b", "dt_proj_b", "D_param")], axis=1))
    a["scal"] = np.ascontiguousarray(np.broadcast_to(np.concatenate([
        f[c + "skip_scale"], f["L0_ffn_input_scale"], f["L0_ffn_kernel_scale"]]), (P, 3)))
    a["alog"] = f[c + "A_log"]
    a["c_ident"] = np.eye(P, dtype=np.float32)
    a["c_mean"] = np.full((P, P), 1.0 / C, np.float32)
    g = np.arange(P) // 8
    a["c_group"] = (g[:, None] == g[None, :]).astype(np.float32) / (8 * L)
    part = np.arange(P)
    used = (part < 32) | (part >= 64)
    a["c_sel"] = np.broadcast_to(((part[:, None] % 32 == np.arange(32)[None, :]) & used[:, None])[:, :, None],
                                 (P, 32, P)).astype(np.float32)
    m = "L1_ffn_"
    a["gateT"] = by_tile(f[m + "gate_w"].T)
    a["w1T"] = np.ascontiguousarray(f[m + "w1"].reshape(E, HID, CT, P).transpose(0, 3, 2, 1))
    a["w2T"] = np.ascontiguousarray(f[m + "w2"].reshape(E, C, HB, P).transpose(0, 3, 2, 1))
    a["b1"] = np.ascontiguousarray(f[m + "b1"].reshape(E, HB, P).transpose(2, 0, 1))
    a["b2"] = np.ascontiguousarray(np.broadcast_to(f[m + "b2"], (P, E, C)))
    a["c_empty"] = (3 * TOK + np.arange(P)[:, None] + P * np.arange(NT)[None, :]).astype(np.float32)
    r = np.arange(P, dtype=np.float32)
    a["c_iota_e"] = np.ascontiguousarray(np.broadcast_to(np.arange(E, dtype=np.float32), (P, NG_, E)))
    a["c_iota_p"] = np.ascontiguousarray(np.broadcast_to(r, (P, P)))
    a["c_iota_t"] = np.ascontiguousarray(np.broadcast_to(np.arange(NT, dtype=np.float32) * P, (P, NT)))
    blocks = P * np.arange(NG_, dtype=np.float32)[None, :] + TOK * np.arange(1, 3, dtype=np.float32)[:, None]
    a["c_token"] = np.ascontiguousarray(np.stack([np.broadcast_to(blocks, (P, 2, NG_)),
                                                  np.broadcast_to(r[:, None, None], (P, 2, NG_))], axis=3))
    a["c_before"] = (r[:, None] < r[None, :]).astype(np.float32)
    return a


def build_moe(nc, t, x3_dram, xm_rows, y_rows, logits, routing, experts, out):
    with ExitStack() as ctx:
        def sb(name, shape, dt=F32):
            return ctx.enter_context(nc.sbuf_tensor(f"{name}_sb", shape, dt))

        def sem(name):
            return ctx.enter_context(nc.semaphore(name))

        psum = ctx.enter_context(nc.psum_tensor("psum_moe", [P, 8, 512], F32))
        iota_e, iota_p, iota_t, token, empty, before = (routing[name] for name, _ in ROUTING_CONSTANTS)
        ident = sb("m_ident", [P, P])
        b1 = sb("b1", [P, E, HB])
        b2 = sb("b2", [P, E, C])
        ones = sb("ones", [P, P])
        restart = sb("restart", [P, E, NG_])
        W1, W2 = expert_weights(experts)
        EQ, CAND, OH1, OH2, LG2, POS = (sb(n, [P, NG_, E]) for n in ("eq", "cand", "oh1", "oh2", "lg2", "pos"))
        TOT, INCL = (sb(n, [P, E, NG_]) for n in ("tot", "incl"))
        M1, M2, IDX, DIF, EX, P1, P2, SL, SLF = (sb(n, [P, NG_]) for n in ("m1", "m2", "idx", "dif", "ex", "p1", "p2", "sl", "slf"))
        SLOT = sb("slot", [P, 2, NG_], U32)
        LO_I, HI_I = (sb(n, [P, 2, NG_], U32) for n in ("lo_i", "hi_i"))
        LO, HI = (sb(n, [P, 2, NG_]) for n in ("lo", "hi"))
        PADI = sb("padi", [P, E], U32)
        PADF, PINC, START = (sb(n, [P, E]) for n in ("padf", "pinc", "start"))
        TEC = sb("tec", [P, NT, E])
        TEF = sb("tef", [P, NT])
        TE = sb("te", [P, NT], mybir.dt.int32)
        ROWF = sb("rowf", [P, NT])
        EMPTY = sb("empty_row", [P, NT])
        ROW = sb("row", [P, NT], U32)
        TAB = sb("tab", [P, NT], U32)
        HG = sb("hg", [P, HID])
        HGT = sb("hgt", [P, HB, P])
        OLO = HG[:, :].bitcast(BF16).rearrange("p (g k m) -> p g k m", g=2, k=8)
        TILE1 = HGT[:, :, :].rearrange("p k m -> p (k m)").bitcast(BF16)[:, 0:16 * NT].rearrange("p (g k t) -> p g k t", g=2, k=8)
        OHI = sb("ohi", [P, 2, 8, 2, NT], BF16)
        IX = sb("ix", [P, RING], U32)
        XG = sb("XG", [P, RING, C])
        XGT = sb("XGT", [P, 2, CT, P])
        YS = sb("YS", [P, 2, C])
        O = sb("O", [P, RING, C])
        IY = sb("iy", [P, 2], U32)
        X3_EARLY = sb("X3", [P, B - 1, CT, L])
        X3 = [X3_EARLY[:, b, :, :] for b in range(B - 1)]
        X3.append(experts[:, LAST_W2:EXPERT_FLOATS].rearrange("p (c l) -> p c l", c=CT))
        Y = experts[:, 0:E * CT * HID].rearrange("p (b j n c) -> p b j n c", b=B, j=2, n=NB)

        c_loaded = sem("c_loaded"); x3_loaded = sem("x3_loaded")
        route = sem("route"); route_exp = sem("route_exp"); rank_ready = sem("rank_ready")
        onehot_ready = sem("onehot_ready"); onehot_used = sem("onehot_used"); onehot_tile = sem("onehot_tile"); tab_step = sem("tab_step"); tab_done = sem("tab_done")
        ix_ready = sem("ix_ready"); indices_there = sem("indices_there")
        xg_ready = [sem(f"xg_ready{k}") for k in range(RING)]
        t1_ready = sem("t1_ready"); xgt_done = sem("xgt_done"); m1_ready = sem("m1_ready"); hg_done = sem("hg_done")
        t2_ready = sem("t2_ready"); gelu_done = sem("gelu_done"); m2_ready = sem("m2_ready"); y_copied = sem("y_copied")
        y_stored = [sem(f"y_stored{k}") for k in range(2)]
        iy_ready = sem("iy_ready"); rows_there = sem("rows_there"); y_loaded = [sem(f"y_loaded{b}") for b in range(B)]
        o_half = sem("o_half"); o_ready = sem("o_ready"); ot_ready = sem("ot_ready"); o_done = sem("o_done")
        out_stored = sem("out_stored")
        block = ctx.enter_context(nc.Block())

        consts = [(ident[:, :], t["c_ident"]), (b1[:, :, :], t["b1"]), (b2[:, :, :], t["b2"])]
        C_ALL = 16 * len(consts)

        @block.sync
        def _(sp):
            for d, s in consts:
                sp.dma_start(d, s).then_inc(c_loaded, 16)
            for b in range(B - 1):
                sp.dma_start(X3[b], x3_dram[b]).then_inc(x3_loaded, 16)
            for k in range(2):
                sp.wait_ge(y_stored[k], 16 * ((NT + 1 - k) // 2))
            chosen = y_rows[TOK:3 * TOK, :].rearrange("(j b n p) c -> b p j n c", j=2, b=B, n=NB)
            for b in range(B):
                for j in range(2):
                    sp.dma_start(Y[:, b, j, :, :], chosen[b][:, j]).then_inc(y_loaded[b], 16)
            sp.dma_start(X3[B - 1], x3_dram[B - 1]).then_inc(x3_loaded, 16)
            for b in range(B):
                sp.wait_ge(o_done, b * NB + NB)
                sp.dma_start(out[b], X3[b]).then_inc(out_stored, 16)
            sp.wait_ge(out_stored, B * 16)

        @block.gpsimd
        def _(pool):
            def gather(tile, k):
                nc.gpsimd.tensor_copy(IX[:, k:k + 1], TAB[:, bass.ds(tile, 1)]).then_inc(ix_ready, 1)
                pool.wait_ge(ix_ready, tile + 1)
                pool.sem_inc(indices_there, 1)
                pool.indirect_dma_start(XG[:, k, :], None, xm_rows,
                                        bass.IndirectOffsetOnAxis(ap=IX[:, k:k + 1], axis=0)).then_inc(xg_ready[k], 16)

            def scatter(tile, k):
                nc.gpsimd.tensor_copy(IY[:, k:k + 1], ROW[:, bass.ds(tile, 1)]).then_inc(iy_ready, 1)
                pool.wait_ge(iy_ready, tile + 1)
                pool.wait_ge(y_copied, tile + 1)
                pool.sem_inc(rows_there, 1)
                pool.indirect_dma_start(y_rows, bass.IndirectOffsetOnAxis(ap=IY[:, k:k + 1], axis=0), YS[:, k, :],
                                        None).then_inc(y_stored[k], 16)

            pool.wait_ge(tab_done, 1)
            for k in range(RING):
                gather(k, k)

            def gather_next(i, k):
                pool.wait_ge(t1_ready, i * RING + (k - RING + 1))
                gather(i * RING + k, k)
            for k in range(RING):
                gather_next(1, k)
                if k == 2:
                    pool.wait_ge(tab_done, 2)
                if k >= 2:
                    scatter(k - 2, k % 2)
            with pool.Fori(2, NT // RING) as i:
                for k in range(RING):
                    gather_next(i, k)
                    pool.wait_ge(y_stored[k % 2], i * 32 + ((k - 6) // 2) * 16)
                    scatter(i * RING + (k - 6), k % 2)
            for tile in range(RING * (NT // RING), NT + 6):
                if tile < NT:
                    gather_next(tile // RING, tile % RING)
                pool.wait_ge(y_stored[tile % 2], 16 * ((tile - 6) // 2))
                scatter(tile - 6, tile % 2)

        @block.tensor
        def _(pe):
            def mm(o, lhsT, rhs, start, stop, **k):
                return nc.tensor.matmul(o, lhsT, rhs, start=start, stop=stop, **k)

            pe.wait_ge(route, R_CHOSEN)
            flat = LG2[:, :, :].rearrange("p n e -> p (n e)")
            mm(psum[:, 0, 0:NG_ * E], before[:, :], flat, True, True)
            mm(psum[:, 1, 0:NG_ * E], ones[:, :], flat, True, True).then_inc(rank_ready, 1)
            for g in range(8):
                pe.wait_ge(onehot_ready, 2 * g + 2)
                for k in range(8):
                    i = mm(psum[:, 2, 0:2 * NT], OLO[:, g % 2, k, :],
                           OHI[:, g % 2, k, :, :].rearrange("p i t -> p (i t)"), g == 0 and k == 0,
                           g == 7 and k == 7)
                i.then_inc(onehot_used, 1)

            def turn_rows(tile, k, i):
                pe.wait_ge(xg_ready[k], i)
                if not isinstance(tile, int) or tile:
                    pe.wait_ge(xgt_done, tile)
                for c in range(CT):
                    m = nc.tensor.transpose(psum[:, 6, c * P:(c + 1) * P], XG[:, k, c * P:(c + 1) * P], ident[:, :])
                m.then_inc(t1_ready, 1)

            def up(tile, k2):
                e = pe.value_load(TE[0:1, bass.ds(tile, 1)], min_val=0, max_val=E - 1)
                pe.wait_ge(xgt_done, tile + 1)
                for h in range(NH):
                    for c in range(CT):
                        m = mm(psum[:, h, :], XGT[:, k2, c, :], W1[:, bass.ds(e, 1), c, h * HL:(h + 1) * HL],
                               c == 0, c == CT - 1)
                m.then_inc(m1_ready, 1)

            def turn_hidden(tile):
                pe.wait_ge(hg_done, tile + 1)
                for k in range(HB):
                    m = nc.tensor.transpose(psum[:, 2 + k // 4, (k % 4) * P:(k % 4 + 1) * P], HG[:, k * P:(k + 1) * P],
                                            ident[:, :])
                m.then_inc(t2_ready, 1)

            def down(tile):
                e = pe.value_load(TE[0:1, bass.ds(tile, 1)], min_val=0, max_val=E - 1)
                if not isinstance(tile, int) or tile:
                    pe.wait_ge(y_copied, tile)
                pe.wait_ge(gelu_done, tile + 1)
                for k in range(HB):
                    m = mm(psum[:, 4, 0:C], HGT[:, k, :], W2[:, bass.ds(e, 1), k, :], k == 0, k == HB - 1)
                m.then_inc(m2_ready, 1)

            pe.wait_ge(route, R_ALL)
            pe.wait_ge(c_loaded, C_ALL)
            turn_rows(0, 0, 16)
            turn_rows(1, 1, 16)
            up(0, 0)

            def step(tile, k, i):
                turn_hidden(tile - 1)
                turn_rows(tile + 1, (k + 2) % RING, (i + (k + 2) // RING) * 16 + 16)
                up(tile, (k + 1) % 2)
                down(tile - 1)
            for k in range(RING):
                step(k + 1, k, 0)
            with pe.Fori(1, NT // RING - 1) as i:
                for k in range(RING):
                    step(i * RING + (k + 1), k, i)
            for tile in range(TAIL, NT):
                turn_hidden(tile - 1)
                if tile + 1 < NT:
                    turn_rows(tile + 1, (tile + 1) % RING, 16 * ((tile + 1) // RING + 1))
                up(tile, tile % 2)
                down(tile - 1)
            turn_hidden(NT - 1)
            down(NT - 1)
            with pe.Fori(0, NG_ // RING) as i:
                for k in range(RING):
                    pe.wait_ge(o_ready, i * RING + (k + 1))
                    for c in range(CT):
                        m = nc.tensor.transpose(psum[:, k, c * P:(c + 1) * P], O[:, k, c * P:(c + 1) * P],
                                                ident[:, :])
                    m.then_inc(ot_ready, 1)

        @block.scalar
        def _(act):
            act.wait_ge(route, R_DIF)
            nc.scalar.activation(EX[:, :], DIF[:, :], ACT.Exp).then_inc(route_exp, 1)
            act.wait_ge(route, R_ALL)
            act.wait_ge(c_loaded, C_ALL)

            def gelu(tile):
                e = act.value_load(TE[0:1, bass.ds(tile, 1)], min_val=0, max_val=E - 1)
                act.wait_ge(t2_ready, tile + 1)
                for j in range(HB):
                    m = nc.scalar.activation(HGT[:, j, :], psum[:, 2 + j // 4, (j % 4) * P:(j % 4 + 1) * P], ACT.Gelu,
                                             bias=b1[:, bass.ds(e, 1), j])
                m.then_inc(gelu_done, 1)
            with act.Fori(0, NT // (2 * RING)) as i:
                for k in range(2 * RING):
                    gelu(i * (2 * RING) + k)
            for tile in range(NT - NT % (2 * RING), NT):
                gelu(tile)
            for b in range(B):
                act.wait_ge(y_loaded[b], 32)
                for n in range(NB):
                    g, k = b * NB + n, n % RING
                    if g >= RING:
                        act.wait_ge(o_done, g - RING + 1)
                    nc.scalar.activation(O[:, k, :], Y[:, b, 0, n, :], ACT.Identity,
                                         scale=P1[:, g:g + 1]).then_inc(o_half, 1)

        @block.vector
        def _(dve):
            v = nc.vector
            done = [0]

            def step(i):
                done[0] += 1
                i.then_inc(route, 1)
                dve.wait_ge(route, done[0])

            def wide(x):
                return x.unsqueeze(2).broadcast_to((P, NG_, E))

            def best(lg, m, onehot):
                step(v.tensor_reduce(m, lg, AX_X, ALU.max))
                step(v.tensor_tensor(EQ[:, :, :], lg, wide(m), ALU.is_equal))
                step(v.scalar_tensor_tensor(CAND[:, :, :], EQ[:, :, :], -float(E), iota_e[:, :, :], ALU.mult, ALU.add))
                step(v.tensor_reduce(IDX[:, :], CAND[:, :, :], AX_X, ALU.min))
                step(v.tensor_tensor(onehot, CAND[:, :, :], wide(IDX[:, :]), ALU.is_equal))

            v.memset(ones[:, :], 1.0)
            step(v.memset(restart[:, :, :], 1.0))
            step(v.memset(restart[:, :, 0:1], 0.0))
            best(logits[:, :, :], M1[:, :], OH1[:, :, :])
            step(v.scalar_tensor_tensor(LG2[:, :, :], OH1[:, :, :], -3.0e38, logits[:, :, :], ALU.mult, ALU.add))
            best(LG2[:, :, :], M2[:, :], OH2[:, :, :])
            step(v.tensor_tensor(DIF[:, :], M2[:, :], M1[:, :], ALU.subtract))
            assert done[0] == R_DIF
            step(v.tensor_tensor(LG2[:, :, :], OH1[:, :, :], OH2[:, :, :], ALU.add))
            assert done[0] == R_CHOSEN
            dve.wait_ge(rank_ready, 1)
            step(v.tensor_copy(TOT[:, :, :].rearrange("p e n -> p n e"),
                               psum[:, 1, 0:NG_ * E].rearrange("p (n e) -> p n e", n=NG_)))
            step(v.tensor_copy(POS[:, :, :].rearrange("p n e -> p (n e)"), psum[:, 0, 0:NG_ * E]))

            def flat(x):
                return x[:, :, :].rearrange("p e n -> p (e n)")
            step(v.tensor_tensor_scan(flat(INCL), flat(restart), flat(TOT), 0.0, ALU.mult, ALU.add))
            step(v.tensor_scalar(PADI[:, :], INCL[:, :, NG_ - 1], float(P - 1), None, ALU.add))
            step(v.tensor_scalar(PADI[:, :], PADI[:, :], 0xFFFFFFFF ^ (P - 1), None, ALU.bitwise_and))
            step(v.tensor_copy(PADF[:, :], PADI[:, :]))
            step(v.tensor_tensor_scan(PINC[:, :], ones[:, 0:E], PADF[:, :], 0.0, ALU.mult, ALU.add))
            step(v.tensor_tensor(START[:, :], PINC[:, :], PADF[:, :], ALU.subtract))
            step(v.tensor_tensor(INCL[:, :, :], INCL[:, :, :], TOT[:, :, :], ALU.subtract))
            step(v.tensor_tensor(INCL[:, :, :], INCL[:, :, :], START[:, :].unsqueeze(2).broadcast_to((P, E, NG_)), ALU.add))
            step(v.tensor_tensor(POS[:, :, :], POS[:, :, :], INCL[:, :, :].rearrange("p e n -> p n e"), ALU.add))
            for j, oh in enumerate((OH1, OH2)):
                step(v.tensor_tensor(EQ[:, :, :], oh[:, :, :], POS[:, :, :], ALU.mult))
                step(v.tensor_reduce(SLF[:, :], EQ[:, :, :], AX_X, ALU.add))
                step(v.tensor_copy(SLOT[:, j, :], SLF[:, :]))
            step(v.tensor_scalar(LO_I[:, :, :], SLOT[:, :, :], P - 1, None, ALU.bitwise_and))
            step(v.tensor_scalar(HI_I[:, :, :], SLOT[:, :, :], 7, None, ALU.logical_shift_right))
            step(v.tensor_copy(LO[:, :, :], LO_I[:, :, :]))
            step(v.tensor_copy(HI[:, :, :], HI_I[:, :, :]))
            step(v.tensor_tensor(TEC[:, :, :], START[:, :].unsqueeze(1).broadcast_to((P, NT, E)),
                                 iota_t[:, :].unsqueeze(2).broadcast_to((P, NT, E)), ALU.is_le))
            step(v.tensor_reduce(TEF[:, :], TEC[:, :, :], AX_X, ALU.add))
            step(v.tensor_scalar(TE[:, :], TEF[:, :], -1.0, None, ALU.add))
            dve.wait_ge(route_exp, 1)
            step(v.tensor_scalar(P2[:, :], EX[:, :], 1.0, None, ALU.add))
            step(v.reciprocal(P1[:, :], P2[:, :]))
            step(v.tensor_tensor(P2[:, :], EX[:, :], P1[:, :], ALU.mult))
            assert done[0] == R_ALL
            lo, hi = (x[:, :, :].rearrange("p j n -> p (j n)") for x in (LO, HI))
            tok = token[:, :, :, :].rearrange("p j n i -> p (j n) i")
            for g in range(8):
                s = slice(8 * g, 8 * g + 8)
                if g >= 2:
                    dve.wait_ge(onehot_used, g - 1)
                v.tensor_tensor(OLO[:, g % 2, :, :], iota_p[:, :].unsqueeze(1).broadcast_to((P, 8, P)),
                                lo[:, s].unsqueeze(2).broadcast_to((P, 8, P)), ALU.is_equal).then_inc(onehot_ready, 1)
                v.tensor_tensor(TILE1[:, g % 2, :, :], iota_p[:, 0:NT].unsqueeze(1).broadcast_to((P, 8, NT)),
                                hi[:, s].unsqueeze(2).broadcast_to((P, 8, NT)), ALU.is_equal).then_inc(onehot_tile, 1)
                dve.wait_ge(onehot_tile, g + 1)
                v.tensor_tensor(OHI[:, g % 2, :, :, :], TILE1[:, g % 2, :, :].unsqueeze(2).broadcast_to((P, 8, 2, NT)),
                                tok[:, s, :].unsqueeze(3).broadcast_to((P, 8, 2, NT)), ALU.mult).then_inc(onehot_ready, 1)
            dve.wait_ge(onehot_used, 8)
            table = [0]

            def table_step(i):
                table[0] += 1
                i.then_inc(tab_step, 1)
                dve.wait_ge(tab_step, table[0])
            table_step(v.tensor_copy(ROWF[:, :], psum[:, 2, 0:NT]))
            table_step(v.tensor_tensor(ROW[:, :], psum[:, 2, NT:2 * NT], ROWF[:, :], ALU.add))
            v.tensor_scalar(TAB[:, :], ROW[:, :], TOK - 1, None, ALU.bitwise_and).then_inc(tab_done, 1)
            table_step(v.tensor_copy(ROWF[:, :], ROW[:, :]))
            table_step(v.scalar_tensor_tensor(EMPTY[:, :], ROWF[:, :], 1.0, empty[:, :], ALU.is_lt, ALU.mult))
            table_step(v.tensor_tensor(ROWF[:, :], ROWF[:, :], EMPTY[:, :], ALU.add))
            dve.wait_ge(tab_done, 1)
            v.tensor_copy(ROW[:, :], ROWF[:, :]).then_inc(tab_done, 1)

            def rows_turned(tile, k2):
                dve.wait_ge(t1_ready, tile + 1)
                v.tensor_copy(XGT[:, k2, :, :].rearrange("p c m -> p (c m)"), psum[:, 6, 0:C]).then_inc(xgt_done, 1)

            def hidden(tile):
                dve.wait_ge(m1_ready, tile + 1)
                v.tensor_copy(HG[:, :].rearrange("p (h n) -> p h n", h=NH), psum[:, 0:2, :]).then_inc(hg_done, 1)

            def result(tile, k, free):
                e = dve.value_load(TE[0:1, bass.ds(tile, 1)], min_val=0, max_val=E - 1)
                dve.wait_ge(m2_ready, tile + 1)
                if free is not None:
                    dve.wait_ge(y_stored[k], free)
                v.tensor_tensor(YS[:, k, :].unsqueeze(1), psum[:, 4, 0:C].unsqueeze(1), b2[:, bass.ds(e, 1), :],
                                ALU.add).then_inc(y_copied, 1)
            dve.wait_ge(c_loaded, C_ALL)
            rows_turned(0, 0)
            rows_turned(1, 1)
            hidden(0)
            for k in range(RING):
                rows_turned(k + 2, k % 2)
                hidden(k + 1)
                result(k, k % 2, 16 if k >= 2 else None)
            with dve.Fori(1, NT // RING - 1) as i:
                for k in range(RING):
                    rows_turned(i * RING + (k + 2), k % 2)
                    hidden(i * RING + (k + 1))
                    result(i * RING + k, k % 2, i * 32 + (k // 2) * 16)
            for tile in range(TAIL, NT):
                if tile + 1 < NT:
                    rows_turned(tile + 1, (tile + 1) % 2)
                hidden(tile)
                result(tile - 1, (tile - 1) % 2, 16 * ((tile - 1) // 2))
            result(NT - 1, (NT - 1) % 2, 16 * ((NT - 1) // 2))
            dve.wait_ge(x3_loaded, (B - 1) * 16)

            def add(g):
                if g == (B - 1) * NB:
                    dve.wait_ge(x3_loaded, B * 16)
                dve.wait_ge(ot_ready, g + 1)
                x = X3[g // NB][:, :, (g % NB) * P:(g % NB + 1) * P]
                v.tensor_tensor(x, psum[:, g % RING, 0:C].rearrange("p (c m) -> p c m", c=CT), x,
                                ALU.add).then_inc(o_done, 1)
            for g in range(NG_):
                k = g % RING
                dve.wait_ge(y_loaded[g // NB], 32)
                dve.wait_ge(o_half, g + 1)
                v.scalar_tensor_tensor(O[:, k, :], Y[:, g // NB, 1, g % NB, :], P2[:, g:g + 1], O[:, k, :], ALU.mult,
                                       ALU.add).then_inc(o_ready, 1)
                if g:
                    add(g - 1)
            add(NG_ - 1)


def kernel(**inputs):
    import numpy as np
    import concourse.bacc as bacc
    from concourse.bass_utils import run_bass_kernel_spmd

    arrays = lay_out(inputs)
    nc = bacc.Bacc("TRN2", target_bir_lowering=False, num_devices=1)
    t = {k: nc.dram_tensor(k, a.shape, mybir.dt.from_np(a.dtype), kind="ExternalInput").ap() for k, a in arrays.items()}
    out = nc.dram_tensor("out", (B, P, CT, L), F32, kind="ExternalOutput").ap()
    x3_dram = nc.dram_tensor("x3_dram", (B, P, CT, L), F32).ap()
    xm_rows = nc.dram_tensor("xm_rows", (B * L, C), F32).ap()
    y_rows = nc.dram_tensor("y_rows", (Y_ROWS, C), F32).ap()
    with ExitStack() as ctx:
        logits = ctx.enter_context(nc.sbuf_tensor("logits_sb", [P, NG_, E], F32))
        routing = {name: ctx.enter_context(nc.sbuf_tensor(name + "_sb", shape, F32)) for name, shape in ROUTING_CONSTANTS}
        experts = ctx.enter_context(nc.sbuf_tensor("experts_sb", [P, EXPERT_FLOATS], F32))
        build_front(nc, t, x3_dram, xm_rows, logits, routing, experts)
        build_moe(nc, t, x3_dram, xm_rows, y_rows, logits, routing, experts, out)
    r = run_bass_kernel_spmd(nc, [arrays], core_ids=[0])
    got = r.results[0]["out"]
    return np.ascontiguousarray(got.transpose(0, 2, 1, 3)).reshape(B, C, 32, 32)
```
